# Optimizing a Trainium2 kernel written in Bass

```python
import numpy as np
import jax
import jax.numpy as jnp

def _softmax(x, axis=-1):
    return jax.nn.softmax(x, axis=axis)

def _gelu(x):
    return jax.nn.gelu(x, approximate=True)

def _silu(x):
    return jax.nn.silu(x)

def _sigmoid(x):
    return jax.nn.sigmoid(x)

def _layernorm(x, axis=-1, eps=1e-05):
    m = jnp.mean(x, axis=axis, keepdims=True)
    v = jnp.var(x, axis=axis, keepdims=True)
    return (x - m) / jnp.sqrt(v + eps)

def _scatter_add(tgt, idx, src, axis=0):
    return tgt.at[idx].add(src)

def _segment_sum(src, seg, n):
    return jax.ops.segment_sum(src, seg, n)
kernel_name = 'mk_macaron_d1_jaxref_r8_05f8ff'

def setup_inputs(seed: int=0):
    np.random.seed(seed)
    _w = jnp.asarray

    def _L0_attn_setup():
        import jax, jax.numpy as jnp
        import numpy as np
        B, S, D, H, DFF = (4, 256, 128, 16, 512)
        HD = D // H

        def rmsnorm(x, scale, eps=1e-06):
            var = jnp.mean(jnp.square(x), axis=-1, keepdims=True)
            return x * jax.lax.rsqrt(var + eps) * scale

        def gdn_attention(x, wq, bq, wk, bk, wv, bv, wbeta, bbeta, wo, bo):
            b, s, _ = x.shape
            q = (x @ wq + bq).reshape(b, s, H, HD)
            k = (x @ wk + bk).reshape(b, s, H, HD)
            v = (x @ wv + bv).reshape(b, s, H, HD)
            k = k / (jnp.linalg.norm(k, axis=-1, keepdims=True) + 1e-06)
            beta = jax.nn.sigmoid(x @ wbeta + bbeta)[..., None]
            q = jnp.transpose(q, (1, 0, 2, 3))
            k = jnp.transpose(k, (1, 0, 2, 3))
            v = jnp.transpose(v, (1, 0, 2, 3))
            beta = jnp.transpose(beta, (1, 0, 2, 3))

            def _step(Sm, inputs):
                q_t, k_t, v_t, beta_t = inputs
                Sk = jnp.einsum('bhde,bhe->bhd', Sm, k_t)
                delta = v_t - Sk
                Sm = Sm + beta_t[..., None] * jnp.einsum('bhd,bhe->bhde', delta, k_t)
                o_t = jnp.einsum('bhde,bhe->bhd', Sm, q_t)
                return (Sm, o_t)
            S0 = jnp.zeros((b, H, HD, HD), x.dtype)
            _, outputs = jax.lax.scan(_step, S0, (q, k, v, beta))
            outputs = jnp.transpose(outputs, (1, 0, 2, 3)).reshape(b, s, D)
            return outputs @ wo + bo
        key = jax.random.key(seed)
        ks = jax.random.split(key, 16)
        s = 1.0 / np.sqrt(D)
        inp = {'x': jax.random.normal(ks[0], (B, S, D), jnp.float32), 'wq': jax.random.normal(ks[1], (D, D), jnp.float32) * s, 'bq': jnp.zeros((D,), jnp.float32), 'wk': jax.random.normal(ks[2], (D, D), jnp.float32) * s, 'bk': jnp.zeros((D,), jnp.float32), 'wv': jax.random.normal(ks[3], (D, D), jnp.float32) * s, 'bv': jnp.zeros((D,), jnp.float32), 'wbeta': jax.random.normal(ks[4], (D, H), jnp.float32) * s, 'bbeta': jnp.zeros((H,), jnp.float32), 'wo': jax.random.normal(ks[5], (D, D), jnp.float32) * s, 'bo': jnp.zeros((D,), jnp.float32), 'w1': jax.random.normal(ks[6], (D, DFF), jnp.float32) * s, 'b1': jnp.zeros((DFF,), jnp.float32), 'w2': jax.random.normal(ks[7], (DFF, D), jnp.float32) * (1.0 / np.sqrt(DFF)), 'b2': jnp.zeros((D,), jnp.float32), 'ln1_scale': jnp.ones((D,), jnp.float32), 'ln2_scale': jnp.ones((D,), jnp.float32)}
        return inp
    _L0_attn_in = _L0_attn_setup()

    def _L0_ffn_setup():
        import math
        import jax, jax.numpy as jnp
        import numpy as np
        B, S, D, H, E, F = (2, 128, 128, 16, 16, 512)
        HEAD = D // H
        MOE_TOKEN_DROPOUT = 0.2
        EPS = 1e-05

        def layer_norm(x, w, b):
            mu = x.mean(-1, keepdims=True)
            var = ((x - mu) ** 2).mean(-1, keepdims=True)
            return (x - mu) * jax.lax.rsqrt(var + EPS) * w + b
        key = jax.random.key(seed)
        ks = jax.random.split(key, 16)
        w = lambda k, shape: jax.random.normal(k, shape, jnp.float32) * 0.02
        return {'hidden_states': jax.random.normal(ks[0], (B, S, D), jnp.float32), 'ln1_w': jnp.ones((D,), jnp.float32), 'ln1_b': jnp.zeros((D,), jnp.float32), 'q_w': w(ks[1], (D, D)), 'q_b': jnp.zeros((D,), jnp.float32), 'k_w': w(ks[2], (D, D)), 'k_b': jnp.zeros((D,), jnp.float32), 'v_w': w(ks[3], (D, D)), 'v_b': jnp.zeros((D,), jnp.float32), 'o_w': w(ks[4], (D, D)), 'o_b': jnp.zeros((D,), jnp.float32), 'ln2_w': jnp.ones((D,), jnp.float32), 'ln2_b': jnp.zeros((D,), jnp.float32), 'router_w': w(ks[5], (D, E)), 'fc1_w': w(ks[6], (E, D, F)), 'fc1_b': jnp.zeros((E, F), jnp.float32), 'fc2_w': w(ks[7], (E, F, D)), 'fc2_b': jnp.zeros((E, D), jnp.float32)}
    _L0_ffn_in = _L0_ffn_setup()
    _d = {'L0_attn_x': _L0_attn_in['x'], 'L0_attn_wq': _L0_attn_in['wq'], 'L0_attn_bq': _L0_attn_in['bq'], 'L0_attn_wk': _L0_attn_in['wk'], 'L0_attn_bk': _L0_attn_in['bk'], 'L0_attn_wv': _L0_attn_in['wv'], 'L0_attn_bv': _L0_attn_in['bv'], 'L0_attn_wbeta': _L0_attn_in['wbeta'], 'L0_attn_bbeta': _L0_attn_in['bbeta'], 'L0_attn_wo': _L0_attn_in['wo'], 'L0_attn_bo': _L0_attn_in['bo'], 'L0_attn_w1': _L0_attn_in['w1'], 'L0_attn_b1': _L0_attn_in['b1'], 'L0_attn_w2': _L0_attn_in['w2'], 'L0_attn_b2': _L0_attn_in['b2'], 'L0_attn_ln1_scale': _L0_attn_in['ln1_scale'], 'L0_attn_ln2_scale': _L0_attn_in['ln2_scale'], 'L0_ffn_ln1_w': _L0_ffn_in['ln1_w'], 'L0_ffn_ln1_b': _L0_ffn_in['ln1_b'], 'L0_ffn_q_w': _L0_ffn_in['q_w'], 'L0_ffn_q_b': _L0_ffn_in['q_b'], 'L0_ffn_k_w': _L0_ffn_in['k_w'], 'L0_ffn_k_b': _L0_ffn_in['k_b'], 'L0_ffn_v_w': _L0_ffn_in['v_w'], 'L0_ffn_v_b': _L0_ffn_in['v_b'], 'L0_ffn_o_w': _L0_ffn_in['o_w'], 'L0_ffn_o_b': _L0_ffn_in['o_b'], 'L0_ffn_ln2_w': _L0_ffn_in['ln2_w'], 'L0_ffn_ln2_b': _L0_ffn_in['ln2_b'], 'L0_ffn_router_w': _L0_ffn_in['router_w'], 'L0_ffn_fc1_w': _L0_ffn_in['fc1_w'], 'L0_ffn_fc1_b': _L0_ffn_in['fc1_b'], 'L0_ffn_fc2_w': _L0_ffn_in['fc2_w'], 'L0_ffn_fc2_b': _L0_ffn_in['fc2_b']}
    _x0 = _d['L0_attn_x']
    _d['L0_attn_x'] = jax.random.normal(jax.random.fold_in(jax.random.key(seed), 1), (4, 1024, 128), dtype=_x0.dtype)
    del _x0
    return _d

def reference(L0_attn_x, L0_attn_wq, L0_attn_bq, L0_attn_wk, L0_attn_bk, L0_attn_wv, L0_attn_bv, L0_attn_wbeta, L0_attn_bbeta, L0_attn_wo, L0_attn_bo, L0_attn_w1, L0_attn_b1, L0_attn_w2, L0_attn_b2, L0_attn_ln1_scale, L0_attn_ln2_scale, L0_ffn_ln1_w, L0_ffn_ln1_b, L0_ffn_q_w, L0_ffn_q_b, L0_ffn_k_w, L0_ffn_k_b, L0_ffn_v_w, L0_ffn_v_b, L0_ffn_o_w, L0_ffn_o_b, L0_ffn_ln2_w, L0_ffn_ln2_b, L0_ffn_router_w, L0_ffn_fc1_w, L0_ffn_fc1_b, L0_ffn_fc2_w, L0_ffn_fc2_b):

    def _L0_attn_ref(x, wq, bq, wk, bk, wv, bv, wbeta, bbeta, wo, bo, w1, b1, w2, b2, ln1_scale, ln2_scale):
        import jax, jax.numpy as jnp
        import numpy as np
        B, S, D, H, DFF = (4, 256, 128, 16, 512)
        HD = D // H

        def rmsnorm(x, scale, eps=1e-06):
            var = jnp.mean(jnp.square(x), axis=-1, keepdims=True)
            return x * jax.lax.rsqrt(var + eps) * scale

        def gdn_attention(x, wq, bq, wk, bk, wv, bv, wbeta, bbeta, wo, bo):
            b, s, _ = x.shape
            q = (x @ wq + bq).reshape(b, s, H, HD)
            k = (x @ wk + bk).reshape(b, s, H, HD)
            v = (x @ wv + bv).reshape(b, s, H, HD)
            k = k / (jnp.linalg.norm(k, axis=-1, keepdims=True) + 1e-06)
            beta = jax.nn.sigmoid(x @ wbeta + bbeta)[..., None]
            q = jnp.transpose(q, (1, 0, 2, 3))
            k = jnp.transpose(k, (1, 0, 2, 3))
            v = jnp.transpose(v, (1, 0, 2, 3))
            beta = jnp.transpose(beta, (1, 0, 2, 3))

            def _step(Sm, inputs):
                q_t, k_t, v_t, beta_t = inputs
                Sk = jnp.einsum('bhde,bhe->bhd', Sm, k_t)
                delta = v_t - Sk
                Sm = Sm + beta_t[..., None] * jnp.einsum('bhd,bhe->bhde', delta, k_t)
                o_t = jnp.einsum('bhde,bhe->bhd', Sm, q_t)
                return (Sm, o_t)
            S0 = jnp.zeros((b, H, HD, HD), x.dtype)
            _, outputs = jax.lax.scan(_step, S0, (q, k, v, beta))
            outputs = jnp.transpose(outputs, (1, 0, 2, 3)).reshape(b, s, D)
            return outputs @ wo + bo
        residual = x
        h = rmsnorm(x, ln1_scale)
        h = gdn_attention(h, wq, bq, wk, bk, wv, bv, wbeta, bbeta, wo, bo)
        x = h + residual
        residual = x
        h = rmsnorm(x, ln2_scale)
        h = jax.nn.gelu(h @ w1 + b1) @ w2 + b2
        return h + residual

    def _L0_ffn_ref(hidden_states, ln1_w, ln1_b, q_w, q_b, k_w, k_b, v_w, v_b, o_w, o_b, ln2_w, ln2_b, router_w, fc1_w, fc1_b, fc2_w, fc2_b):
        import math
        import jax, jax.numpy as jnp
        import numpy as np
        B, S, D, H, E, F = (2, 128, 128, 16, 16, 512)
        HEAD = D // H
        MOE_TOKEN_DROPOUT = 0.2
        EPS = 1e-05

        def layer_norm(x, w, b):
            mu = x.mean(-1, keepdims=True)
            var = ((x - mu) ** 2).mean(-1, keepdims=True)
            return (x - mu) * jax.lax.rsqrt(var + EPS) * w + b
        b, s, _ = hidden_states.shape
        T = b * s
        neg = jnp.finfo(jnp.float32).min
        resid = hidden_states
        x = layer_norm(hidden_states, ln1_w, ln1_b)
        q = (x @ q_w + q_b) / math.sqrt(HEAD)
        k = x @ k_w + k_b
        v = x @ v_w + v_b
        split = lambda t: t.reshape(b, s, H, HEAD).transpose(0, 2, 1, 3)
        q, k, v = (split(q), split(k), split(v))
        scores = jnp.einsum('bhqd,bhkd->bhqk', q, k)
        causal = jnp.tril(jnp.ones((s, s), bool))
        scores = jnp.where(causal, scores, neg)
        attn = jax.nn.softmax(scores, axis=-1)
        ctx = jnp.einsum('bhqk,bhkd->bhqd', attn, v)
        ctx = ctx.transpose(0, 2, 1, 3).reshape(b, s, D)
        hidden = resid + (ctx @ o_w + o_b)
        resid = hidden
        xt = layer_norm(hidden, ln2_w, ln2_b).reshape(T, D)
        logits = xt @ router_w
        probs = jax.nn.softmax(logits, axis=-1)
        top1 = jnp.argmax(probs, axis=-1)
        m1 = jax.nn.one_hot(top1, E, dtype=jnp.float32)
        logits_no1 = jnp.where(m1 > 0, -jnp.inf, logits)
        top2 = jnp.argmax(logits_no1, axis=-1)
        m2 = jax.nn.one_hot(top2, E, dtype=jnp.float32)
        loc1 = jnp.cumsum(m1, axis=0) - 1.0
        loc2 = jnp.cumsum(m2, axis=0) - 1.0 + m1.sum(axis=0, keepdims=True)
        C = 2 * math.ceil(T / E)
        m1 = m1 * (loc1 < C)
        m2 = m2 * (loc2 < C)
        g1 = (probs * m1).sum(-1)
        g2 = (probs * m2).sum(-1)
        denom = jnp.maximum(g1 + g2, jnp.finfo(jnp.float32).eps)
        g1, g2 = (g1 / denom, g2 / denom)
        slot1 = (loc1 * m1).sum(-1).astype(jnp.int32)
        slot2 = (loc2 * m2).sum(-1).astype(jnp.int32)
        d1 = m1[:, :, None] * jax.nn.one_hot(slot1, C, dtype=jnp.float32)[:, None, :]
        d2 = m2[:, :, None] * jax.nn.one_hot(slot2, C, dtype=jnp.float32)[:, None, :]
        dispatch = d1 + d2
        combine = g1[:, None, None] * d1 + g2[:, None, None] * d2
        xin = jnp.einsum('tec,td->ecd', dispatch, xt)
        h = jnp.einsum('ecd,edf->ecf', xin, fc1_w) + fc1_b[:, None, :]
        h = jax.nn.gelu(h, approximate=False)
        eout = jnp.einsum('ecf,efd->ecd', h, fc2_w) + fc2_b[:, None, :]
        eout = eout * (1.0 - MOE_TOKEN_DROPOUT)
        moe_out = jnp.einsum('tec,ecd->td', combine, eout).reshape(b, s, D)
        return resid + moe_out
    x = L0_attn_x
    x = x + 0.5 * _L0_ffn_ref(_layernorm(x, axis=-1), L0_ffn_ln1_w, L0_ffn_ln1_b, L0_ffn_q_w, L0_ffn_q_b, L0_ffn_k_w, L0_ffn_k_b, L0_ffn_v_w, L0_ffn_v_b, L0_ffn_o_w, L0_ffn_o_b, L0_ffn_ln2_w, L0_ffn_ln2_b, L0_ffn_router_w, L0_ffn_fc1_w, L0_ffn_fc1_b, L0_ffn_fc2_w, L0_ffn_fc2_b)
    x = x + _L0_attn_ref(_layernorm(x, axis=-1), L0_attn_wq, L0_attn_bq, L0_attn_wk, L0_attn_bk, L0_attn_wv, L0_attn_bv, L0_attn_wbeta, L0_attn_bbeta, L0_attn_wo, L0_attn_bo, L0_attn_w1, L0_attn_b1, L0_attn_w2, L0_attn_b2, L0_attn_ln1_scale, L0_attn_ln2_scale)
    x = x + 0.5 * _L0_ffn_ref(_layernorm(x, axis=-1), L0_ffn_ln1_w, L0_ffn_ln1_b, L0_ffn_q_w, L0_ffn_q_b, L0_ffn_k_w, L0_ffn_k_b, L0_ffn_v_w, L0_ffn_v_b, L0_ffn_o_w, L0_ffn_o_b, L0_ffn_ln2_w, L0_ffn_ln2_b, L0_ffn_router_w, L0_ffn_fc1_w, L0_ffn_fc1_b, L0_ffn_fc2_w, L0_ffn_fc2_b)
    return x

_drawn_inputs = setup_inputs


def setup_inputs(seed=0):
    import zlib

    import numpy as np

    out = dict(_drawn_inputs(seed))
    spreads = {'L0_attn_bq': (0.0, 0.1),
     'L0_attn_bk': (0.0, 0.1),
     'L0_attn_bv': (0.0, 0.1),
     'L0_attn_bbeta': (0.0, 0.382),
     'L0_attn_bo': (0.0, 0.1),
     'L0_attn_b1': (0.0, 0.411),
     'L0_attn_b2': (0.0, 0.1),
     'L0_attn_ln1_scale': (1.0, 0.2),
     'L0_attn_ln2_scale': (1.0, 0.2),
     'L0_ffn_ln1_w': (1.0, 0.6),
     'L0_ffn_ln1_b': (0.0, 0.8),
     'L0_ffn_q_b': (0.0, 0.8),
     'L0_ffn_k_b': (0.0, 0.8),
     'L0_ffn_v_b': (0.0, 0.596),
     'L0_ffn_o_b': (0.0, 0.1),
     'L0_ffn_ln2_w': (1.0, 0.6),
     'L0_ffn_ln2_b': (0.0, 0.488),
     'L0_ffn_fc1_b': (0.0, 0.8),
     'L0_ffn_fc2_b': (0.0, 0.1)}
    factors = {'L0_ffn_q_w': 8.0,
     'L0_ffn_k_w': 8.0,
     'L0_ffn_v_w': 8.0,
     'L0_ffn_o_w': 4.011,
     'L0_ffn_fc1_w': 3.042,
     'L0_ffn_fc2_w': 2.765}
    for name, (base, spread) in spreads.items():
        noise = np.random.default_rng([zlib.crc32(name.encode()), seed]).standard_normal(out[name].shape)
        drawn = base * np.exp(spread * noise) if base else spread * noise
        out[name] = jnp.asarray(drawn.astype(out[name].dtype))
    for name, factor in factors.items():
        out[name] = (out[name] * factor).astype(out[name].dtype)
    return out
```

```python
from contextlib import ExitStack

import concourse.bass as bass
from concourse import mybir

F32 = mybir.dt.float32
BF16 = mybir.dt.bfloat16
U32 = mybir.dt.uint32
ALU = mybir.AluOpType
ACT = mybir.ActivationFunctionType
AX = mybir.AxisListType.X

P = 128
BATCH, SEQ, D = 4, 1024, 128
TOK = BATCH * SEQ
TILES = TOK // P
BT = SEQ // P
BCOL = BT * D
H, HD = 16, 8
GH = 4
GROUPS = H // GH
UNITS = BATCH * GROUPS
E, F = 16, 512
FC = F // P
CAP = 2 * ((TOK + E - 1) // E)
CC = CAP // P
SLOTS = E * CAP
LOWEST = -3.0e38
LN_EPS = 1e-5
RMS_EPS = 1e-6
F32_EPS = 1.1920928955078125e-07
Q_SPLIT = (0, 0, 0, 1, 1, 2)
K_SPLIT = (0, 1, 2, 0, 1, 0)
TERMS = len(Q_SPLIT)
KROWS = TERMS * HD
SROWS = KROWS + 3


PASSED = []


class Chain:

    def __init__(self, eng, sem):
        self.eng, self.sem, self.n, self.turn = eng, sem, 0, 0

    def link(self, ins):
        self.n += 1
        ins.then_inc(self.sem, 1)
        apart(self.eng, self.sem, self.turn + self.n)

    def each(self, turns, per_turn, first=0):
        base = self.n
        with self.eng.Fori(first, first + turns) as i:
            self.turn = i * per_turn - first * per_turn
            yield i
            assert self.n - base == per_turn, (self.n - base, per_turn)
        self.turn = 0
        self.n = base + turns * per_turn


class Core:

    def __init__(self, nc, ctx):
        self.nc = nc
        PASSED[:] = [self.sem(ctx, "passed")]

    def sb(self, ctx, name, shape, dt=F32):
        return ctx.enter_context(self.nc.sbuf_tensor(name, shape, dt))

    def ps(self, ctx, name, shape, dt=F32):
        return ctx.enter_context(self.nc.psum_tensor(name, shape, dt))

    def sem(self, ctx, name):
        return self.nc.alloc_semaphore(name)


def normalise(vec, link, out, x, mv, rstd):
    for t in range(BT):
        last = vec.tensor_scalar(out[:, t * D:(t + 1) * D], x[:, t * D:(t + 1) * D],
                                 mv[:, t, 0:1], rstd[:, t:t + 1], ALU.subtract, ALU.mult)
    link(last)


def per_column(vec, link, out, x, row, op):
    link(vec.tensor_tensor(out.rearrange("p (t d) -> p t d", d=D), x.rearrange("p (t d) -> p t d", d=D),
                           row[:, :].unsqueeze(1).to_broadcast([P, BT, D]), op))


def apart(eng, sem, count):
    eng.wait_ge(sem, count)
    if not isinstance(count, int):
        eng.sem_inc(PASSED[0], 1)


def reached(eng, sem, count):
    if not isinstance(count, int) or count > 0:
        eng.wait_ge(sem, count)


def constants(core, ctx, w):
    c = {}
    for name in ("ident", "upper", "ones"):
        c[name] = core.sb(ctx, name, [P, P])
    c["ident_b"] = core.sb(ctx, "ident_b", [P, P], BF16)
    c["causal"] = core.sb(ctx, "causal", [P, SEQ])
    c["rev"] = core.sb(ctx, "rev_expert", [P, E])
    c["num"] = core.sb(ctx, "expert_number", [P, E])
    c["spill"] = core.sb(ctx, "spill_row", [P, TILES])
    c["restart"] = core.sb(ctx, "restart", [P, E, TILES])
    c["eps"] = core.sb(ctx, "eps", [P, 2])
    c["zero"] = core.sb(ctx, "zero", [P, 2048])
    rows = ("L0_ffn_ln1_w", "L0_ffn_ln1_b", "L0_ffn_v_b", "L0_ffn_o_b", "L0_ffn_ln2_w", "L0_ffn_ln2_b")
    mats = ("L0_ffn_q_w", "L0_ffn_k_w", "L0_ffn_v_w", "L0_ffn_o_w")
    for n in rows:
        c[n] = core.sb(ctx, "row_" + n, [P, D])
    for n in mats:
        c[n] = core.sb(ctx, "sb_" + n, [P, D])
    c["router"] = core.sb(ctx, "sb_router", [P, E])
    c["qb"] = core.sb(ctx, "col_q_b", [P, 1])
    c["kb"] = core.sb(ctx, "col_k_b", [P, 1])
    loads = len(rows) + len(mats) + 3
    s_load = core.sem(ctx, "const_loaded")
    s_set = core.sem(ctx, "const_set")
    s_zero = core.sem(ctx, "zero_set")
    s_wipe = core.sem(ctx, "slots_wiped")
    nc = core.nc
    with nc.Block() as block:
        @block.sync
        def _(sp):
            for n in rows:
                sp.dma_start(c[n][:, :], w[n].partition_broadcast(P)).then_inc(s_load, 16)
            for n in mats:
                sp.dma_start(c[n][:, :], w[n]).then_inc(s_load, 16)
            sp.dma_start(c["router"][:, :], w["L0_ffn_router_w"]).then_inc(s_load, 16)
            sp.dma_start(c["qb"][:, :], w["L0_ffn_q_b"].rearrange("(p o) -> p o", o=1)).then_inc(s_load, 16)
            sp.dma_start(c["kb"][:, :], w["L0_ffn_k_b"].rearrange("(p o) -> p o", o=1)).then_inc(s_load, 16)
            sp.wait_ge(s_zero, 1)
            wiped = w["xin"][0:SLOTS, :].rearrange("(n p r) d -> n p (r d)", p=P, r=16)
            for n in range(SLOTS // (P * 16)):
                sp.dma_start(wiped[n], c["zero"][:, :]).then_inc(s_wipe, 16)
            sp.wait_ge(s_load, 16 * loads)
            sp.wait_ge(s_wipe, 16 * (SLOTS // (P * 16)))

        @block.vector
        def _(vec):
            vec.memset(c["zero"][:, :], 0.0).then_inc(s_zero, 1)
            vec.memset(c["eps"][:, 0:1], LN_EPS)
            vec.memset(c["eps"][:, 1:2], RMS_EPS)
            vec.memset(c["ones"][:, :], 1.0)

        @block.gpsimd
        def _(pool):
            chain = Chain(pool, s_set)
            chain.link(pool.memset(c["ident"][:, :], 0.0))
            chain.link(pool.affine_select(out=c["ident"][:, :], in_=c["ident"][:, :], compare_op=ALU.not_equal, fill=1.0,
                                          base=0, pattern=[[-1, P]], channel_multiplier=1))
            chain.link(pool.tensor_copy(c["ident_b"][:, :], c["ident"][:, :]))
            chain.link(pool.memset(c["upper"][:, :], 1.0))
            chain.link(pool.affine_select(out=c["upper"][:, :], in_=c["upper"][:, :], compare_op=ALU.is_ge, fill=0.0,
                                          base=0, pattern=[[1, P]], channel_multiplier=-1))
            chain.link(pool.memset(c["causal"][:, :], 0.0))
            chain.link(pool.affine_select(out=c["causal"][:, SEQ - P:], in_=c["causal"][:, SEQ - P:],
                                          compare_op=ALU.is_ge, fill=LOWEST,
                                          base=0, pattern=[[-1, P]], channel_multiplier=1))
            pool.iota(c["rev"][:, :], pattern=[[-1, E]], base=E, channel_multiplier=0,
                      allow_small_or_imprecise_dtypes=True)
            pool.iota(c["num"][:, :], pattern=[[1, E]], base=0, channel_multiplier=0,
                      allow_small_or_imprecise_dtypes=True)
            pool.iota(c["spill"][:, :], pattern=[[P, TILES]], base=SLOTS, channel_multiplier=1,
                      allow_small_or_imprecise_dtypes=True)
            chain.link(pool.memset(c["restart"][:, :, :], 1.0))
            chain.link(pool.memset(c["restart"][:, :, 0:1], 0.0))
    return c


def ffn_project(core, keep, w, c, x_dram, tag):
    nc = core.nc
    with ExitStack() as ctx:
        sb = lambda n, s, dt=F32: core.sb(ctx, n + tag, s, dt)
        ps = lambda n, s, dt=F32: core.ps(ctx, n + tag, s, dt)
        sem = lambda n: core.sem(ctx, n + tag)
        stats, mv, rstd = sb("stats", [P, BT, 6]), sb("mv", [P, BT, 2]), sb("rstd", [P, BT])
        std = sb("std", [P, BT])
        xn, xT = sb("xn", [P, BCOL]), sb("xT", [P, SEQ])
        full = [sb("qf", [P, SEQ]), sb("kf", [P, SEQ])]
        rest = [sb("qr", [P, SEQ]), sb("kr", [P, SEQ])]
        parts = [sb("qp", [P, 3, SEQ], BF16), sb("kp", [P, 3, SEQ], BF16)]
        pT, pV = ps("pT", [P, SEQ]), ps("pV", [P, BCOL])
        pQK = [ps("pQ", [P, SEQ]), ps("pK", [P, SEQ])]
        x_loaded, var_ready, std_ready = sem("x_loaded"), sem("var_ready"), sem("std_ready")
        xn_ready, xnT_ready, xT_ready = sem("xn_ready"), sem("xnT_ready"), sem("xT_ready")
        qk_ready, v_ready = sem("qk_ready"), sem("v_ready")
        parts_ready, parts_stored = sem("parts_ready"), sem("parts_stored")
        dve = sem("dve")
        x_rows = x_dram.rearrange("(b t p) d -> b p t d", p=P, t=BT)
        with nc.Block() as block:
            @block.sync
            def _(sp):
                with sp.Fori(0, BATCH) as b:
                    sp.dma_start(keep["x"][:, bass.ds(b * BCOL, BCOL)].rearrange("p (t d) -> p t d", d=D),
                                 x_rows[bass.ds(b, 1)].rearrange("o p t d -> (o p) t d")).then_inc(x_loaded, 16)
                    apart(sp, x_loaded, b * 16 + 16)

            @block.vector
            def _(vec):
                chain = Chain(vec, dve)
                link = chain.link
                for b in chain.each(BATCH, 17):
                    x = keep["x"][:, bass.ds(b * BCOL, BCOL)]
                    hidden = keep["hid"][:, bass.ds(b * BCOL, BCOL)]
                    apart(vec, x_loaded, b * 16 + 16)
                    for n, (src, dst) in enumerate(((x, hidden), (hidden, xn[:, :]))):
                        for t in range(BT):
                            last = vec.bn_stats(stats[:, t, :], src[:, t * D:(t + 1) * D])
                        link(last)
                        for t in range(BT):
                            last = vec.bn_aggr(mv[:, t, :], stats[:, t, :])
                        last.then_inc(var_ready, 1)
                        vec.wait_ge(std_ready, b * 2 + (n + 1))
                        link(vec.reciprocal(rstd[:, :], std[:, :]))
                        normalise(vec, link, dst, src, mv, rstd)
                    per_column(vec, link, xn[:, :], xn[:, :], c["L0_ffn_ln1_w"], ALU.mult)
                    per_column(vec, link, xn[:, :], xn[:, :], c["L0_ffn_ln1_b"], ALU.add)
                    vec.sem_inc(xn_ready, 1)
                    for s, bias in ((0, "qb"), (1, "kb")):
                        vec.wait_ge(qk_ready, b * 2 + (s + 1))
                        ins = vec.tensor_scalar(full[s][:, :], pQK[s][:, :], c[bias][:, 0:1],
                                                HD ** -0.5 if s == 0 else 1.0, ALU.add, ALU.mult)
                        link(ins)
                        link(vec.tensor_copy(parts[s][:, 0, :], full[s][:, :]))
                        link(vec.tensor_tensor(rest[s][:, :], full[s][:, :], parts[s][:, 0, :], ALU.subtract))
                        link(vec.tensor_copy(parts[s][:, 1, :], rest[s][:, :]))
                        vec.tensor_tensor(parts[s][:, 2, :], rest[s][:, :], parts[s][:, 1, :],
                                          ALU.subtract).then_inc(parts_ready, 1)
                    vec.wait_ge(v_ready, b + 1)
                    link(vec.tensor_tensor(
                        keep["v"][:, bass.ds(b * GROUPS * BT * GH * HD, GROUPS * BT * GH * HD)]
                        .rearrange("p (g t r) -> p g t r", g=GROUPS, t=BT),
                        pV[:, :].rearrange("p (t g r) -> p g t r", t=BT, g=GROUPS),
                        c["L0_ffn_v_b"][:, :].rearrange("p (g r) -> p g r", g=GROUPS).unsqueeze(2)
                        .to_broadcast([P, GROUPS, BT, GH * HD]), ALU.add))
                    vec.wait_ge(parts_stored, b * 96 + 96)

            @block.scalar
            def _(act):
                with act.Fori(0, BATCH) as b:
                    for n in range(2):
                        act.wait_ge(var_ready, b * 2 + (n + 1))
                        act.activation(std[:, :], mv[:, :, 1], ACT.Sqrt, bias=c["eps"][:, 0:1]).then_inc(std_ready, 1)
                    act.wait_ge(xnT_ready, b + 1)
                    act.copy(xT[:, :], pT[:, :]).then_inc(xT_ready, 1)
                    for s in range(2):
                        act.wait_ge(parts_ready, b * 2 + (s + 1))
                        for r in range(3):
                            act.dma_start(w["qk_parts"][s, r, bass.ds(b * GROUPS, GROUPS)]
                                          .rearrange("g h t -> (g h) t"), parts[s][:, r, :]).then_inc(parts_stored, 16)
                act.wait_ge(parts_stored, BATCH * 96)

            @block.tensor
            def _(pe):
                with pe.Fori(0, BATCH) as b:
                    pe.wait_ge(xn_ready, b + 1)
                    for t in range(BT):
                        last = pe.transpose(pT[:, t * P:(t + 1) * P], xn[:, t * D:(t + 1) * D], c["ident"][:, :])
                    last.then_inc(xnT_ready, 1)
                    pe.wait_ge(xT_ready, b + 1)
                    for s, name in ((0, "L0_ffn_q_w"), (1, "L0_ffn_k_w")):
                        for half in range(2):
                            last = pe.matmul(pQK[s][:, half * 512:(half + 1) * 512], c[name][:, :],
                                             xT[:, half * 512:(half + 1) * 512], start=True, stop=True)
                        last.then_inc(qk_ready, 1)
                    for t in range(BT):
                        last = pe.matmul(pV[:, t * D:(t + 1) * D], xT[:, t * P:(t + 1) * P], c["L0_ffn_v_w"][:, :],
                                         start=True, stop=True)
                    last.then_inc(v_ready, 1)


class Step:

    def __init__(self, u, stage, fills):
        self.u, self.stage, self.fills = u, stage, fills

    def shift(self, d):
        at = self.stage + d
        return Step(self.u + d, at % 3, self.fills + at // 3)


def attention_steps(eng, step, last_b, first_a):
    first_a(Step(0, 0, 0))
    step(Step(1, 1, 0))
    with eng.Fori(0, (UNITS - 4) // 3) as turn:
        for n in range(3):
            step(Step(turn * 3 + (n + 2), (n + 2) % 3, turn + (n + 2) // 3))
    for u in (UNITS - 2, UNITS - 1):
        step(Step(u, u % 3, u // 3))
    last_b(Step(UNITS, UNITS % 3, UNITS // 3))


def ffn_attention(core, keep, w, c, tag):
    nc = core.nc
    TILE_OF = [(h, i) for h in range(GH) for i in range(BT)]
    NT = len(TILE_OF)
    CHUNK = []
    for j in range(BT):
        for h in range(GH):
            if j < BT // 2:
                CHUNK.append((j, h, j * P, SEQ // 2))
            CHUNK.append((j, h, max(j * P, SEQ // 2), SEQ))
    NCH = len(CHUNK)
    DIAG = [j * P == a for j, h, a, e in CHUNK]
    NDIAG = sum(DIAG)
    NEV = NT + 2
    MAXIMA, CONTEXT = NT, NT + 1
    NB, NW = 2, 4
    LAG = 2
    with ExitStack() as ctx:
        sb = lambda n, s, dt=F32: core.sb(ctx, n + tag, s, dt)
        ps = lambda n, s, dt=F32: core.ps(ctx, n + tag, s, dt)
        sem = lambda n: core.sem(ctx, n + tag)
        qa = [sb(f"qa{i}", [64, GH, SEQ], BF16) for i in range(3)]
        ka = [sb(f"ka{i}", [64, GH, SEQ], BF16) for i in range(3)]
        va = [sb(f"va{i}", [P, BT, GH, 32]) for i in range(3)]
        mx, nm, nr = sb("mx", [P, BT, GH]), sb("nm", [P, BT, GH]), sb("nr", [P, BT, GH])
        nparts = sb("nparts", [P, BT, 3 * GH], BF16)
        mT = sb("mT", [3 * GH, SEQ], BF16)
        sums = [sb(f"sums{i}", [P, (i + 1) * P], BF16) for i in range(BT)]
        wt = [sb(f"wt{i}", [P, 512]) for i in range(NW)]
        cT = sb("cT", [P, SEQ])
        rden = sb("rden", [P, BT, GH])
        pA = [ps(f"pA{i}", [P, SEQ]) for i in range(2)]
        pB = [ps(f"pB{i}", [P, 512]) for i in range(NB)]
        pC = ps("pC", [P, SEQ])
        qk_loaded = [sem(f"qk_loaded{i}") for i in range(3)]
        v_staged = [sem(f"v_staged{i}") for i in range(3)]
        max_loaded = [sem(f"max_loaded{i}") for i in range(3)]
        a_done, a_used, mT_stored, nparts_ready = sem("a_done"), sem("a_used"), sem("mT_stored"), sem("nparts_ready")
        st_done, exp_done, masked, pv_done, cT_ready = (sem("st_done"), sem("exp_done"), sem("masked"),
                                                        sem("pv_done"), sem("cT_ready"))
        ones_set, va_chain, dve = sem("ones_set"), sem("va_chain"), sem("dve_a")

        def event(s, e):
            return s.u * NEV + (e - 1) if not isinstance(s.u, int) or s.u else e

        def context_event(s):
            return 0 if isinstance(s.u, int) and s.u == UNITS else CONTEXT

        def slot(s, e):
            return pA[(e - 1) % 2 if not isinstance(s.u, int) or s.u else e % 2]

        with nc.Block() as block:
            @block.sync
            def _(sp):
                def load(s):
                    for dst, which, split in ((qa[s.stage], 0, Q_SPLIT), (ka[s.stage], 1, K_SPLIT)):
                        for r in range(TERMS):
                            sp.dma_start(dst[r * HD:(r + 1) * HD, :, :],
                                         w["qk_parts"][which, split[r], bass.ds(s.u, 1)]
                                         .rearrange("o (h d) t -> (o d) h t", d=HD)).then_inc(qk_loaded[s.stage], 16)

                def maxima_rows(s):
                    sp.wait_ge(a_used, event(s, MAXIMA) + 1)
                    sp.dma_start(w["neg_max"][s.stage], mT[:, :]).then_inc(mT_stored, 16)
                    sp.wait_ge(mT_stored, s.u * 16 + 16)
                    sp.dma_start(qa[s.stage][KROWS:SROWS, :, :].rearrange("r h t -> r (h t)"),
                                 w["neg_max"][s.stage].rearrange("(s h) t -> s (h t)", s=3)
                                 ).then_inc(max_loaded[s.stage], 16)

                def first(s):
                    sp.wait_ge(ones_set, 1)
                    for d in range(3):
                        load(s.shift(d))
                    maxima_rows(s)

                def step(s):
                    maxima_rows(s)
                    if not isinstance(s.u, int) or s.u + 2 < UNITS:
                        sp.wait_ge(pv_done, s.u * NCH)
                        load(s.shift(2))

                attention_steps(sp, step, lambda s: None, first)

            @block.tensor
            def _(pe):
                def tile(s, e):
                    h, i = TILE_OF[e]
                    if e == 0:
                        pe.wait_ge(qk_loaded[s.stage], s.fills * 32 * TERMS + 32 * TERMS)
                    reached(pe, a_used, event(s, e) - 1)
                    for a in range(0, (i + 1) * P, 512):
                        b = min(a + 512, (i + 1) * P)
                        last = pe.matmul(slot(s, e)[:, a:b], qa[s.stage][0:KROWS, h, i * P:(i + 1) * P],
                                         ka[s.stage][0:KROWS, h, a:b], start=True, stop=True)
                    last.then_inc(a_done, 1)

                def maxima(s):
                    pe.wait_ge(nparts_ready, s.u + 1)
                    reached(pe, a_used, event(s, MAXIMA) - 1)
                    rows = slot(s, MAXIMA)[0:3 * GH, 0:SEQ // 2].bitcast(BF16)
                    for i in range(BT):
                        last = pe.transpose(rows[:, i * P:(i + 1) * P], nparts[:, i, :], c["ident_b"][:, :])
                    last.then_inc(a_done, 1)

                def scores(s, i):
                    j, h, a, e = CHUNK[i]
                    v = s.shift(-1)
                    if i == 0:
                        pe.wait_ge(max_loaded[v.stage], v.fills * 16 + 16)
                    reached(pe, exp_done, v.u * NCH + (i - NB + 1))
                    pe.matmul(pB[i % NB][:, 0:e - a], ka[v.stage][0:SROWS, h, j * P:(j + 1) * P],
                              qa[v.stage][0:SROWS, h, a:e], start=True, stop=True).then_inc(st_done, 1)

                def product(s, i):
                    j, h, a, e = CHUNK[i]
                    v = s.shift(-1)
                    if i == 0:
                        pe.wait_ge(v_staged[v.stage], v.fills + 1)
                        reached(pe, cT_ready, v.u)
                    if DIAG[i]:
                        pe.wait_ge(masked, v.u * NDIAG + (sum(DIAG[:i]) + 1))
                    else:
                        pe.wait_ge(exp_done, v.u * NCH + (i + 1))
                    top = BT // 2 - 1 if e == SEQ // 2 else BT - 1
                    pe.matmul(pC[32 * h:32 * h + 32, a:e], va[v.stage][:, j, h, :], wt[i % NW][:, 0:e - a],
                              start=j == 0, stop=j == top).then_inc(pv_done, 1)

                def context(s):
                    v = s.shift(-1)
                    pe.wait_ge(cT_ready, v.u + 1)
                    reached(pe, a_used, event(s, context_event(s)) - 1)
                    for i in range(BT):
                        last = pe.transpose(slot(s, context_event(s))[:, i * P:(i + 1) * P],
                                            cT[:, i * P:(i + 1) * P], c["ident"][:, :])
                    last.then_inc(a_done, 1)

                def first(s):
                    for e in range(NT):
                        tile(s, e)
                    maxima(s)

                def step(s):
                    for i in range(NCH):
                        scores(s, i)
                        if i < NT:
                            tile(s, i)
                        if i == NT + 4:
                            maxima(s)
                        if i >= LAG:
                            product(s, i - LAG)
                    for i in range(NCH - LAG, NCH):
                        product(s, i)
                    context(s)

                def last_b(s):
                    for i in range(NCH + LAG):
                        if i < NCH:
                            scores(s, i)
                        if i >= LAG:
                            product(s, i - LAG)
                    context(s)

                attention_steps(pe, step, last_b, first)

            @block.vector
            def _(vec):
                for st in range(3):
                    last = vec.memset(ka[st][:, :, :], 1.0)
                last.then_inc(ones_set, 1)
                links = [0]
                A_LINKS, C_LINKS = 4, 1

                def link(s, ins, n):
                    ins.then_inc(dve, 1)
                    base = A_LINKS + (s.u - 1) * (A_LINKS + C_LINKS) if not isinstance(s.u, int) or s.u else 0
                    vec.wait_ge(dve, base + (n + 1))

                def maxima(s):
                    for e, (h, i) in enumerate(TILE_OF):
                        n = (i + 1) * P
                        if e and i == 0:
                            apart(vec, a_used, event(s, e))
                        apart(vec, a_done, event(s, e) + 1)
                        vec.tensor_tensor_reduce(out=sums[i][:, :], in0=slot(s, e)[:, 0:n], in1=c["causal"][:, SEQ - n:],
                                                 scale=1.0, scalar=LOWEST, op0=ALU.add, op1=ALU.max,
                                                 accum_out=mx[:, i, h:h + 1]).then_inc(a_used, 1)
                    vec.wait_ge(a_used, event(s, NT))
                    link(s, vec.tensor_scalar(nm[:, :, :], mx[:, :, :], -1.0, None, ALU.mult), 0)
                    link(s, vec.tensor_copy(nparts[:, :, 0:GH], nm[:, :, :]), 1)
                    link(s, vec.tensor_tensor(nr[:, :, :], nm[:, :, :], nparts[:, :, 0:GH], ALU.subtract), 2)
                    link(s, vec.tensor_copy(nparts[:, :, GH:2 * GH], nr[:, :, :]), 3)
                    vec.tensor_tensor(nparts[:, :, 2 * GH:], nr[:, :, :], nparts[:, :, GH:2 * GH],
                                      ALU.subtract).then_inc(nparts_ready, 1)
                    vec.wait_ge(a_done, event(s, MAXIMA) + 1)
                    reached(vec, mT_stored, s.u * 16)
                    vec.tensor_copy(mT[:, :], slot(s, MAXIMA)[0:3 * GH, 0:SEQ // 2].bitcast(BF16)).then_inc(a_used, 1)

                def context(s):
                    e = context_event(s)
                    if e == 0:
                        vec.wait_ge(a_used, event(s, e))
                    vec.wait_ge(a_done, event(s, e) + 1)
                    rows = slot(s, e)[:, :].rearrange("p (t h r) -> p t h r", t=BT, h=GH)
                    n = A_LINKS if e else 0
                    link(s, vec.reciprocal(rden[:, :, :], rows[:, :, :, HD]), n)
                    size = BT * GH * HD
                    vec.tensor_tensor(keep["ctx"][:, bass.ds((s.u - 1) * size, size)]
                                      .rearrange("p (t h r) -> p t h r", t=BT, h=GH),
                                      rows[:, :, :, 0:HD], rden[:, :, :].unsqueeze(3).to_broadcast([P, BT, GH, HD]),
                                      ALU.mult).then_inc(a_used, 1)

                def step(s):
                    maxima(s)
                    context(s)

                attention_steps(vec, step, context, maxima)

            @block.scalar
            def _(act):
                def weights(s):
                    v = s.shift(-1)
                    for i, (j, h, a, e) in enumerate(CHUNK):
                        act.wait_ge(st_done, v.u * NCH + (i + 1))
                        reached(act, pv_done, v.u * NCH + (i - NW + 1))
                        act.activation(wt[i % NW][:, 0:e - a], pB[i % NB][:, 0:e - a], ACT.Exp).then_inc(exp_done, 1)
                    act.wait_ge(pv_done, v.u * NCH + NCH)
                    reached(act, a_done, event(s, 0) if not isinstance(s.u, int) or s.u > 1 else 0)
                    act.copy(cT[:, :], pC[:, :]).then_inc(cT_ready, 1)

                attention_steps(act, weights, weights, lambda s: None)

            @block.gpsimd
            def _(pool):
                size = BT * GH * HD

                def stage(s):
                    pool.tensor_copy(va[s.stage][:, :, :, 0:HD],
                                     keep["v"][:, bass.ds(s.u * size, size)]
                                     .rearrange("p (t h r) -> p t h r", t=BT, h=GH)).then_inc(v_staged[s.stage], 1)

                def first(s):
                    for st in range(3):
                        last = pool.memset(va[st][:, :, :, :], 0.0)
                    last.then_inc(va_chain, 1)
                    pool.wait_ge(va_chain, 1)
                    for st in range(3):
                        last = pool.memset(va[st][:, :, :, HD:HD + 1], 1.0)
                    last.then_inc(va_chain, 1)
                    pool.wait_ge(va_chain, 2)
                    for d in range(3):
                        stage(s.shift(d))

                def mask(s):
                    v = s.shift(-1)
                    n = 0
                    for i, (j, h, a, e) in enumerate(CHUNK):
                        if DIAG[i]:
                            apart(pool, exp_done, v.u * NCH + (i + 1))
                            block_ = wt[i % NW][:, 0:P]
                            pool.affine_select(out=block_, in_=block_, compare_op=ALU.is_ge, fill=0.0, base=0,
                                               pattern=[[1, P]], channel_multiplier=-1).then_inc(masked, 1)

                def step(s):
                    mask(s)
                    if not isinstance(s.u, int) or s.u + 2 < UNITS:
                        apart(pool, pv_done, s.u * NCH)
                        stage(s.shift(2))

                attention_steps(pool, step, mask, first)


def ffn_output(core, keep, w, c, tag):
    nc = core.nc
    with ExitStack() as ctx:
        sb = lambda n, s, dt=F32: core.sb(ctx, n + tag, s, dt)
        ps = lambda n, s, dt=F32: core.ps(ctx, n + tag, s, dt)
        sem = lambda n: core.sem(ctx, n + tag)
        rows, cT = sb("ctx_rows", [P, BCOL]), sb("ctxT", [P, SEQ])
        stats, mv = sb("stats_o", [P, BT, 6]), sb("mv_o", [P, BT, 2])
        std, rstd = sb("std_o", [P, BT]), sb("rstd_o", [P, BT])
        xn, xnT = sb("xn_o", [P, BCOL]), sb("xnT_o", [P, SEQ])
        pT, pO, pX, pL = ps("pT_o", [P, SEQ]), ps("pO", [P, BCOL]), ps("pX_o", [P, SEQ]), ps("pL", [P, BT * E])
        rows_ready, T_done, T_ready, o_done = sem("rows_ready"), sem("T_done"), sem("T_ready"), sem("o_done")
        var_ready, std_ready, xn_ready, logits_done = sem("var_o"), sem("std_rdy_o"), sem("xn_ready_o"), sem("logits_done")
        xn_kept, dve = sem("xn_kept"), sem("dve_o")
        with nc.Block() as block:
            @block.gpsimd
            def _(pool):
                with pool.Fori(0, BATCH) as b:
                    pool.tensor_copy(rows[:, :].rearrange("p (t g r) -> p g t r", t=BT, g=GROUPS),
                                     keep["ctx"][:, bass.ds(b * BCOL, BCOL)]
                                     .rearrange("p (g t r) -> p g t r", g=GROUPS, t=BT)).then_inc(rows_ready, 1)
                    apart(pool, xn_ready, b + 1)
                    pool.tensor_copy(keep["xt"][:, bass.ds(b * BCOL, BCOL)], xn[:, :]).then_inc(xn_kept, 1)
                    apart(pool, xn_kept, b + 1)

            @block.tensor
            def _(pe):
                with pe.Fori(0, BATCH) as b:
                    pe.wait_ge(rows_ready, b + 1)
                    for t in range(BT):
                        last = pe.transpose(pT[:, t * P:(t + 1) * P], rows[:, t * D:(t + 1) * D], c["ident"][:, :])
                    last.then_inc(T_done, 1)
                    pe.wait_ge(T_ready, b * 2 + 1)
                    for t in range(BT):
                        last = pe.matmul(pO[:, t * D:(t + 1) * D], cT[:, t * P:(t + 1) * P], c["L0_ffn_o_w"][:, :],
                                         start=True, stop=True)
                    last.then_inc(o_done, 1)
                    pe.wait_ge(xn_ready, b + 1)
                    for t in range(BT):
                        last = pe.transpose(pX[:, t * P:(t + 1) * P], xn[:, t * D:(t + 1) * D], c["ident"][:, :])
                    last.then_inc(T_done, 1)
                    pe.wait_ge(T_ready, b * 2 + 2)
                    for t in range(BT):
                        last = pe.matmul(pL[:, t * E:(t + 1) * E], xnT[:, t * P:(t + 1) * P], c["router"][:, :],
                                         start=True, stop=True)
                    last.then_inc(logits_done, 1)

            @block.scalar
            def _(act):
                with act.Fori(0, BATCH) as b:
                    act.wait_ge(T_done, b * 2 + 1)
                    act.copy(cT[:, :], pT[:, :]).then_inc(T_ready, 1)
                    act.wait_ge(var_ready, b + 1)
                    act.activation(std[:, :], mv[:, :, 1], ACT.Sqrt, bias=c["eps"][:, 0:1]).then_inc(std_ready, 1)
                    act.wait_ge(T_done, b * 2 + 2)
                    act.copy(xnT[:, :], pX[:, :]).then_inc(T_ready, 1)

            @block.vector
            def _(vec):
                chain = Chain(vec, dve)
                link = chain.link
                for b in chain.each(BATCH, 8):
                    hidden = keep["hid"][:, bass.ds(b * BCOL, BCOL)]
                    vec.wait_ge(o_done, b + 1)
                    link(vec.tensor_tensor(hidden, hidden, pO[:, :], ALU.add))
                    per_column(vec, link, hidden, hidden, c["L0_ffn_o_b"], ALU.add)
                    for t in range(BT):
                        last = vec.bn_stats(stats[:, t, :], hidden[:, t * D:(t + 1) * D])
                    link(last)
                    for t in range(BT):
                        last = vec.bn_aggr(mv[:, t, :], stats[:, t, :])
                    last.then_inc(var_ready, 1)
                    vec.wait_ge(std_ready, b + 1)
                    link(vec.reciprocal(rstd[:, :], std[:, :]))
                    normalise(vec, link, xn[:, :], hidden, mv, rstd)
                    per_column(vec, link, xn[:, :], xn[:, :], c["L0_ffn_ln2_w"], ALU.mult)
                    per_column(vec, link, xn[:, :], xn[:, :], c["L0_ffn_ln2_b"], ALU.add)
                    vec.sem_inc(xn_ready, 1)
                    vec.wait_ge(logits_done, b + 1)
                    link(vec.tensor_copy(keep["logits"][:, bass.ds(b * BT * E, BT * E)], pL[:, :]))
                    vec.wait_ge(xn_kept, b + 1)


def ffn_route(core, keep, c, tag):
    nc = core.nc
    with ExitStack() as ctx:
        sb = lambda n, s, dt=F32: core.sb(ctx, n + tag, s, dt)
        sem = lambda n: core.sem(ctx, n + tag)
        G = [P, TILES, E]
        prob, logit2, work, one = sb("prob", G), sb("logit2", G), sb("work_r", G), [sb("top1", G), sb("top2", G)]
        kept, loc = [sb("kept1", G), sb("kept2", G)], [sb("loc1", G), sb("loc2", G)]
        tot, run = [sb("tot1", [P, E, TILES]), sb("tot2", [P, E, TILES])], [sb("run1", [P, E, TILES]), sb("run2", [P, E, TILES])]
        best, first, total, recip = (sb(n, [P, TILES]) for n in ("best", "first", "total", "recip"))
        gate, at, dropped = (sb("gate", [P, 2, TILES]), sb("at", [P, 2, TILES]), sb("dropped", [P, TILES]))
        place = sb("place", [P, 2, TILES])
        pCum = [core.ps(ctx, f"pCum{i}{tag}", [P, TILES * E]) for i in range(2)]
        pTot = [core.ps(ctx, f"pTot{i}{tag}", [P, TILES * E]) for i in range(2)]
        max_found, exps_ready, one_ready, counted, dve = (sem("max_found"), sem("exps_ready"), sem("one_ready"),
                                                          sem("counted"), sem("dve_r"))
        over_e = lambda v: v.unsqueeze(2).to_broadcast(G)
        over_t = lambda v: v.unsqueeze(1).to_broadcast(G)
        L = keep["logits"][:, :].rearrange("p (t e) -> p t e", e=E)
        with nc.Block() as block:
            @block.vector
            def _(vec):
                link = Chain(vec, dve).link

                def top(values, n):
                    link(vec.reduce_max(best[:, :], values, AX))
                    link(vec.tensor_tensor(work[:, :, :], values, over_e(best[:, :]), ALU.is_equal))
                    link(vec.tensor_tensor(work[:, :, :], work[:, :, :], over_t(c["rev"][:, :]), ALU.mult))
                    link(vec.reduce_max(first[:, :], work[:, :, :], AX))
                    vec.tensor_tensor(one[n][:, :, :], over_t(c["rev"][:, :]), over_e(first[:, :]),
                                      ALU.is_equal).then_inc(one_ready, 1)
                    vec.wait_ge(one_ready, n + 1)

                link(vec.reduce_max(best[:, :], L, AX))
                vec.tensor_tensor(work[:, :, :], L, over_e(best[:, :]), ALU.subtract).then_inc(max_found, 1)
                vec.wait_ge(exps_ready, 1)
                link(vec.reduce_sum(total[:, :], prob[:, :, :], AX))
                link(vec.reciprocal(recip[:, :], total[:, :]))
                link(vec.tensor_tensor(prob[:, :, :], prob[:, :, :], over_e(recip[:, :]), ALU.mult))
                top(prob[:, :, :], 0)
                link(vec.scalar_tensor_tensor(logit2[:, :, :], one[0][:, :, :], LOWEST, L, ALU.mult, ALU.add))
                top(logit2[:, :, :], 1)
                for n in range(2):
                    vec.wait_ge(counted, n + 1)
                    link(vec.tensor_copy(tot[n][:, :, :], pTot[n][:, :].rearrange("p (t e) -> p e t", e=E)))
                    link(vec.tensor_tensor_scan(run[n][:, :, :].rearrange("p e t -> p (e t)"),
                                                c["restart"][:, :, :].rearrange("p e t -> p (e t)"),
                                                tot[n][:, :, :].rearrange("p e t -> p (e t)"), 0.0, ALU.mult, ALU.add))
                    link(vec.tensor_tensor(tot[n][:, :, :], run[n][:, :, :], tot[n][:, :, :], ALU.subtract))
                    link(vec.scalar_tensor_tensor(loc[n][:, :, :], pCum[n][:, :].rearrange("p (t e) -> p t e", e=E), -1.0,
                                                  tot[n][:, :, :].rearrange("p e t -> p t e"), ALU.add, ALU.add))
                    if n == 1:
                        link(vec.tensor_tensor(loc[1][:, :, :], loc[1][:, :, :], over_t(run[0][:, :, TILES - 1]), ALU.add))
                    link(vec.scalar_tensor_tensor(kept[n][:, :, :], loc[n][:, :, :], float(CAP), one[n][:, :, :],
                                                  ALU.is_lt, ALU.mult))
                    link(vec.tensor_tensor(work[:, :, :], prob[:, :, :], kept[n][:, :, :], ALU.mult))
                    link(vec.reduce_sum(gate[:, n, :], work[:, :, :], AX))
                    link(vec.scalar_tensor_tensor(loc[n][:, :, :], over_t(c["num"][:, :]), float(CAP), loc[n][:, :, :],
                                                  ALU.mult, ALU.add))
                    link(vec.tensor_tensor(work[:, :, :], loc[n][:, :, :], kept[n][:, :, :], ALU.mult))
                    link(vec.reduce_sum(at[:, n, :], work[:, :, :], AX))
                    link(vec.tensor_copy(keep["take"][:, n, :], at[:, n, :]))
                    link(vec.reduce_sum(dropped[:, :], kept[n][:, :, :], AX))
                    link(vec.tensor_scalar(dropped[:, :], dropped[:, :], -1.0, 1.0, ALU.mult, ALU.add))
                    link(vec.scalar_tensor_tensor(place[:, n, :], c["spill"][:, :], float(n * TOK), dropped[:, :],
                                                  ALU.add, ALU.mult))
                    link(vec.tensor_tensor(place[:, n, :], place[:, n, :], at[:, n, :], ALU.add))
                    link(vec.tensor_copy(keep["send"][:, n, :], place[:, n, :]))
                link(vec.tensor_tensor(total[:, :], gate[:, 0, :], gate[:, 1, :], ALU.add))
                link(vec.tensor_scalar(total[:, :], total[:, :], F32_EPS, None, ALU.max))
                link(vec.reciprocal(recip[:, :], total[:, :]))
                vec.tensor_tensor(keep["gate"][:, :, :], gate[:, :, :],
                                  recip[:, :].unsqueeze(1).to_broadcast([P, 2, TILES]), ALU.mult)

            @block.scalar
            def _(act):
                act.wait_ge(max_found, 1)
                act.activation(prob[:, :, :], work[:, :, :], ACT.Exp).then_inc(exps_ready, 1)

            @block.tensor
            def _(pe):
                for n in range(2):
                    pe.wait_ge(one_ready, n + 1)
                    flat = one[n][:, :, :].rearrange("p t e -> p (t e)")
                    pe.matmul(pCum[n][:, :], c["upper"][:, :], flat, start=True, stop=True)
                    pe.matmul(pTot[n][:, :], c["ones"][:, :], flat, start=True, stop=True).then_inc(counted, 1)


def ffn_experts(core, keep, w, c, x_out, tag):
    nc = core.nc
    with ExitStack() as ctx:
        sb = lambda n, s, dt=F32: core.sb(ctx, n + tag, s, dt)
        ps = lambda n, s, dt=F32: core.ps(ctx, n + tag, s, dt)
        sem = lambda n: core.sem(ctx, n + tag)
        two = range(2)
        xi = [sb(f"xi{i}", [P, CC, D]) for i in two]
        w1 = [sb(f"w1_{i}", [P, F]) for i in two]
        w2 = [sb(f"w2_{i}", [P, FC, D]) for i in two]
        b1 = [sb(f"b1_{i}", [P, FC]) for i in two]
        b2 = [sb(f"b2_{i}", [P, D]) for i in two]
        b2s = [sb(f"b2s_{i}", [P, D]) for i in two]
        xiT = sb("xiT", [P, CAP])
        hT = [sb(f"hT{i}", [P, CAP]) for i in range(FC)]
        eo = [sb(f"eo{i}", [P, CC, D]) for i in two]
        pX = ps("pXi", [P, CAP])
        pH = [ps(f"pH{i}", [P, CAP]) for i in range(FC)]
        pO = [ps(f"pOe{i}", [P, CC, D]) for i in two]
        sent = sem("sent")
        x_loaded = [sem(f"xi_loaded{i}") for i in two]
        w_loaded = [sem(f"we_loaded{i}") for i in two]
        xT_done, xT_ready, h_done, h_ready, o_done, o_ready, b_ready = (
            sem(n) for n in ("xiT_done", "xiT_ready", "h_done", "h_ready", "oe_done", "oe_ready", "b2s_ready"))
        stored = [sem(f"eo_stored{i}") for i in two]
        xin = w["xin"][0:SLOTS, :].rearrange("(e p c) d -> e p c d", p=P, c=CC)
        eout = w["eout"].rearrange("(e p c) d -> e p c d", p=P, c=CC)
        with nc.Block() as block:
            @block.gpsimd
            def _(pool):
                for t in range(TILES):
                    for n in two:
                        pool.indirect_dma_start(
                            out=w["xin"], out_offset=bass.IndirectOffsetOnAxis(ap=keep["send"][:, n, t:t + 1], axis=0),
                            in_=keep["xt"][:, t * D:(t + 1) * D], in_offset=None).then_inc(sent, 16)

            def experts(eng, one_expert):
                for n in two:
                    one_expert(n, n, 0)
                with eng.Fori(1, E // 2) as turn:
                    for n in two:
                        one_expert(turn * 2 + n, n, turn)

            @block.sync
            def _(sp):
                def load(e, n, turn):
                    if not isinstance(e, int):
                        sp.wait_ge(o_ready, e - 1)
                        sp.wait_ge(o_done, e - 1)
                    for dst, src in ((w1[n][:, :], w["L0_ffn_fc1_w"][bass.ds(e, 1)].rearrange("o d f -> (o d) f")),
                                     (w2[n][:, :, :], w["L0_ffn_fc2_w"][bass.ds(e, 1)]
                                      .rearrange("o (p c) d -> (o p) c d", c=FC)),
                                     (b1[n][:, :], w["L0_ffn_fc1_b"][bass.ds(e, 1)]
                                      .rearrange("o (p c) -> (o p) c", c=FC)),
                                     (b2[n][:, :], w["L0_ffn_fc2_b"][bass.ds(e, 1)]
                                      .rearrange("o d -> (o d)").partition_broadcast(P))):
                        sp.dma_start(dst, src).then_inc(w_loaded[n], 16)
                    if isinstance(e, int):
                        sp.wait_ge(sent, 16 * 2 * TILES)
                    sp.dma_start(xi[n][:, :, :], xin[bass.ds(e, 1)].rearrange("o p c d -> (o p) c d")
                                 ).then_inc(x_loaded[n], 16)

                experts(sp, load)

            @block.tensor
            def _(pe):
                def run(e, n, turn):
                    pe.wait_ge(x_loaded[n], turn * 16 + 16)
                    for cc in range(CC):
                        last = pe.transpose(pX[:, cc * P:(cc + 1) * P], xi[n][:, cc, :], c["ident"][:, :])
                    last.then_inc(xT_done, 1)
                    pe.wait_ge(w_loaded[n], turn * 64 + 64)
                    pe.wait_ge(xT_ready, e + 1)
                    cols = w1[n][:, :].rearrange("d (p c) -> d c p", c=FC)
                    for f in range(FC):
                        pe.matmul(pH[f][:, :], cols[:, f, :], xiT[:, :], start=True, stop=True).then_inc(h_done, 1)
                    pe.wait_ge(h_ready, e * FC + FC)
                    if not isinstance(e, int):
                        pe.wait_ge(o_ready, e - 1)
                    for cc in range(CC):
                        for f in range(FC):
                            last = pe.matmul(pO[n][:, cc, :], hT[f][:, cc * P:(cc + 1) * P], w2[n][:, f, :],
                                             start=f == 0, stop=f == FC - 1)
                    last.then_inc(o_done, 1)

                experts(pe, run)

            @block.scalar
            def _(act):
                def gelu(e, n, turn):
                    act.wait_ge(w_loaded[n], turn * 64 + 64)
                    for f in range(FC):
                        act.wait_ge(h_done, e * FC + (f + 1))
                        if f == 0:
                            reached(act, o_done, e)
                        act.activation(hT[f][:, :], pH[f][:, :], ACT.Gelu, bias=b1[n][:, f:f + 1]).then_inc(h_ready, 1)
                    act.wait_ge(o_ready, e + 1)
                    act.dma_start(eout[bass.ds(e, 1)].rearrange("o p c d -> (o p) c d"),
                                  eo[n][:, :, :]).then_inc(stored[n], 16)

                experts(act, gelu)
                for n in two:
                    act.wait_ge(stored[n], 16 * (E // 2))

            @block.vector
            def _(vec):
                def finish(e, n, turn):
                    vec.wait_ge(xT_done, e + 1)
                    vec.tensor_copy(xiT[:, :], pX[:, :]).then_inc(xT_ready, 1)
                    vec.wait_ge(w_loaded[n], turn * 64 + 64)
                    vec.tensor_scalar(b2s[n][:, :], b2[n][:, :], 0.8, None, ALU.mult).then_inc(b_ready, 1)
                    vec.wait_ge(b_ready, e + 1)
                    vec.wait_ge(o_done, e + 1)
                    if not isinstance(e, int):
                        vec.wait_ge(stored[n], turn * 16)
                    vec.scalar_tensor_tensor(eo[n][:, :, :], pO[n][:, :, :], 0.8,
                                             b2s[n][:, :].unsqueeze(1).to_broadcast([P, CC, D]),
                                             ALU.mult, ALU.add).then_inc(o_ready, 1)

                experts(vec, finish)

    with ExitStack() as ctx:
        sb = lambda n, s, dt=F32: core.sb(ctx, n + tag, s, dt)
        sem = lambda n: core.sem(ctx, n + tag)
        got = [keep["ctx"], keep["xt"]]
        gathered = [sem(f"gathered{b}") for b in range(BATCH)]
        dve, x_ready, x_stored = sem("dve_c"), sem("x_ready"), sem("x_stored")
        x_rows = x_out.rearrange("(b t p) d -> b p t d", p=P, t=BT)
        T3 = [P, BT, D]
        with nc.Block() as block:
            @block.gpsimd
            def _(pool):
                for b in range(BATCH):
                    for t in range(b * BT, (b + 1) * BT):
                        for n in range(2):
                            pool.indirect_dma_start(
                                out=got[n][:, t * D:(t + 1) * D], out_offset=None, in_=w["eout"],
                                in_offset=bass.IndirectOffsetOnAxis(ap=keep["take"][:, n, t:t + 1], axis=0)
                            ).then_inc(gathered[b], 16)

            @block.vector
            def _(vec):
                link = Chain(vec, dve).link
                for b in range(BATCH):
                    vec.wait_ge(gathered[b], 16 * 2 * BT)
                    cols = slice(b * BCOL, (b + 1) * BCOL)
                    part = [got[n][:, cols].rearrange("p (t d) -> p t d", d=D) for n in range(2)]
                    for n in range(2):
                        gate = keep["gate"][:, n, b * BT:(b + 1) * BT].unsqueeze(2).to_broadcast(T3)
                        link(vec.tensor_tensor(part[n], part[n], gate, ALU.mult))
                    link(vec.tensor_tensor(got[0][:, cols], got[0][:, cols], got[1][:, cols], ALU.add))
                    link(vec.tensor_tensor(got[0][:, cols], got[0][:, cols], keep["hid"][:, cols], ALU.add))
                    vec.scalar_tensor_tensor(got[0][:, cols], got[0][:, cols], 0.5, keep["x"][:, cols],
                                             ALU.mult, ALU.add).then_inc(x_ready, 1)

            @block.sync
            def _(sp):
                for b in range(BATCH):
                    sp.wait_ge(x_ready, b + 1)
                    sp.dma_start(x_rows[b], got[0][:, b * BCOL:(b + 1) * BCOL].rearrange("p (t d) -> p t d", d=D)
                                 ).then_inc(x_stored, 16)
                sp.wait_ge(x_stored, 16 * BATCH)


def ffn(core, w, c, x, x_out, tag):
    with ExitStack() as ctx:
        keep = {n: core.sb(ctx, f"keep_{n}{tag}", [P, TILES * D]) for n in ("x", "hid", "v", "ctx")}
        keep["xt"] = keep["v"]
        keep["logits"] = core.sb(ctx, f"keep_logits{tag}", [P, TILES * E])
        keep["gate"] = core.sb(ctx, f"keep_gate{tag}", [P, 2, TILES])
        keep["take"] = core.sb(ctx, f"keep_take{tag}", [P, 2, TILES], U32)
        keep["send"] = core.sb(ctx, f"keep_send{tag}", [P, 2, TILES], U32)
        ffn_project(core, keep, w, c, x, tag)
        ffn_attention(core, keep, w, c, tag)
        ffn_output(core, keep, w, c, tag)
        ffn_route(core, keep, c, tag)
        ffn_experts(core, keep, w, c, x_out, tag)


QKVB = 3 * D + H
SEG = TOK // P
SEGS = SEQ // SEG
R2 = 2 * HD
DFC = F // P


def root_mean_square(vec, link, ms, mv):
    link(vec.tensor_tensor(ms[:, :], mv[:, :, 0], mv[:, :, 0], ALU.mult))
    return vec.tensor_tensor(ms[:, :], ms[:, :], mv[:, :, 1], ALU.add)


def delta_block(core, w, c, x_dram, x_out):
    nc = core.nc
    with ExitStack() as ctx:
        sb = lambda n, s, dt=F32: core.sb(ctx, "g_" + n, s, dt)
        sem = lambda n: core.sem(ctx, "g_" + n)
        x, hid = sb("x", [P, SEG * D]), sb("hid", [P, SEG * D])
        qkvb, kbeta = sb("qkvb", [P, SEG, QKVB]), sb("kbeta", [P, SEG, D])
        outs = sb("outs", [P, SEG, H, R2])
        wcat, bcat = sb("wcat", [P, QKVB]), sb("bcat", [P, QKVB])
        wo, w1, w2, b1 = sb("wo", [P, D]), sb("w1", [P, F]), sb("w2", [P, DFC, D]), sb("b1", [P, DFC])
        rows = {n: sb("row_" + n, [P, D]) for n in ("ln1_scale", "ln2_scale", "bo", "b2")}
        w_loaded = sem("w_loaded")
        xs = x_dram.rearrange("(p j) d -> p (j d)", j=SEG)
        with ExitStack() as in1:
            sb1 = lambda n, s, dt=F32: core.sb(in1, "g1_" + n, s, dt)
            sem1 = lambda n: core.sem(in1, "g1_" + n)
            stats, mv, ms = sb1("stats", [P, BT, 6]), sb1("mv", [P, BT, 2]), sb1("ms", [P, BT])
            std, rstd = sb1("std", [P, BT]), sb1("rstd", [P, BT])
            h, hT = sb1("h", [P, BCOL]), sb1("hT", [P, BCOL])
            sq, norm = sb1("sq", [P, BT, D]), sb1("norm", [P, BT, H])
            nstd = sb1("nstd", [P, BT, H])
            pT = core.ps(in1, "g1_pT", [P, BCOL])
            pP = [core.ps(in1, f"g1_pP{i}", [P, 512]) for i in range(4)]
            x_loaded, stat_ready, std_ready, h_ready = sem1("x_loaded"), sem1("stat_ready"), sem1("std_ready"), sem1("h_ready")
            T_done, T_ready, p_done, p_used = sem1("T_done"), sem1("T_ready"), sem1("p_done"), sem1("p_used")
            dve, norm_ready, nstd_ready = sem1("dve"), sem1("norm_ready"), sem1("nstd_ready")
            with nc.Block() as block:
                @block.sync
                def _(sp):
                    at = 0
                    for n, width in (("q", D), ("k", D), ("v", D), ("beta", H)):
                        sp.dma_start(wcat[:, at:at + width], w["L0_attn_w" + n]).then_inc(w_loaded, 16)
                        sp.dma_start(bcat[:, at:at + width], w["L0_attn_b" + n].partition_broadcast(P)
                                     ).then_inc(w_loaded, 16)
                        at += width
                    for n in rows:
                        sp.dma_start(rows[n][:, :], w["L0_attn_" + n].partition_broadcast(P)).then_inc(w_loaded, 16)
                    sp.dma_start(wo[:, :], w["L0_attn_wo"]).then_inc(w_loaded, 16)
                    sp.dma_start(w1[:, :], w["L0_attn_w1"]).then_inc(w_loaded, 16)
                    sp.dma_start(w2[:, :, :], w["L0_attn_w2"].rearrange("(c p) d -> p c d", p=P)).then_inc(w_loaded, 16)
                    sp.dma_start(b1[:, :], w["L0_attn_b1"].rearrange("(c p) -> p c", p=P),
                                 allow_slow_non_contiguous=True).then_inc(w_loaded, 16)
                    sp.wait_ge(w_loaded, 16 * 16)
                    with sp.Fori(0, BATCH) as b:
                        sp.dma_start(x[:, bass.ds(b * BCOL, BCOL)], xs[:, bass.ds(b * BCOL, BCOL)]).then_inc(x_loaded, 16)
                        apart(sp, x_loaded, b * 16 + 16)

                @block.vector
                def _(vec):
                    chain = Chain(vec, dve)
                    link = chain.link
                    vec.wait_ge(w_loaded, 16 * 16)
                    for b in chain.each(BATCH, 15):
                        xb, hb = x[:, bass.ds(b * BCOL, BCOL)], hid[:, bass.ds(b * BCOL, BCOL)]
                        apart(vec, x_loaded, b * 16 + 16)
                        for n, src in enumerate((xb, hb)):
                            for t in range(BT):
                                last = vec.bn_stats(stats[:, t, :], src[:, t * D:(t + 1) * D])
                            link(last)
                            for t in range(BT):
                                last = vec.bn_aggr(mv[:, t, :], stats[:, t, :])
                            link(last)
                            if n == 0:
                                vec.tensor_copy(ms[:, :], mv[:, :, 1]).then_inc(stat_ready, 1)
                            else:
                                root_mean_square(vec, link, ms, mv).then_inc(stat_ready, 1)
                            vec.wait_ge(std_ready, b * 2 + (n + 1))
                            link(vec.reciprocal(rstd[:, :], std[:, :]))
                            if n == 0:
                                normalise(vec, link, hb, xb, mv, rstd)
                        for t in range(BT):
                            last = vec.tensor_scalar(h[:, t * D:(t + 1) * D], hb[:, t * D:(t + 1) * D],
                                                     rstd[:, t:t + 1], None, ALU.mult)
                        link(last)
                        per_column(vec, link, h[:, :], h[:, :], rows["ln1_scale"], ALU.mult)
                        vec.sem_inc(h_ready, 1)
                        for t in range(BT):
                            vec.wait_ge(p_done, b * BT + (t + 1))
                            vec.tensor_tensor(qkvb[:, bass.ds(b * BT + t, 1), :].rearrange("p o c -> p (o c)"),
                                              pP[t % 4][:, 0:QKVB], bcat[:, :], ALU.add).then_inc(p_used, 1)
                        vec.wait_ge(p_used, b * BT + BT)
                        k = qkvb[:, bass.ds(b * BT, BT), D:2 * D]
                        link(vec.tensor_tensor(sq[:, :, :], k, k, ALU.mult))
                        vec.reduce_sum(norm[:, :, :], sq[:, :, :].rearrange("p t (h r) -> p t h r", r=HD),
                                       AX).then_inc(norm_ready, 1)
                        vec.wait_ge(nstd_ready, b * 2 + 2)
                        link(vec.tensor_scalar(nstd[:, :, :], nstd[:, :, :], 1e-6, None, ALU.add))
                        link(vec.reciprocal(norm[:, :, :], nstd[:, :, :]))
                        for t in range(BT):
                            kt = qkvb[:, bass.ds(b * BT + t, 1), D:2 * D].rearrange("p o (h r) -> p (o h) r", r=HD)
                            last = vec.tensor_tensor(kt, kt, norm[:, t, :].unsqueeze(2).to_broadcast([P, H, HD]), ALU.mult)
                        link(last)
                        for t in range(BT):
                            kt = qkvb[:, bass.ds(b * BT + t, 1), D:2 * D].rearrange("p o (h r) -> p (o h) r", r=HD)
                            bt = qkvb[:, bass.ds(b * BT + t, 1), 3 * D:].rearrange("p o h -> p (o h)")
                            last = vec.tensor_tensor(kbeta[:, bass.ds(b * BT + t, 1), :]
                                                     .rearrange("p o (h r) -> p (o h) r", r=HD), kt,
                                                     bt.unsqueeze(2).to_broadcast([P, H, HD]), ALU.mult)
                        link(last)

                @block.scalar
                def _(act):
                    with act.Fori(0, BATCH) as b:
                        for n in range(2):
                            act.wait_ge(stat_ready, b * 2 + (n + 1))
                            act.activation(std[:, :], ms[:, :], ACT.Sqrt, bias=c["eps"][:, n:n + 1]).then_inc(std_ready, 1)
                        act.wait_ge(T_done, b + 1)
                        act.copy(hT[:, :], pT[:, :]).then_inc(T_ready, 1)
                        act.wait_ge(norm_ready, b + 1)
                        act.activation(nstd[:, :, :], norm[:, :, :], ACT.Sqrt).then_inc(nstd_ready, 1)
                        beta = qkvb[:, bass.ds(b * BT, BT), 3 * D:]
                        act.activation(beta, beta, ACT.Sigmoid).then_inc(nstd_ready, 1)

                @block.tensor
                def _(pe):
                    pe.wait_ge(w_loaded, 16 * 16)
                    with pe.Fori(0, BATCH) as b:
                        pe.wait_ge(h_ready, b + 1)
                        for t in range(BT):
                            last = pe.transpose(pT[:, t * P:(t + 1) * P], h[:, t * D:(t + 1) * D], c["ident"][:, :])
                        last.then_inc(T_done, 1)
                        pe.wait_ge(T_ready, b + 1)
                        for t in range(BT):
                            if t >= 4:
                                pe.wait_ge(p_used, b * BT + (t - 3))
                            pe.matmul(pP[t % 4][:, 0:QKVB], hT[:, t * P:(t + 1) * P], wcat[:, :],
                                      start=True, stop=True).then_inc(p_done, 1)

        FULL = [P, H, R2, HD]
        with ExitStack() as in2:
            sb2 = lambda n, s, dt=F32: core.sb(in2, "g2_" + n, s, dt)
            sem2 = lambda n: core.sem(in2, "g2_" + n)
            R, prod, proq = sb2("R", FULL), sb2("prod", FULL), sb2("proq", FULL)
            Rk = sb2("Rk", [P, H, R2])
            pq = core.ps(in2, "g2_pq", [P, H * R2])
            start, dve, R_ready, q_mult, q_sum, q_kept = (sem2(n) for n in ("start", "dve", "R_ready", "q_mult", "q_sum", "q_kept"))
            stored, loaded = sem2("stored"), sem2("loaded")
            with nc.Block() as block:
                @block.gpsimd
                def _(pool):
                    pool.memset(R[:, :, :, :], 0.0).then_inc(start, 1)
                    pool.wait_ge(start, 1)
                    eye = R[:, :, HD:, :]
                    pool.affine_select(out=eye, in_=eye, compare_op=ALU.not_equal, fill=1.0, base=0,
                                       pattern=[[0, H], [1, HD], [-1, HD]], channel_multiplier=0).then_inc(start, 1)
                    with pool.Fori(0, SEG) as j:
                        pool.wait_ge(R_ready, j + 1)
                        q = qkvb[:, bass.ds(j, 1), 0:D].rearrange("p o (h r) -> p (o h) r", r=HD)
                        pool.tensor_tensor(proq[:, :, :, :], R[:, :, :, :], q.unsqueeze(2).to_broadcast(FULL),
                                           ALU.mult).then_inc(q_mult, 1)
                        apart(pool, q_sum, j + 1)

                @block.vector
                def _(vec):
                    chain = Chain(vec, dve)
                    link = chain.link
                    vec.wait_ge(start, 2)
                    def token(j):
                        k = qkvb[:, bass.ds(j, 1), D:2 * D].rearrange("p o (h r) -> p (o h) r", r=HD)
                        v = qkvb[:, bass.ds(j, 1), 2 * D:3 * D].rearrange("p o (h r) -> p (o h) r", r=HD)
                        kb = kbeta[:, bass.ds(j, 1), :].rearrange("p o (h r) -> p (o h) r", r=HD)
                        link(vec.tensor_tensor(prod[:, :, :, :], R[:, :, :, :], k.unsqueeze(2).to_broadcast(FULL), ALU.mult))
                        link(vec.reduce_sum(Rk[:, :, :], prod[:, :, :, :], AX))
                        link(vec.tensor_tensor(Rk[:, :, 0:HD], Rk[:, :, 0:HD], v, ALU.subtract))
                        link(vec.tensor_tensor(prod[:, :, :, :], Rk[:, :, :].unsqueeze(3).to_broadcast(FULL),
                                               kb.unsqueeze(2).to_broadcast(FULL), ALU.mult))
                        reached(vec, q_mult, j)
                        vec.tensor_tensor(R[:, :, :, :], R[:, :, :, :], prod[:, :, :, :], ALU.subtract).then_inc(R_ready, 1)
                        vec.wait_ge(R_ready, j + 1)

                    token(0)
                    for j in chain.each(SEG - 1, 4, first=1):
                        token(j)

                @block.tensor
                def _(pe):
                    with pe.Fori(0, SEG) as j:
                        pe.wait_ge(q_mult, j + 1)
                        for e in range(HD):
                            last = pe.matmul(pq[:, :], c["ident"][:, :], proq[:, :, :, e].rearrange("p h r -> p (h r)"),
                                             start=e == 0, stop=e == HD - 1)
                        last.then_inc(q_sum, 1)
                        pe.wait_ge(q_kept, j + 1)

                @block.scalar
                def _(act):
                    with act.Fori(0, SEG) as j:
                        act.wait_ge(q_sum, j + 1)
                        act.copy(outs[:, bass.ds(j, 1), :, :].rearrange("p o h r -> p (o h r)"), pq[:, :]).then_inc(q_kept, 1)

                @block.sync
                def _(sp):
                    sp.wait_ge(R_ready, SEG)
                    sp.dma_start(w["segments"].rearrange("p h x -> p (h x)"),
                                 R[:, :, :, :].rearrange("p h r e -> p (h r e)")).then_inc(stored, 16)
                    sp.wait_ge(stored, 16)

        with ExitStack() as in3:
            sb3 = lambda n, s, dt=F32: core.sb(in3, "g3_" + n, s, dt)
            sem3 = lambda n: core.sem(in3, "g3_" + n)
            Rt, S = sb3("Rt", [BATCH * H, SEGS, R2 * HD]), sb3("S", [BATCH * H, SEGS, HD, HD])
            prod, part = sb3("prod", [BATCH * H, HD, HD, HD]), sb3("part", [BATCH * H, HD, HD])
            loaded, dve, S_ready, stored = sem3("loaded"), sem3("dve"), sem3("S_ready"), sem3("stored")
            ALL = [BATCH * H, HD, HD, HD]
            with nc.Block() as block:
                @block.sync
                def _(sp):
                    for b in range(BATCH):
                        sp.dma_start(Rt[b * H:(b + 1) * H, :, :],
                                     w["segments"][b * SEGS:(b + 1) * SEGS].rearrange("s h x -> h s x")).then_inc(loaded, 16)
                    sp.wait_ge(S_ready, 1)
                    for b in range(BATCH):
                        sp.dma_start(w["entries"][b * SEGS:(b + 1) * SEGS].rearrange("s h x -> h s x"),
                                     S[b * H:(b + 1) * H, :, :, :].rearrange("p s d e -> p s (d e)")).then_inc(stored, 16)
                    sp.wait_ge(stored, 16 * BATCH)

                @block.vector
                def _(vec):
                    chain = Chain(vec, dve)
                    link = chain.link
                    link(vec.memset(S[:, 0:1, :, :], 0.0))
                    vec.wait_ge(loaded, 16 * BATCH)
                    for s in chain.each(SEGS - 1, 3):
                        Sv = S[:, bass.ds(s, 1), :, :].rearrange("p o d e -> p (o d) e")
                        M = Rt[:, bass.ds(s, 1), HD * HD:].rearrange("p o (e f) -> p (o f) e", e=HD)
                        local = Rt[:, bass.ds(s, 1), 0:HD * HD].rearrange("p o x -> p (o x)")
                        link(vec.tensor_tensor(prod[:, :, :, :], Sv.unsqueeze(2).to_broadcast(ALL),
                                               M.unsqueeze(1).to_broadcast(ALL), ALU.mult))
                        link(vec.reduce_sum(part[:, :, :], prod[:, :, :, :], AX))
                        link(vec.tensor_tensor(S[:, bass.ds(s + 1, 1), :, :].rearrange("p o d e -> p (o d e)"),
                                               part[:, :, :].rearrange("p d f -> p (d f)"), local, ALU.add))
                    vec.sem_inc(S_ready, 1)

        with ExitStack() as in4:
            sb4 = lambda n, s, dt=F32: core.sb(in4, "g4_" + n, s, dt)
            sem4 = lambda n: core.sem(in4, "g4_" + n)
            S = sb4("S", [P, H, HD, HD])
            prod = [sb4(f"prod{i}", [P, H, HD, HD]) for i in range(2)]
            stats, mv, ms = sb4("stats", [P, BT, 6]), sb4("mv", [P, BT, 2]), sb4("ms", [P, BT])
            std, rstd = sb4("std", [P, BT]), sb4("rstd", [P, BT])
            oT, h2, h2T = sb4("oT", [P, BCOL]), sb4("h2", [P, BCOL]), sb4("h2T", [P, BCOL])
            oloc, oloc_ready = sb4("oloc", [P, BT, D]), sem4("oloc_ready")
            gT = [sb4(f"gT{i}", [P, 512]) for i in range(DFC)]
            pT, pO = core.ps(in4, "g4_pT", [P, BCOL]), core.ps(in4, "g4_pO", [P, BCOL])
            pH = [core.ps(in4, f"g4_pH{i}", [P, 512]) for i in range(DFC)]
            (S_loaded, prod_ready, sum_done, T_ready, o_done, stat_ready, std_ready, h2_ready, hT_done, h_done,
             g_ready, y_done, y_ready, y_stored, dve) = (sem4(n) for n in (
                 "S_loaded", "prod_ready", "sum_done", "T_ready", "o_done", "stat_ready", "std_ready", "h2_ready",
                 "hT_done", "h_done", "g_ready", "y_done", "y_ready", "y_stored", "dve"))
            out_rows = x_out.rearrange("(p j) d -> p (j d)", j=SEG)
            HALF = [P, H, HD, HD]
            with nc.Block() as block:
                @block.sync
                def _(sp):
                    sp.dma_start(S[:, :, :, :].rearrange("p h d e -> p (h d e)"),
                                 w["entries"].rearrange("p h x -> p (h x)")).then_inc(S_loaded, 16)
                    with sp.Fori(0, BATCH) as b:
                        sp.wait_ge(y_ready, b + 1)
                        sp.dma_start(out_rows[:, bass.ds(b * BCOL, BCOL)], x[:, bass.ds(b * BCOL, BCOL)]).then_inc(y_stored, 16)
                    sp.wait_ge(y_stored, 16 * BATCH)

                @block.vector
                def _(vec):
                    chain = Chain(vec, dve)
                    link = chain.link
                    vec.wait_ge(S_loaded, 16)

                    for b in chain.each(BATCH, 10):
                        for t in range(BT):
                            if t >= 2:
                                vec.wait_ge(sum_done, b * BT + (t - 1))
                            Mq = outs[:, bass.ds(b * BT + t, 1), :, HD:].rearrange("p o h e -> p (o h) e")
                            vec.tensor_tensor(prod[t % 2][:, :, :, :], S[:, :, :, :], Mq.unsqueeze(2).to_broadcast(HALF),
                                              ALU.mult).then_inc(prod_ready, 1)
                        hb, xb = hid[:, bass.ds(b * BCOL, BCOL)], x[:, bass.ds(b * BCOL, BCOL)]
                        vec.wait_ge(o_done, b + 1)
                        link(vec.tensor_tensor(hb, hb, pO[:, :], ALU.add))
                        per_column(vec, link, hb, hb, rows["bo"], ALU.add)
                        for t in range(BT):
                            last = vec.bn_stats(stats[:, t, :], hb[:, t * D:(t + 1) * D])
                        link(last)
                        for t in range(BT):
                            last = vec.bn_aggr(mv[:, t, :], stats[:, t, :])
                        link(last)
                        root_mean_square(vec, link, ms, mv).then_inc(stat_ready, 1)
                        vec.wait_ge(std_ready, b + 1)
                        link(vec.reciprocal(rstd[:, :], std[:, :]))
                        for t in range(BT):
                            last = vec.tensor_scalar(h2[:, t * D:(t + 1) * D], hb[:, t * D:(t + 1) * D],
                                                     rstd[:, t:t + 1], None, ALU.mult)
                        link(last)
                        vec.tensor_tensor(h2[:, :].rearrange("p (t d) -> p t d", d=D), h2[:, :].rearrange("p (t d) -> p t d", d=D),
                                          rows["ln2_scale"][:, :].unsqueeze(1).to_broadcast([P, BT, D]),
                                          ALU.mult).then_inc(h2_ready, 1)
                        link(vec.tensor_tensor(xb, xb, hb, ALU.add))
                        per_column(vec, link, xb, xb, rows["b2"], ALU.add)
                        vec.wait_ge(y_done, b * 2 + 2)
                        link(vec.tensor_tensor(xb, xb, pO[:, :], ALU.add))
                        vec.sem_inc(y_ready, 1)

                @block.scalar
                def _(act):
                    with act.Fori(0, BATCH) as b:
                        act.wait_ge(sum_done, b * BT + BT)
                        act.copy(oT[:, :], pT[:, :]).then_inc(T_ready, 1)
                        act.wait_ge(stat_ready, b + 1)
                        act.activation(std[:, :], ms[:, :], ACT.Sqrt, bias=c["eps"][:, 1:2]).then_inc(std_ready, 1)
                        act.wait_ge(hT_done, b + 1)
                        act.copy(h2T[:, :], pT[:, :]).then_inc(T_ready, 1)
                        for half in range(2):
                            for f in range(DFC):
                                act.wait_ge(h_done, b * 8 + (half * DFC + f + 1))
                                if half == 1 and f == 0:
                                    act.wait_ge(y_done, b * 2 + 1)
                                act.activation(gT[f][:, :], pH[f][:, :], ACT.Gelu_apprx_tanh,
                                               bias=b1[:, f:f + 1]).then_inc(g_ready, 1)

                @block.tensor
                def _(pe):
                    with pe.Fori(0, BATCH) as b:
                        for t in range(BT):
                            pe.wait_ge(prod_ready, b * BT + (t + 1))
                            for e in range(HD):
                                pe.matmul(pT[:, t * P:(t + 1) * P], prod[t % 2][:, :, :, e].rearrange("p h d -> p (h d)"),
                                          c["ident"][:, :], start=e == 0, stop=False)
                            if t == 0:
                                pe.wait_ge(oloc_ready, b + 1)
                            pe.matmul(pT[:, t * P:(t + 1) * P], oloc[:, t, :], c["ident"][:, :],
                                      start=False, stop=True).then_inc(sum_done, 1)
                        pe.wait_ge(T_ready, b * 2 + 1)
                        for t in range(BT):
                            last = pe.matmul(pO[:, t * D:(t + 1) * D], oT[:, t * P:(t + 1) * P], wo[:, :], start=True, stop=True)
                        last.then_inc(o_done, 1)
                        pe.wait_ge(h2_ready, b + 1)
                        for t in range(BT):
                            last = pe.transpose(pT[:, t * P:(t + 1) * P], h2[:, t * D:(t + 1) * D], c["ident"][:, :])
                        last.then_inc(hT_done, 1)
                        pe.wait_ge(T_ready, b * 2 + 2)
                        for half in range(2):
                            for f in range(DFC):
                                pe.matmul(pH[f][:, :], w1[:, f * P:(f + 1) * P], h2T[:, half * 512:(half + 1) * 512],
                                          start=True, stop=True).then_inc(h_done, 1)
                            pe.wait_ge(g_ready, b * 8 + (half * DFC + DFC))
                            for t in range(4):
                                at = (half * 4 + t) * D
                                for f in range(DFC):
                                    last = pe.matmul(pO[:, at:at + D], gT[f][:, t * P:(t + 1) * P], w2[:, f, :],
                                                     start=f == 0, stop=f == DFC - 1)
                            last.then_inc(y_done, 1)

                @block.gpsimd
                def _(pool):
                    with pool.Fori(0, BATCH) as b:
                        apart(pool, prod_ready, b * BT + 1)
                        pool.tensor_copy(oloc[:, :, :].rearrange("p t (h r) -> p t h r", r=HD),
                                         outs[:, bass.ds(b * BT, BT), :, 0:HD]).then_inc(oloc_ready, 1)
                        apart(pool, sum_done, b * BT + BT)


def build(nc, names, aps, out):
    w = dict(zip(names, aps))
    with ExitStack() as ctx:
        core = Core(nc, ctx)
        scratch = lambda n, shape, dt=F32: nc.dram_tensor(n, shape, dt, kind="Internal").ap()
        w["qk_parts"] = scratch("qk_parts", [2, 3, UNITS, GH * HD, SEQ], BF16)
        w["neg_max"] = scratch("neg_max", [3, 3 * GH, SEQ], BF16)
        w["xin"] = scratch("xin", [SLOTS + TOK * 2, D])
        w["eout"] = scratch("eout", [SLOTS, D])
        w["segments"] = scratch("segments", [P, H, R2 * HD])
        w["entries"] = scratch("entries", [P, H, HD * HD])
        x1, x2 = scratch("x1", [TOK, D]), scratch("x2", [TOK, D])
        flat = lambda a: a.rearrange("b s d -> (b s) d")
        c = constants(core, ctx, w)
        with nc.cleanup_on_exit():
            ffn(core, w, c, flat(w["L0_attn_x"]), x1, "_1")
        with nc.cleanup_on_exit():
            delta_block(core, w, c, x1, x2)
        with nc.cleanup_on_exit():
            ffn(core, w, c, x2, flat(out), "_2")


_INS = ["L0_attn_x", "L0_attn_wq", "L0_attn_bq", "L0_attn_wk", "L0_attn_bk", "L0_attn_wv", "L0_attn_bv",
        "L0_attn_wbeta", "L0_attn_bbeta", "L0_attn_wo", "L0_attn_bo", "L0_attn_w1", "L0_attn_b1", "L0_attn_w2",
        "L0_attn_b2", "L0_attn_ln1_scale", "L0_attn_ln2_scale", "L0_ffn_ln1_w", "L0_ffn_ln1_b", "L0_ffn_q_w",
        "L0_ffn_q_b", "L0_ffn_k_w", "L0_ffn_k_b", "L0_ffn_v_w", "L0_ffn_v_b", "L0_ffn_o_w", "L0_ffn_o_b",
        "L0_ffn_ln2_w", "L0_ffn_ln2_b", "L0_ffn_router_w", "L0_ffn_fc1_w", "L0_ffn_fc1_b", "L0_ffn_fc2_w",
        "L0_ffn_fc2_b"]
_OUTS = [((4, 1024, 128), "float32")]


def kernel(**inputs):
    import numpy as _np
    import concourse.bacc as _bacc
    from concourse import mybir as _mybir
    from concourse.bass_utils import run_bass_kernel_spmd as _run

    nc = _bacc.Bacc("TRN2", target_bir_lowering=False, num_devices=1)
    arrays, args = {}, []
    for name in _INS:
        a = _np.ascontiguousarray(inputs[name])
        arrays[f"in_{name}_dram"] = a
        args.append(nc.dram_tensor(f"in_{name}_dram", a.shape, _mybir.dt.from_np(a.dtype), kind="ExternalInput").ap())
    for i, (shape, dtype) in enumerate(_OUTS):
        dt = _mybir.dt.from_np(_np.dtype(dtype))
        args.append(nc.dram_tensor(f"out_{i}_dram", shape, dt, kind="ExternalOutput").ap())
    build(nc, _INS, args[:-1], args[-1])
    r = _run(nc, [arrays], core_ids=[0])
    return r.results[0]["out_0_dram"]
```

```python
from contextlib import ExitStack

import concourse.bass as bass
from concourse import mybir

F32 = mybir.dt.float32
BF16 = mybir.dt.bfloat16
U32 = mybir.dt.uint32
ALU = mybir.AluOpType
ACT = mybir.ActivationFunctionType
AX = mybir.AxisListType.X

P = 128
BATCH, SEQ, D = 4, 1024, 128
TOK = BATCH * SEQ
TILES = TOK // P
BT = SEQ // P
BCOL = BT * D
H, HD = 16, 8
GH = 4
GROUPS = H // GH
UNITS = BATCH * GROUPS
E, F = 16, 512
FC = F // P
CAP = 2 * ((TOK + E - 1) // E)
CC = CAP // P
SLOTS = E * CAP
LOWEST = -3.0e38
LN_EPS = 1e-5
RMS_EPS = 1e-6
F32_EPS = 1.1920928955078125e-07
Q_SPLIT = (0, 0, 0, 1, 1, 2)
K_SPLIT = (0, 1, 2, 0, 1, 0)
TERMS = len(Q_SPLIT)
KROWS = TERMS * HD
MROW = P - 3


PASSED = []


class Chain:

    def __init__(self, eng, sem):
        self.eng, self.sem, self.n, self.turn = eng, sem, 0, 0

    def link(self, ins):
        self.n += 1
        ins.then_inc(self.sem, 1)
        apart(self.eng, self.sem, self.turn + self.n)

    def each(self, turns, per_turn, first=0):
        base = self.n
        with self.eng.Fori(first, first + turns) as i:
            self.turn = i * per_turn - first * per_turn
            yield i
            assert self.n - base == per_turn, (self.n - base, per_turn)
        self.turn = 0
        self.n = base + turns * per_turn


class Core:

    def __init__(self, nc, ctx):
        self.nc = nc
        PASSED[:] = [self.sem(ctx, "passed")]

    def sb(self, ctx, name, shape, dt=F32):
        return ctx.enter_context(self.nc.sbuf_tensor(name, shape, dt))

    def ps(self, ctx, name, shape, dt=F32):
        return ctx.enter_context(self.nc.psum_tensor(name, shape, dt))

    def sem(self, ctx, name):
        return self.nc.alloc_semaphore(name)


def normalise(vec, link, out, x, mv, rstd):
    for t in range(BT):
        last = vec.tensor_scalar(out[:, t * D:(t + 1) * D], x[:, t * D:(t + 1) * D],
                                 mv[:, t, 0:1], rstd[:, t:t + 1], ALU.subtract, ALU.mult)
    link(last)


def per_column(vec, link, out, x, row, op):
    link(vec.tensor_tensor(out.rearrange("p (t d) -> p t d", d=D), x.rearrange("p (t d) -> p t d", d=D),
                           row[:, :].unsqueeze(1).to_broadcast([P, BT, D]), op))


def apart(eng, sem, count):
    eng.wait_ge(sem, count)
    if not isinstance(count, int):
        eng.sem_inc(PASSED[0], 1)


def reached(eng, sem, count):
    if not isinstance(count, int) or count > 0:
        eng.wait_ge(sem, count)


def constants(core, ctx, w):
    c = {}
    for name in ("ident", "upper", "ones"):
        c[name] = core.sb(ctx, name, [P, P])
    c["ident_b"] = core.sb(ctx, "ident_b", [P, P], BF16)
    c["causal"] = core.sb(ctx, "causal", [P, SEQ])
    c["rev"] = core.sb(ctx, "rev_expert", [P, E])
    c["num"] = core.sb(ctx, "expert_number", [P, E])
    c["spill"] = core.sb(ctx, "spill_row", [P, TILES])
    c["restart"] = core.sb(ctx, "restart", [P, E, TILES])
    c["eps"] = core.sb(ctx, "eps", [P, 2])
    c["zero"] = core.sb(ctx, "zero", [P, 2048])
    rows = ("L0_ffn_v_b", "L0_ffn_o_b", "L0_ffn_ln2_w", "L0_ffn_ln2_b")
    mats = ("L0_ffn_q_w", "L0_ffn_k_w", "L0_ffn_v_w", "L0_ffn_o_w")
    for n in rows:
        c[n] = core.sb(ctx, "row_" + n, [P, D])
    for n in mats:
        c[n] = core.sb(ctx, "sb_" + n, [P, D])
    c["router"] = core.sb(ctx, "sb_router", [P, E])
    cols = {"qb": "L0_ffn_q_b", "kb": "L0_ffn_k_b", "ln1_w": "L0_ffn_ln1_w", "ln1_b": "L0_ffn_ln1_b"}
    for n in (*cols, "qb_scaled"):
        c[n] = core.sb(ctx, "col_" + n, [P, 1])
    loads = len(rows) + len(mats) + 1 + len(cols)
    s_load = core.sem(ctx, "const_loaded")
    s_set = core.sem(ctx, "const_set")
    s_zero = core.sem(ctx, "zero_set")
    s_wipe = core.sem(ctx, "slots_wiped")
    nc = core.nc
    with nc.Block() as block:
        @block.sync
        def _(sp):
            for n in rows:
                sp.dma_start(c[n][:, :], w[n].partition_broadcast(P)).then_inc(s_load, 16)
            for n in mats:
                sp.dma_start(c[n][:, :], w[n]).then_inc(s_load, 16)
            sp.dma_start(c["router"][:, :], w["L0_ffn_router_w"]).then_inc(s_load, 16)
            for n, vector in cols.items():
                sp.dma_start(c[n][:, :], w[vector].rearrange("(p o) -> p o", o=1)).then_inc(s_load, 16)
            sp.wait_ge(s_zero, 1)
            wiped = w["xin"][0:SLOTS, :].rearrange("(n p r) d -> n p (r d)", p=P, r=16)
            for n in range(SLOTS // (P * 16)):
                sp.dma_start(wiped[n], c["zero"][:, :]).then_inc(s_wipe, 16)
            sp.wait_ge(s_load, 16 * loads)
            sp.wait_ge(s_wipe, 16 * (SLOTS // (P * 16)))

        @block.vector
        def _(vec):
            vec.memset(c["zero"][:, :], 0.0).then_inc(s_zero, 1)
            vec.memset(c["eps"][:, 0:1], LN_EPS)
            vec.memset(c["eps"][:, 1:2], RMS_EPS)
            vec.memset(c["ones"][:, :], 1.0)
            vec.wait_ge(s_load, 16 * loads)
            vec.tensor_scalar(c["qb_scaled"][:, :], c["qb"][:, :], HD ** -0.5, None, ALU.mult)

        @block.gpsimd
        def _(pool):
            chain = Chain(pool, s_set)
            chain.link(pool.memset(c["ident"][:, :], 0.0))
            chain.link(pool.affine_select(out=c["ident"][:, :], in_=c["ident"][:, :], compare_op=ALU.not_equal, fill=1.0,
                                          base=0, pattern=[[-1, P]], channel_multiplier=1))
            chain.link(pool.tensor_copy(c["ident_b"][:, :], c["ident"][:, :]))
            chain.link(pool.memset(c["upper"][:, :], 1.0))
            chain.link(pool.affine_select(out=c["upper"][:, :], in_=c["upper"][:, :], compare_op=ALU.is_ge, fill=0.0,
                                          base=0, pattern=[[1, P]], channel_multiplier=-1))
            chain.link(pool.memset(c["causal"][:, :], 0.0))
            chain.link(pool.affine_select(out=c["causal"][:, SEQ - P:], in_=c["causal"][:, SEQ - P:],
                                          compare_op=ALU.is_ge, fill=LOWEST,
                                          base=0, pattern=[[-1, P]], channel_multiplier=1))
            pool.iota(c["rev"][:, :], pattern=[[-1, E]], base=E, channel_multiplier=0,
                      allow_small_or_imprecise_dtypes=True)
            pool.iota(c["num"][:, :], pattern=[[1, E]], base=0, channel_multiplier=0,
                      allow_small_or_imprecise_dtypes=True)
            pool.iota(c["spill"][:, :], pattern=[[P, TILES]], base=SLOTS, channel_multiplier=1,
                      allow_small_or_imprecise_dtypes=True)
            chain.link(pool.memset(c["restart"][:, :, :], 1.0))
            chain.link(pool.memset(c["restart"][:, :, 0:1], 0.0))
    return c


def attention_buffers(core, ctx, tag):
    a = {"qa": [core.sb(ctx, f"qa{i}{tag}", [P, GH, SEQ], BF16) for i in range(3)],
         "ka": [core.sb(ctx, f"ka{i}{tag}", [P, GH, SEQ], BF16) for i in range(3)],
         "va": [core.sb(ctx, f"va{i}{tag}", [P, BT, GH, 32]) for i in range(3)],
         "qk_loaded": [core.sem(ctx, f"qk_loaded{i}{tag}") for i in range(3)]}
    return a


def load_qk(sp, w, a, stage, u):
    for dst, which, split in ((a["qa"][stage], 0, Q_SPLIT), (a["ka"][stage], 1, K_SPLIT)):
        for r in range(TERMS):
            sp.dma_start(dst[r * HD:(r + 1) * HD, :, :],
                         w["qk_parts"][which, split[r], bass.ds(u, 1)]
                         .rearrange("o (h d) t -> (o d) h t", d=HD)).then_inc(a["qk_loaded"][stage], 16)


def batches(eng, one):
    one(0)
    with eng.Fori(1, BATCH) as b:
        one(b)


def ffn_project(core, keep, w, c, a, x_dram, tag):
    nc = core.nc
    with ExitStack() as ctx:
        sb = lambda n, s, dt=F32: core.sb(ctx, n + tag, s, dt)
        ps = lambda n, s, dt=F32: core.ps(ctx, n + tag, s, dt)
        sem = lambda n: core.sem(ctx, n + tag)
        stats, mv, rstd = sb("stats", [P, BT, 6]), sb("mv", [P, BT, 2]), sb("rstd", [P, BT])
        std = sb("std", [P, BT])
        xn, xT = sb("xn", [P, BCOL]), sb("xT", [P, SEQ])
        full = [sb("qf", [P, SEQ]), sb("kf", [P, SEQ])]
        rest = [sb("qr", [P, SEQ]), sb("kr", [P, SEQ])]
        parts = [sb("qp", [P, 3, SEQ], BF16), sb("kp", [P, 3, SEQ], BF16)]
        pT, pV = ps("pT", [P, SEQ]), ps("pV", [P, BCOL])
        pQK = [ps("pQ", [P, SEQ]), ps("pK", [P, SEQ])]
        x_loaded, var_ready, std_ready = sem("x_loaded"), sem("var_ready"), sem("std_ready")
        xn_ready, xnT_ready, xT_ready = sem("xn_ready"), sem("xnT_ready"), sem("xT_ready")
        qk_ready, v_ready, v_kept = sem("qk_ready"), sem("v_ready"), sem("v_kept")
        full_ready, rest_ready, second_ready = sem("full_ready"), sem("rest_ready"), sem("second_ready")
        parts_ready, parts_stored = sem("parts_ready"), sem("parts_stored")
        stages_set, va_zero, dve = sem("stages_set"), sem("va_zero"), sem("dve")
        x_rows = x_dram.rearrange("(b t p) d -> b p t d", p=P, t=BT)
        with nc.Block() as block:
            @block.sync
            def _(sp):
                with sp.Fori(0, BATCH) as b:
                    sp.dma_start(keep["x"][:, bass.ds(b * BCOL, BCOL)].rearrange("p (t d) -> p t d", d=D),
                                 x_rows[bass.ds(b, 1)].rearrange("o p t d -> (o p) t d")).then_inc(x_loaded, 16)
                    apart(sp, x_loaded, b * 16 + 16)

                def store(b):
                    for s in range(2):
                        sp.wait_ge(parts_ready, b * 2 + (s + 1))
                        for r in range(3):
                            sp.dma_start(w["qk_parts"][s, r, bass.ds(b * GROUPS, GROUPS)]
                                         .rearrange("g h t -> (g h) t"), parts[s][:, r, :]).then_inc(parts_stored, 16)

                store(0)
                sp.wait_ge(stages_set, 1)
                sp.wait_ge(parts_stored, 96)
                for u in range(3):
                    load_qk(sp, w, a, u, u)
                with sp.Fori(1, BATCH) as b:
                    store(b)
                sp.wait_ge(parts_stored, BATCH * 96)
                for u in range(3):
                    sp.wait_ge(a["qk_loaded"][u], 32 * TERMS)

            @block.gpsimd
            def _(pool):
                for st in range(3):
                    pool.memset(a["qa"][st][:, :, :], 0.0)
                    pool.memset(a["ka"][st][:, :, :], -1.0)
                    pool.memset(a["va"][st][:, :, :, :], 0.0).then_inc(va_zero, 1)
                pool.wait_ge(va_zero, 3)
                for st in range(3):
                    last = pool.memset(a["va"][st][:, :, :, HD:HD + 1], 1.0)
                last.then_inc(stages_set, 1)

            @block.vector
            def _(vec):
                chain = Chain(vec, dve)
                link = chain.link

                def norm(b, n):
                    x = keep["x"][:, bass.ds(b * BCOL, BCOL)]
                    hidden = keep["hid"][:, bass.ds(b * BCOL, BCOL)]
                    src, dst = ((x, hidden), (hidden, xn[:, :]))[n]
                    if n == 0:
                        apart(vec, x_loaded, b * 16 + 16)
                    for t in range(BT):
                        last = vec.bn_stats(stats[:, t, :], src[:, t * D:(t + 1) * D])
                    link(last)
                    for t in range(BT):
                        last = vec.bn_aggr(mv[:, t, :], stats[:, t, :])
                    last.then_inc(var_ready, 1)
                    vec.wait_ge(std_ready, b * 2 + (n + 1))
                    link(vec.reciprocal(rstd[:, :], std[:, :]))
                    if n == 1:
                        reached(vec, xnT_ready, b)
                    normalise(vec, link, dst, src, mv, rstd)
                    if n == 1:
                        vec.sem_inc(xn_ready, 1)

                def values(b):
                    vec.wait_ge(v_ready, b + 1)
                    vec.tensor_tensor(
                        keep["v"][:, bass.ds(b * GROUPS * BT * GH * HD, GROUPS * BT * GH * HD)]
                        .rearrange("p (g t r) -> p g t r", g=GROUPS, t=BT),
                        pV[:, :].rearrange("p (t g r) -> p g t r", t=BT, g=GROUPS),
                        c["L0_ffn_v_b"][:, :].rearrange("p (g r) -> p g r", g=GROUPS).unsqueeze(2)
                        .to_broadcast([P, GROUPS, BT, GH * HD]), ALU.add).then_inc(v_kept, 1)

                def remainder(b):
                    for s in range(2):
                        vec.wait_ge(full_ready, b * 2 + (s + 1))
                        vec.tensor_tensor(rest[s][:, :], full[s][:, :], parts[s][:, 0, :],
                                          ALU.subtract).then_inc(rest_ready, 1)

                def third(b):
                    for s in range(2):
                        vec.wait_ge(second_ready, b * 2 + (s + 1))
                        vec.tensor_tensor(parts[s][:, 2, :], rest[s][:, :], parts[s][:, 1, :],
                                          ALU.subtract).then_inc(parts_ready, 1)

                def batch(b):
                    norm(b + 1, 0)
                    values(b)
                    remainder(b)
                    norm(b + 1, 1)
                    third(b)

                norm(0, 0)
                norm(0, 1)
                batch(0)
                for b in chain.each(BATCH - 2, 6, first=1):
                    batch(b)
                values(BATCH - 1)
                remainder(BATCH - 1)
                third(BATCH - 1)

            @block.scalar
            def _(act):
                def root(b, n):
                    act.wait_ge(var_ready, b * 2 + (n + 1))
                    act.activation(std[:, :], mv[:, :, 1], ACT.Sqrt, bias=c["eps"][:, 0:1]).then_inc(std_ready, 1)

                def batch(b, more=True):
                    act.wait_ge(xnT_ready, b + 1)
                    reached(act, v_ready, b)
                    act.activation(xT[:, :], pT[:, :], ACT.Identity, bias=c["ln1_b"][:, 0:1],
                                   scale=c["ln1_w"][:, 0:1]).then_inc(xT_ready, 1)
                    if more:
                        root(b + 1, 0)
                    reached(act, parts_stored, b * 96)
                    for s, bias in ((0, "qb_scaled"), (1, "kb")):
                        scale = HD ** -0.5 if s == 0 else 1.0
                        act.wait_ge(qk_ready, b * 2 + (s + 1))
                        act.activation(full[s][:, :], pQK[s][:, :], ACT.Identity, bias=c[bias][:, 0:1], scale=scale)
                        act.activation(parts[s][:, 0, :], pQK[s][:, :], ACT.Identity, bias=c[bias][:, 0:1],
                                       scale=scale).then_inc(full_ready, 1)
                    for s in range(2):
                        act.wait_ge(rest_ready, b * 2 + (s + 1))
                        act.copy(parts[s][:, 1, :], rest[s][:, :]).then_inc(second_ready, 1)
                    if more:
                        root(b + 1, 1)

                root(0, 0)
                root(0, 1)
                batch(0)
                with act.Fori(1, BATCH - 1) as b:
                    batch(b)
                batch(BATCH - 1, more=False)

            @block.tensor
            def _(pe):
                def batch(b):
                    pe.wait_ge(xn_ready, b + 1)
                    reached(pe, xT_ready, b)
                    for t in range(BT):
                        last = pe.transpose(pT[:, t * P:(t + 1) * P], xn[:, t * D:(t + 1) * D], c["ident"][:, :])
                    last.then_inc(xnT_ready, 1)
                    pe.wait_ge(xT_ready, b + 1)
                    reached(pe, full_ready, b * 2)
                    for s, name in ((0, "L0_ffn_q_w"), (1, "L0_ffn_k_w")):
                        for half in range(2):
                            last = pe.matmul(pQK[s][:, half * 512:(half + 1) * 512], c[name][:, :],
                                             xT[:, half * 512:(half + 1) * 512], start=True, stop=True)
                        last.then_inc(qk_ready, 1)
                    reached(pe, v_kept, b)
                    for t in range(BT):
                        last = pe.matmul(pV[:, t * D:(t + 1) * D], xT[:, t * P:(t + 1) * P], c["L0_ffn_v_w"][:, :],
                                         start=True, stop=True)
                    last.then_inc(v_ready, 1)

                batches(pe, batch)


class Step:

    def __init__(self, u, stage, fills):
        self.u, self.stage, self.fills = u, stage, fills

    def shift(self, d):
        at = self.stage + d
        return Step(self.u + d, at % 3, self.fills + at // 3)


def attention_steps(eng, step, last_b, first_a):
    first_a(Step(0, 0, 0))
    step(Step(1, 1, 0))
    with eng.Fori(0, (UNITS - 4) // 3) as turn:
        for n in range(3):
            step(Step(turn * 3 + (n + 2), (n + 2) % 3, turn + (n + 2) // 3))
    for u in (UNITS - 2, UNITS - 1):
        step(Step(u, u % 3, u // 3))
    last_b(Step(UNITS, UNITS % 3, UNITS // 3))


def ffn_attention(core, keep, w, c, buffers, tag):
    nc = core.nc
    HALF = SEQ // 2
    HT = BT // 2
    PIECE = [(h, i, a, min(a + HALF, (i + 1) * P)) for tiles in (range(HT, BT), range(HT))
             for i in tiles for h in range(GH) for a in range(0, (i + 1) * P, HALF)]
    LATE = sum(i >= HT for h, i, a, b in PIECE)
    GROUP = [(j, max(j * P, HALF), SEQ) for j in (0, 7, 1, 6, 2, 5, 3, 4)]
    GROUP += [(j, j * P, HALF) for j in (0, 3, 1, 2)]
    LATE_G = BT
    DIAG = [j * P == a for j, a, e in GROUP]
    NDIAG = GH * sum(DIAG)
    NG, NCH = len(GROUP), GH * len(GROUP)
    MAX_LO, MAX_HI, CTX_HI, CTX_LO = "max_lo", "max_hi", "ctx_hi", "ctx_lo"

    def events(first, contexts):
        order = list(range(len(PIECE)))
        order.insert(LATE + 6, MAX_HI)
        if contexts:
            order[12:12] = [CTX_HI, CTX_LO]
        if not first:
            order.insert(7, MAX_LO)
        return order

    ORDER = (events(True, False), events(False, False), events(False, True))
    FINAL = [MAX_LO, CTX_HI, CTX_LO]
    NEV = len(ORDER[2])
    LINKS_LO, LINKS_HI, LINKS_CTX = 3, 4, 2
    NA, NB = 3, 3
    NLINK = LINKS_LO + LINKS_HI + LINKS_CTX
    with ExitStack() as ctx:
        sb = lambda n, s, dt=F32: core.sb(ctx, n + tag, s, dt)
        ps = lambda n, s, dt=F32: core.ps(ctx, n + tag, s, dt)
        sem = lambda n: core.sem(ctx, n + tag)
        qa, ka, va, qk_loaded = (buffers[n] for n in ("qa", "ka", "va", "qk_loaded"))
        mx = [sb(f"mx{i}", [P, BT, GH]) for i in range(2)]
        top, rest = sb("top", [P, BT, GH]), sb("rest", [P, BT, GH])
        mparts = sb("mparts", [P, BT, GH, 3], BF16)
        mT = sb("mT", [3 * GH, SEQ], BF16)
        wt = [[sb(f"wt{i}{h}", [P, HALF]) for h in range(GH)] for i in range(2)]
        cT = sb("cT", [P, SEQ])
        rden = sb("rden", [P, BT, GH])
        pA = [ps(f"pA{i}", [P, HALF]) for i in range(NA)]
        pB = [ps(f"pB{i}", [P, HALF]) for i in range(NB)]
        pC = ps("pC", [P, SEQ])
        v_staged = [sem(f"v_staged{i}") for i in range(3)]
        hi_loaded = [sem(f"max_hi_loaded{i}") for i in range(3)]
        lo_loaded = [sem(f"max_lo_loaded{i}") for i in range(3)]
        a_done, a_used, mparts_ready = sem("a_done"), sem("a_used"), sem("mparts_ready")
        st_done, exp_done, masked, pv_done, cT_ready = (sem("st_done"), sem("exp_done"), sem("masked"),
                                                        sem("pv_done"), sem("cT_ready"))
        dve = sem("dve_a")

        def fixed(s, upto):
            return isinstance(s.u, int) and s.u <= upto

        def order(s):
            if fixed(s, UNITS) and s.u == UNITS:
                return FINAL + [CTX_HI, CTX_LO]
            return ORDER[s.u] if fixed(s, 1) else ORDER[2]

        def before(s):
            if fixed(s, 1):
                return s.u * len(ORDER[0])
            return s.u * NEV + (len(ORDER[0]) + len(ORDER[1]) - 2 * NEV)

        def event(s, n):
            return before(s) + n

        def slot(s, n):
            u = s.u if isinstance(s.u, int) else s.stage + 3
            return pA[(before(Step(u, 0, 0)) + n) % NA]

        def links(s):
            if fixed(s, 1):
                return s.u * LINKS_HI
            return s.u * NLINK + (2 * LINKS_HI + LINKS_LO - 2 * NLINK)

        with nc.Block() as block:
            @block.sync
            def _(sp):
                def max_rows(s, n, stage, loaded, a):
                    sp.wait_ge(a_used, event(s, n) + 1)
                    for h in range(GH):
                        sp.dma_start(qa[stage][MROW:P, h, a:a + HALF],
                                     mT[3 * h:3 * h + 3, a:a + HALF]).then_inc(loaded[stage], 16)

                def rows(s):
                    for n, e in enumerate(order(s)):
                        if e == MAX_LO:
                            max_rows(s, n, s.shift(-1).stage, lo_loaded, 0)
                        if e == MAX_HI:
                            max_rows(s, n, s.stage, hi_loaded, HALF)

                def step(s):
                    rows(s)
                    if not isinstance(s.u, int) or s.u + 2 < UNITS:
                        sp.wait_ge(pv_done, s.u * NCH)
                        load_qk(sp, w, buffers, s.shift(2).stage, s.u + 2)

                attention_steps(sp, step, rows, rows)

            @block.tensor
            def _(pe):
                def piece(s, n, e):
                    h, i, a, b = PIECE[e]
                    if e == 0:
                        pe.wait_ge(qk_loaded[s.stage], s.fills * 32 * TERMS + 32 * TERMS)
                    reached(pe, a_used, event(s, n) - (NA - 1))
                    pe.matmul(slot(s, n)[:, 0:b - a], qa[s.stage][0:MROW, h, i * P:(i + 1) * P],
                              ka[s.stage][0:MROW, h, a:b], start=True, stop=True).then_inc(a_done, 1)

                def maxima(s, n, half, count):
                    pe.wait_ge(mparts_ready, count)
                    reached(pe, a_used, event(s, n) - (NA - 1))
                    rows = slot(s, n)[0:3 * GH, 0:HALF // 2].bitcast(BF16)
                    for i in range(HT):
                        last = pe.transpose(rows[:, i * P:(i + 1) * P],
                                            mparts[:, half * HT + i, :, :].rearrange("p h s -> p (h s)"),
                                            c["ident_b"][:, :])
                    last.then_inc(a_done, 1)

                def context(s, n, half, back):
                    pe.wait_ge(cT_ready, s.u * 2 - (2 * back - 2 + half))
                    reached(pe, a_used, event(s, n) - (NA - 1))
                    for i in range(HT):
                        at = (half * HT + i) * P
                        last = pe.transpose(slot(s, n)[:, i * P:(i + 1) * P], cT[:, at:at + P], c["ident"][:, :])
                    last.then_inc(a_done, 1)

                def run(s, n, back=2):
                    e = order(s)[n]
                    if e == MAX_LO:
                        maxima(s, n, 0, s.u * 2)
                    elif e == MAX_HI:
                        maxima(s, n, 1, s.u * 2 + 1)
                    elif e in (CTX_HI, CTX_LO):
                        context(s, n, int(e == CTX_HI), back)
                    else:
                        piece(s, n, e)

                def scores(s, g, h):
                    j, a, e = GROUP[g]
                    v = s.shift(-1)
                    if h == 0 and g in (0, LATE_G):
                        pe.wait_ge((lo_loaded if g else hi_loaded)[v.stage], v.fills * 16 * GH + 16 * GH)
                    reached(pe, exp_done, v.u * NCH + (g * GH + h - (NB - 1)))
                    pe.matmul(pB[(g * GH + h) % NB][:, 0:e - a], ka[v.stage][0:P, h, j * P:(j + 1) * P],
                              qa[v.stage][0:P, h, a:e], start=True, stop=True).then_inc(st_done, 1)

                def products(s, g):
                    j, a, e = GROUP[g]
                    v = s.shift(-1)
                    if g == 0:
                        pe.wait_ge(v_staged[v.stage], v.fills + 1)
                    if g in (0, LATE_G):
                        reached(pe, cT_ready, v.u * 2 - (0 if g else 1))
                    for h in range(GH):
                        if DIAG[g]:
                            pe.wait_ge(masked, v.u * NDIAG + (GH * sum(DIAG[:g]) + h + 1))
                        else:
                            pe.wait_ge(exp_done, v.u * NCH + (g * GH + h + 1))
                        pe.matmul(pC[32 * h:32 * h + 32, a:e], va[v.stage][:, j, h, :], wt[g % 2][h][:, 0:e - a],
                                  start=g in (0, LATE_G), stop=g in (LATE_G - 1, NG - 1)).then_inc(pv_done, 1)

                def first(s):
                    for n in range(len(order(s))):
                        run(s, n)

                def step(s, count=None):
                    count = count or len(order(s))
                    total = GH * sum(e - a for j, a, e in GROUP)
                    done = n = 0
                    for g, (j, a, e) in enumerate(GROUP):
                        for h in range(GH):
                            scores(s, g, h)
                            done += e - a
                            while n < min(count, count * done // total + 1):
                                run(s, n)
                                n += 1
                        if g:
                            products(s, g - 1)
                    products(s, NG - 1)

                def last_b(s):
                    step(s, len(FINAL))
                    for n in range(len(FINAL), len(order(s))):
                        run(s, n, 1)

                attention_steps(pe, step, last_b, first)

            @block.vector
            def _(vec):
                def split(s, half, k, n):
                    t = slice(half * HT, (half + 1) * HT)
                    src = top if half else mx[0]
                    if half == 0:
                        k += 1
                    first = k == (0 if half else 1)
                    if not first:
                        vec.wait_ge(dve, links(s) + n)
                    parts = [mparts[:, t, :, r] for r in range(3)]
                    if k == 0:
                        ins = vec.tensor_tensor(top[:, t, :], mx[0][:, t, :], mx[1][:, t, :], ALU.max)
                    elif k == 1:
                        ins = vec.tensor_copy(parts[0], src[:, t, :])
                    elif k == 2:
                        ins = vec.tensor_tensor(rest[:, t, :], src[:, t, :], parts[0], ALU.subtract)
                    elif k == 3:
                        ins = vec.tensor_copy(parts[1], rest[:, t, :])
                    else:
                        ins = vec.tensor_tensor(parts[2], rest[:, t, :], parts[1], ALU.subtract)
                    ins.then_inc(mparts_ready if k == 4 else dve, 1)

                def copy_maxima(s, n, half, unit, loaded):
                    vec.wait_ge(a_done, event(s, n) + 1)
                    if unit.fills is not None:
                        vec.wait_ge(loaded[unit.stage], unit.fills * 16 * GH + 16 * GH)
                    vec.tensor_copy(mT[:, half * HALF:(half + 1) * HALF],
                                    slot(s, n)[0:3 * GH, 0:HALF // 2].bitcast(BF16)).then_inc(a_used, 1)

                def context(s, n, half, link, back=2):
                    vec.wait_ge(a_done, event(s, n) + 1)
                    rows = slot(s, n)[:, :].rearrange("p (t h r) -> p t h r", t=HT, h=GH)
                    den = rden[:, half * HT:(half + 1) * HT, :]
                    vec.reciprocal(den, rows[:, :, :, HD]).then_inc(dve, 1)
                    vec.wait_ge(dve, links(s) + link)
                    size = HT * GH * HD
                    vec.tensor_tensor(keep["ctx"][:, bass.ds((s.u - back) * (2 * size) + half * size, size)]
                                      .rearrange("p (t h r) -> p t h r", t=HT, h=GH),
                                      rows[:, :, :, 0:HD], den.unsqueeze(3).to_broadcast([P, HT, GH, HD]),
                                      ALU.mult).then_inc(a_used, 1)

                def step(s):
                    n_lo = 0 if fixed(s, 0) else LINKS_LO
                    n_ctx = 0 if fixed(s, 1) else LINKS_CTX
                    for n, e in enumerate(order(s)):
                        if e == MAX_LO:
                            copy_maxima(s, n, 0, before_unit(s, 2), lo_loaded)
                        elif e == MAX_HI:
                            copy_maxima(s, n, 1, before_unit(s, 1), hi_loaded)
                        elif e == CTX_HI:
                            context(s, n, 1, n_lo + 1)
                        elif e == CTX_LO:
                            context(s, n, 0, n_lo + 2)
                        else:
                            h, i, a, b = PIECE[e]
                            size = b - a
                            mask = c["causal"][:, SEQ - size:] if b == (i + 1) * P else c["causal"][:, 0:size]
                            apart(vec, a_done, event(s, n) + 1)
                            vec.tensor_tensor_reduce(out=slot(s, n)[:, 0:size], in0=slot(s, n)[:, 0:size], in1=mask,
                                                     scale=1.0, scalar=LOWEST, op0=ALU.add, op1=ALU.max,
                                                     accum_out=mx[a // HALF][:, i, h:h + 1]).then_inc(a_used, 1)
                            if 0 <= e <= 3 and n_lo:
                                if e == 0:
                                    vec.wait_ge(a_used, before(s))
                                split(s, 0, e, e)
                            if LATE <= e <= LATE + 4:
                                if e == LATE:
                                    vec.wait_ge(a_used, event(s, n))
                                split(s, 1, e - LATE, n_lo + n_ctx + e - LATE)

                def before_unit(s, back):
                    if isinstance(s.u, int) and s.u < back:
                        return Step(0, 0, None)
                    return s.shift(-back)

                def last(s):
                    vec.wait_ge(a_used, before(s))
                    for k in range(4):
                        split(s, 0, k, k)
                    copy_maxima(s, 0, 0, s.shift(-2), lo_loaded)
                    context(s, 1, 1, LINKS_LO + 1)
                    context(s, 2, 0, LINKS_LO + 2)
                    vec.wait_ge(a_used, event(s, 3))
                    context(s, 3, 1, LINKS_LO + 3, 1)
                    context(s, 4, 0, LINKS_LO + 4, 1)

                attention_steps(vec, step, last, step)

            @block.scalar
            def _(act):
                def copy_context(half):
                    at = half * HALF
                    act.copy(cT[:, at:at + HALF], pC[:, at:at + HALF]).then_inc(cT_ready, 1)

                def weights(s):
                    v = s.shift(-1)
                    for g, (j, a, e) in enumerate(GROUP):
                        for h in range(GH):
                            act.wait_ge(st_done, v.u * NCH + (g * GH + h + 1))
                            reached(act, pv_done, v.u * NCH + ((g - 2) * GH + h + 1))
                            act.activation(wt[g % 2][h][:, 0:e - a], pB[(g * GH + h) % NB][:, 0:e - a], ACT.Exp).then_inc(exp_done, 1)
                        if g == 1 and not fixed(s, 1):
                            act.wait_ge(pv_done, v.u * NCH)
                            if not fixed(s, 2):
                                act.wait_ge(a_done, before(s) - (NEV - ORDER[2].index(CTX_LO) - 1))
                            copy_context(0)
                        if g == LATE_G + 1:
                            act.wait_ge(pv_done, v.u * NCH + LATE_G * GH)
                            if not fixed(s, 1):
                                act.wait_ge(a_done, event(s, order(s).index(CTX_HI)) + 1)
                            copy_context(1)

                def last_weights(s):
                    weights(s)
                    act.wait_ge(pv_done, s.u * NCH)
                    act.wait_ge(a_done, event(s, len(FINAL)))
                    copy_context(0)

                attention_steps(act, weights, last_weights, lambda s: None)

            @block.gpsimd
            def _(pool):
                size = BT * GH * HD

                def stage(s):
                    pool.tensor_copy(va[s.stage][:, :, :, 0:HD],
                                     keep["v"][:, bass.ds(s.u * size, size)]
                                     .rearrange("p (t h r) -> p t h r", t=BT, h=GH)).then_inc(v_staged[s.stage], 1)

                def first(s):
                    for d in range(3):
                        stage(s.shift(d))

                def mask(s):
                    v = s.shift(-1)
                    for g in range(NG):
                        for h in range(GH if DIAG[g] else 0):
                            apart(pool, exp_done, v.u * NCH + (g * GH + h + 1))
                            block_ = wt[g % 2][h][:, 0:P]
                            pool.affine_select(out=block_, in_=block_, compare_op=ALU.is_ge, fill=0.0, base=0,
                                               pattern=[[1, P]], channel_multiplier=-1).then_inc(masked, 1)

                def step(s):
                    mask(s)
                    if not isinstance(s.u, int) or s.u + 2 < UNITS:
                        apart(pool, pv_done, s.u * NCH)
                        stage(s.shift(2))

                attention_steps(pool, step, mask, first)


def ffn_output(core, keep, w, c, tag):
    nc = core.nc
    with ExitStack() as ctx:
        sb = lambda n, s, dt=F32: core.sb(ctx, n + tag, s, dt)
        ps = lambda n, s, dt=F32: core.ps(ctx, n + tag, s, dt)
        sem = lambda n: core.sem(ctx, n + tag)
        rows, cT = sb("ctx_rows", [P, BCOL]), sb("ctxT", [P, SEQ])
        stats, mv = sb("stats_o", [P, BT, 6]), sb("mv_o", [P, BT, 2])
        std, rstd = sb("std_o", [P, BT]), sb("rstd_o", [P, BT])
        xn, xnT = sb("xn_o", [P, BCOL]), sb("xnT_o", [P, SEQ])
        pT, pO, pX, pL = ps("pT_o", [P, SEQ]), ps("pO", [P, BCOL]), ps("pX_o", [P, SEQ]), ps("pL", [P, BT * E])
        rows_ready, T_done, T_ready, o_done = sem("rows_ready"), sem("T_done"), sem("T_ready"), sem("o_done")
        var_ready, std_ready, xn_ready, logits_done = sem("var_o"), sem("std_rdy_o"), sem("xn_ready_o"), sem("logits_done")
        xn_kept, dve = sem("xn_kept"), sem("dve_o")
        with nc.Block() as block:
            @block.gpsimd
            def _(pool):
                with pool.Fori(0, BATCH) as b:
                    pool.tensor_copy(rows[:, :].rearrange("p (t g r) -> p g t r", t=BT, g=GROUPS),
                                     keep["ctx"][:, bass.ds(b * BCOL, BCOL)]
                                     .rearrange("p (g t r) -> p g t r", g=GROUPS, t=BT)).then_inc(rows_ready, 1)
                    apart(pool, xn_ready, b + 1)
                    pool.tensor_copy(keep["xt"][:, bass.ds(b * BCOL, BCOL)], xn[:, :]).then_inc(xn_kept, 1)
                    apart(pool, xn_kept, b + 1)

            @block.tensor
            def _(pe):
                with pe.Fori(0, BATCH) as b:
                    pe.wait_ge(rows_ready, b + 1)
                    for t in range(BT):
                        last = pe.transpose(pT[:, t * P:(t + 1) * P], rows[:, t * D:(t + 1) * D], c["ident"][:, :])
                    last.then_inc(T_done, 1)
                    pe.wait_ge(T_ready, b * 2 + 1)
                    for t in range(BT):
                        last = pe.matmul(pO[:, t * D:(t + 1) * D], cT[:, t * P:(t + 1) * P], c["L0_ffn_o_w"][:, :],
                                         start=True, stop=True)
                    last.then_inc(o_done, 1)
                    pe.wait_ge(xn_ready, b + 1)
                    for t in range(BT):
                        last = pe.transpose(pX[:, t * P:(t + 1) * P], xn[:, t * D:(t + 1) * D], c["ident"][:, :])
                    last.then_inc(T_done, 1)
                    pe.wait_ge(T_ready, b * 2 + 2)
                    for t in range(BT):
                        last = pe.matmul(pL[:, t * E:(t + 1) * E], xnT[:, t * P:(t + 1) * P], c["router"][:, :],
                                         start=True, stop=True)
                    last.then_inc(logits_done, 1)

            @block.scalar
            def _(act):
                with act.Fori(0, BATCH) as b:
                    act.wait_ge(T_done, b * 2 + 1)
                    act.copy(cT[:, :], pT[:, :]).then_inc(T_ready, 1)
                    act.wait_ge(var_ready, b + 1)
                    act.activation(std[:, :], mv[:, :, 1], ACT.Sqrt, bias=c["eps"][:, 0:1]).then_inc(std_ready, 1)
                    act.wait_ge(T_done, b * 2 + 2)
                    act.copy(xnT[:, :], pX[:, :]).then_inc(T_ready, 1)

            @block.vector
            def _(vec):
                chain = Chain(vec, dve)
                link = chain.link
                for b in chain.each(BATCH, 8):
                    hidden = keep["hid"][:, bass.ds(b * BCOL, BCOL)]
                    vec.wait_ge(o_done, b + 1)
                    link(vec.tensor_tensor(hidden, hidden, pO[:, :], ALU.add))
                    per_column(vec, link, hidden, hidden, c["L0_ffn_o_b"], ALU.add)
                    for t in range(BT):
                        last = vec.bn_stats(stats[:, t, :], hidden[:, t * D:(t + 1) * D])
                    link(last)
                    for t in range(BT):
                        last = vec.bn_aggr(mv[:, t, :], stats[:, t, :])
                    last.then_inc(var_ready, 1)
                    vec.wait_ge(std_ready, b + 1)
                    link(vec.reciprocal(rstd[:, :], std[:, :]))
                    normalise(vec, link, xn[:, :], hidden, mv, rstd)
                    per_column(vec, link, xn[:, :], xn[:, :], c["L0_ffn_ln2_w"], ALU.mult)
                    per_column(vec, link, xn[:, :], xn[:, :], c["L0_ffn_ln2_b"], ALU.add)
                    vec.sem_inc(xn_ready, 1)
                    vec.wait_ge(logits_done, b + 1)
                    link(vec.tensor_copy(keep["logits"][:, bass.ds(b * BT * E, BT * E)], pL[:, :]))
                    vec.wait_ge(xn_kept, b + 1)


def ffn_route(core, keep, c, tag):
    nc = core.nc
    with ExitStack() as ctx:
        sb = lambda n, s, dt=F32: core.sb(ctx, n + tag, s, dt)
        sem = lambda n: core.sem(ctx, n + tag)
        G = [P, TILES, E]
        prob, logit2, work, one = sb("prob", G), sb("logit2", G), sb("work_r", G), [sb("top1", G), sb("top2", G)]
        kept, loc = [sb("kept1", G), sb("kept2", G)], [sb("loc1", G), sb("loc2", G)]
        tot, run = [sb("tot1", [P, E, TILES]), sb("tot2", [P, E, TILES])], [sb("run1", [P, E, TILES]), sb("run2", [P, E, TILES])]
        best, first, total, recip = (sb(n, [P, TILES]) for n in ("best", "first", "total", "recip"))
        gate, at, dropped = (sb("gate", [P, 2, TILES]), sb("at", [P, 2, TILES]), sb("dropped", [P, TILES]))
        place = sb("place", [P, 2, TILES])
        pCum = [core.ps(ctx, f"pCum{i}{tag}", [P, TILES * E]) for i in range(2)]
        pTot = [core.ps(ctx, f"pTot{i}{tag}", [P, TILES * E]) for i in range(2)]
        max_found, exps_ready, one_ready, counted, dve = (sem("max_found"), sem("exps_ready"), sem("one_ready"),
                                                          sem("counted"), sem("dve_r"))
        over_e = lambda v: v.unsqueeze(2).to_broadcast(G)
        over_t = lambda v: v.unsqueeze(1).to_broadcast(G)
        L = keep["logits"][:, :].rearrange("p (t e) -> p t e", e=E)
        with nc.Block() as block:
            @block.vector
            def _(vec):
                link = Chain(vec, dve).link

                def top(values, n):
                    link(vec.reduce_max(best[:, :], values, AX))
                    link(vec.tensor_tensor(work[:, :, :], values, over_e(best[:, :]), ALU.is_equal))
                    link(vec.tensor_tensor(work[:, :, :], work[:, :, :], over_t(c["rev"][:, :]), ALU.mult))
                    link(vec.reduce_max(first[:, :], work[:, :, :], AX))
                    vec.tensor_tensor(one[n][:, :, :], over_t(c["rev"][:, :]), over_e(first[:, :]),
                                      ALU.is_equal).then_inc(one_ready, 1)
                    vec.wait_ge(one_ready, n + 1)

                link(vec.reduce_max(best[:, :], L, AX))
                vec.tensor_tensor(work[:, :, :], L, over_e(best[:, :]), ALU.subtract).then_inc(max_found, 1)
                vec.wait_ge(exps_ready, 1)
                link(vec.reduce_sum(total[:, :], prob[:, :, :], AX))
                link(vec.reciprocal(recip[:, :], total[:, :]))
                link(vec.tensor_tensor(prob[:, :, :], prob[:, :, :], over_e(recip[:, :]), ALU.mult))
                top(prob[:, :, :], 0)
                link(vec.scalar_tensor_tensor(logit2[:, :, :], one[0][:, :, :], LOWEST, L, ALU.mult, ALU.add))
                top(logit2[:, :, :], 1)
                for n in range(2):
                    vec.wait_ge(counted, n + 1)
                    link(vec.tensor_copy(tot[n][:, :, :], pTot[n][:, :].rearrange("p (t e) -> p e t", e=E)))
                    link(vec.tensor_tensor_scan(run[n][:, :, :].rearrange("p e t -> p (e t)"),
                                                c["restart"][:, :, :].rearrange("p e t -> p (e t)"),
                                                tot[n][:, :, :].rearrange("p e t -> p (e t)"), 0.0, ALU.mult, ALU.add))
                    link(vec.tensor_tensor(tot[n][:, :, :], run[n][:, :, :], tot[n][:, :, :], ALU.subtract))
                    link(vec.scalar_tensor_tensor(loc[n][:, :, :], pCum[n][:, :].rearrange("p (t e) -> p t e", e=E), -1.0,
                                                  tot[n][:, :, :].rearrange("p e t -> p t e"), ALU.add, ALU.add))
                    if n == 1:
                        link(vec.tensor_tensor(loc[1][:, :, :], loc[1][:, :, :], over_t(run[0][:, :, TILES - 1]), ALU.add))
                    link(vec.scalar_tensor_tensor(kept[n][:, :, :], loc[n][:, :, :], float(CAP), one[n][:, :, :],
                                                  ALU.is_lt, ALU.mult))
                    link(vec.tensor_tensor(work[:, :, :], prob[:, :, :], kept[n][:, :, :], ALU.mult))
                    link(vec.reduce_sum(gate[:, n, :], work[:, :, :], AX))
                    link(vec.scalar_tensor_tensor(loc[n][:, :, :], over_t(c["num"][:, :]), float(CAP), loc[n][:, :, :],
                                                  ALU.mult, ALU.add))
                    link(vec.tensor_tensor(work[:, :, :], loc[n][:, :, :], kept[n][:, :, :], ALU.mult))
                    link(vec.reduce_sum(at[:, n, :], work[:, :, :], AX))
                    link(vec.tensor_copy(keep["take"][:, n, :], at[:, n, :]))
                    link(vec.reduce_sum(dropped[:, :], kept[n][:, :, :], AX))
                    link(vec.tensor_scalar(dropped[:, :], dropped[:, :], -1.0, 1.0, ALU.mult, ALU.add))
                    link(vec.scalar_tensor_tensor(place[:, n, :], c["spill"][:, :], float(n * TOK), dropped[:, :],
                                                  ALU.add, ALU.mult))
                    link(vec.tensor_tensor(place[:, n, :], place[:, n, :], at[:, n, :], ALU.add))
                    link(vec.tensor_copy(keep["send"][:, n, :], place[:, n, :]))
                link(vec.tensor_tensor(total[:, :], gate[:, 0, :], gate[:, 1, :], ALU.add))
                link(vec.tensor_scalar(total[:, :], total[:, :], F32_EPS, None, ALU.max))
                link(vec.reciprocal(recip[:, :], total[:, :]))
                vec.tensor_tensor(keep["gate"][:, :, :], gate[:, :, :],
                                  recip[:, :].unsqueeze(1).to_broadcast([P, 2, TILES]), ALU.mult)

            @block.scalar
            def _(act):
                act.wait_ge(max_found, 1)
                act.activation(prob[:, :, :], work[:, :, :], ACT.Exp).then_inc(exps_ready, 1)

            @block.tensor
            def _(pe):
                for n in range(2):
                    pe.wait_ge(one_ready, n + 1)
                    flat = one[n][:, :, :].rearrange("p t e -> p (t e)")
                    pe.matmul(pCum[n][:, :], c["upper"][:, :], flat, start=True, stop=True)
                    pe.matmul(pTot[n][:, :], c["ones"][:, :], flat, start=True, stop=True).then_inc(counted, 1)


def ffn_experts(core, keep, w, c, x_out, tag):
    nc = core.nc
    with ExitStack() as ctx:
        sb = lambda n, s, dt=F32: core.sb(ctx, n + tag, s, dt)
        ps = lambda n, s, dt=F32: core.ps(ctx, n + tag, s, dt)
        sem = lambda n: core.sem(ctx, n + tag)
        two = range(2)
        xi = [sb(f"xi{i}", [P, CC, D]) for i in two]
        w1 = [sb(f"w1_{i}", [P, F]) for i in two]
        w2 = [sb(f"w2_{i}", [P, FC, D]) for i in two]
        b1 = [sb(f"b1_{i}", [P, FC]) for i in two]
        b2 = [sb(f"b2_{i}", [P, D]) for i in two]
        b2s = [sb(f"b2s_{i}", [P, D]) for i in two]
        xiT = sb("xiT", [P, CAP])
        hT = [sb(f"hT{i}", [P, CAP]) for i in range(FC)]
        eo = [sb(f"eo{i}", [P, CC, D]) for i in two]
        pX = ps("pXi", [P, CAP])
        pH = [ps(f"pH{i}", [P, CAP]) for i in range(FC)]
        pO = [ps(f"pOe{i}", [P, CC, D]) for i in two]
        sent = sem("sent")
        x_loaded = [sem(f"xi_loaded{i}") for i in two]
        w_loaded = [sem(f"we_loaded{i}") for i in two]
        xT_done, xT_ready, h_done, h_ready, o_done, o_ready, b_ready = (
            sem(n) for n in ("xiT_done", "xiT_ready", "h_done", "h_ready", "oe_done", "oe_ready", "b2s_ready"))
        stored = [sem(f"eo_stored{i}") for i in two]
        xin = w["xin"][0:SLOTS, :].rearrange("(e p c) d -> e p c d", p=P, c=CC)
        eout = w["eout"].rearrange("(e p c) d -> e p c d", p=P, c=CC)
        with nc.Block() as block:
            @block.gpsimd
            def _(pool):
                for t in range(TILES):
                    for n in two:
                        pool.indirect_dma_start(
                            out=w["xin"], out_offset=bass.IndirectOffsetOnAxis(ap=keep["send"][:, n, t:t + 1], axis=0),
                            in_=keep["xt"][:, t * D:(t + 1) * D], in_offset=None).then_inc(sent, 16)

            def experts(eng, one_expert):
                for n in two:
                    one_expert(n, n, 0)
                with eng.Fori(1, E // 2) as turn:
                    for n in two:
                        one_expert(turn * 2 + n, n, turn)

            @block.sync
            def _(sp):
                def load(e, n, turn):
                    if not isinstance(e, int):
                        sp.wait_ge(o_ready, e - 1)
                        sp.wait_ge(o_done, e - 1)
                    for dst, src in ((w1[n][:, :], w["L0_ffn_fc1_w"][bass.ds(e, 1)].rearrange("o d f -> (o d) f")),
                                     (w2[n][:, :, :], w["L0_ffn_fc2_w"][bass.ds(e, 1)]
                                      .rearrange("o (p c) d -> (o p) c d", c=FC)),
                                     (b1[n][:, :], w["L0_ffn_fc1_b"][bass.ds(e, 1)]
                                      .rearrange("o (p c) -> (o p) c", c=FC)),
                                     (b2[n][:, :], w["L0_ffn_fc2_b"][bass.ds(e, 1)]
                                      .rearrange("o d -> (o d)").partition_broadcast(P))):
                        sp.dma_start(dst, src).then_inc(w_loaded[n], 16)
                    if isinstance(e, int):
                        sp.wait_ge(sent, 16 * 2 * TILES)
                    sp.dma_start(xi[n][:, :, :], xin[bass.ds(e, 1)].rearrange("o p c d -> (o p) c d")
                                 ).then_inc(x_loaded[n], 16)

                experts(sp, load)

            @block.tensor
            def _(pe):
                def run(e, n, turn):
                    pe.wait_ge(x_loaded[n], turn * 16 + 16)
                    for cc in range(CC):
                        last = pe.transpose(pX[:, cc * P:(cc + 1) * P], xi[n][:, cc, :], c["ident"][:, :])
                    last.then_inc(xT_done, 1)
                    pe.wait_ge(w_loaded[n], turn * 64 + 64)
                    pe.wait_ge(xT_ready, e + 1)
                    cols = w1[n][:, :].rearrange("d (p c) -> d c p", c=FC)
                    for f in range(FC):
                        pe.matmul(pH[f][:, :], cols[:, f, :], xiT[:, :], start=True, stop=True).then_inc(h_done, 1)
                    pe.wait_ge(h_ready, e * FC + FC)
                    if not isinstance(e, int):
                        pe.wait_ge(o_ready, e - 1)
                    for cc in range(CC):
                        for f in range(FC):
                            last = pe.matmul(pO[n][:, cc, :], hT[f][:, cc * P:(cc + 1) * P], w2[n][:, f, :],
                                             start=f == 0, stop=f == FC - 1)
                    last.then_inc(o_done, 1)

                experts(pe, run)

            @block.scalar
            def _(act):
                def gelu(e, n, turn):
                    act.wait_ge(w_loaded[n], turn * 64 + 64)
                    for f in range(FC):
                        act.wait_ge(h_done, e * FC + (f + 1))
                        if f == 0:
                            reached(act, o_done, e)
                        act.activation(hT[f][:, :], pH[f][:, :], ACT.Gelu, bias=b1[n][:, f:f + 1]).then_inc(h_ready, 1)
                    act.wait_ge(o_ready, e + 1)
                    act.dma_start(eout[bass.ds(e, 1)].rearrange("o p c d -> (o p) c d"),
                                  eo[n][:, :, :]).then_inc(stored[n], 16)

                experts(act, gelu)
                for n in two:
                    act.wait_ge(stored[n], 16 * (E // 2))

            @block.vector
            def _(vec):
                def finish(e, n, turn):
                    vec.wait_ge(xT_done, e + 1)
                    vec.tensor_copy(xiT[:, :], pX[:, :]).then_inc(xT_ready, 1)
                    vec.wait_ge(w_loaded[n], turn * 64 + 64)
                    vec.tensor_scalar(b2s[n][:, :], b2[n][:, :], 0.8, None, ALU.mult).then_inc(b_ready, 1)
                    vec.wait_ge(b_ready, e + 1)
                    vec.wait_ge(o_done, e + 1)
                    if not isinstance(e, int):
                        vec.wait_ge(stored[n], turn * 16)
                    vec.scalar_tensor_tensor(eo[n][:, :, :], pO[n][:, :, :], 0.8,
                                             b2s[n][:, :].unsqueeze(1).to_broadcast([P, CC, D]),
                                             ALU.mult, ALU.add).then_inc(o_ready, 1)

                experts(vec, finish)

    with ExitStack() as ctx:
        sb = lambda n, s, dt=F32: core.sb(ctx, n + tag, s, dt)
        sem = lambda n: core.sem(ctx, n + tag)
        got = [keep["ctx"], keep["xt"]]
        gathered = [sem(f"gathered{b}") for b in range(BATCH)]
        dve, x_ready, x_stored = sem("dve_c"), sem("x_ready"), sem("x_stored")
        x_rows = x_out.rearrange("(b t p) d -> b p t d", p=P, t=BT)
        T3 = [P, BT, D]
        with nc.Block() as block:
            @block.gpsimd
            def _(pool):
                for b in range(BATCH):
                    for t in range(b * BT, (b + 1) * BT):
                        for n in range(2):
                            pool.indirect_dma_start(
                                out=got[n][:, t * D:(t + 1) * D], out_offset=None, in_=w["eout"],
                                in_offset=bass.IndirectOffsetOnAxis(ap=keep["take"][:, n, t:t + 1], axis=0)
                            ).then_inc(gathered[b], 16)

            @block.vector
            def _(vec):
                link = Chain(vec, dve).link
                for b in range(BATCH):
                    vec.wait_ge(gathered[b], 16 * 2 * BT)
                    cols = slice(b * BCOL, (b + 1) * BCOL)
                    part = [got[n][:, cols].rearrange("p (t d) -> p t d", d=D) for n in range(2)]
                    for n in range(2):
                        gate = keep["gate"][:, n, b * BT:(b + 1) * BT].unsqueeze(2).to_broadcast(T3)
                        link(vec.tensor_tensor(part[n], part[n], gate, ALU.mult))
                    link(vec.tensor_tensor(got[0][:, cols], got[0][:, cols], got[1][:, cols], ALU.add))
                    link(vec.tensor_tensor(got[0][:, cols], got[0][:, cols], keep["hid"][:, cols], ALU.add))
                    vec.scalar_tensor_tensor(got[0][:, cols], got[0][:, cols], 0.5, keep["x"][:, cols],
                                             ALU.mult, ALU.add).then_inc(x_ready, 1)

            @block.sync
            def _(sp):
                for b in range(BATCH):
                    sp.wait_ge(x_ready, b + 1)
                    sp.dma_start(x_rows[b], got[0][:, b * BCOL:(b + 1) * BCOL].rearrange("p (t d) -> p t d", d=D)
                                 ).then_inc(x_stored, 16)
                sp.wait_ge(x_stored, 16 * BATCH)


def ffn(core, w, c, x, x_out, tag):
    with ExitStack() as ctx:
        keep = {n: core.sb(ctx, f"keep_{n}{tag}", [P, TILES * D]) for n in ("x", "hid", "v", "ctx")}
        keep["xt"] = keep["v"]
        keep["logits"] = core.sb(ctx, f"keep_logits{tag}", [P, TILES * E])
        keep["gate"] = core.sb(ctx, f"keep_gate{tag}", [P, 2, TILES])
        keep["take"] = core.sb(ctx, f"keep_take{tag}", [P, 2, TILES], U32)
        keep["send"] = core.sb(ctx, f"keep_send{tag}", [P, 2, TILES], U32)
        with ExitStack() as units:
            buffers = attention_buffers(core, units, tag)
            ffn_project(core, keep, w, c, buffers, x, tag)
            ffn_attention(core, keep, w, c, buffers, tag)
        ffn_output(core, keep, w, c, tag)
        ffn_route(core, keep, c, tag)
        ffn_experts(core, keep, w, c, x_out, tag)


QKVB = 3 * D + H
SEG = TOK // P
SEGS = SEQ // SEG
R2 = 2 * HD
DFC = F // P
HT = BT // 2


def root_mean_square(vec, link, ms, mv):
    link(vec.tensor_tensor(ms[:, :], mv[:, :, 0], mv[:, :, 0], ALU.mult))
    return vec.tensor_tensor(ms[:, :], ms[:, :], mv[:, :, 1], ALU.add)


def delta_block(core, w, c, x_dram, x_out):
    nc = core.nc
    with ExitStack() as ctx:
        sb = lambda n, s, dt=F32: core.sb(ctx, "g_" + n, s, dt)
        sem = lambda n: core.sem(ctx, "g_" + n)
        x, hid = sb("x", [P, SEG * D]), sb("hid", [P, SEG * D])
        qkvb, kbeta = sb("qkvb", [P, SEG, QKVB]), sb("kbeta", [P, SEG, D])
        outs = sb("outs", [P, SEG, H, R2])
        wcat, bcat = sb("wcat", [P, QKVB]), sb("bcat", [P, QKVB])
        wo, w1, w2, b1 = sb("wo", [P, D]), sb("w1", [P, F]), sb("w2", [P, DFC, D]), sb("b1", [P, DFC])
        rows = {n: sb("row_" + n, [P, D]) for n in ("bo", "b2")}
        ln1_scale, ln2_scale = sb("ln1_scale", [P, 1]), sb("ln2_scale", [P, 1])
        w_loaded = sem("w_loaded")
        xs = x_dram.rearrange("(p j) d -> p (j d)", j=SEG)
        with ExitStack() as in1:
            sb1 = lambda n, s, dt=F32: core.sb(in1, "g1_" + n, s, dt)
            sem1 = lambda n: core.sem(in1, "g1_" + n)
            stats, mv, ms = sb1("stats", [P, BT, 6]), sb1("mv", [P, BT, 2]), sb1("ms", [P, BT])
            std, rstd = sb1("std", [P, BT]), sb1("rstd", [P, BT])
            h, hT = sb1("h", [P, BCOL]), sb1("hT", [P, BCOL])
            sq, norm = sb1("sq", [P, BT, D]), sb1("norm", [P, BT, H])
            nstd = sb1("nstd", [P, BT, H])
            pT = core.ps(in1, "g1_pT", [P, BCOL])
            pP = [core.ps(in1, f"g1_pP{i}", [P, 512]) for i in range(4)]
            x_loaded, stat_ready, std_ready, h_ready = sem1("x_loaded"), sem1("stat_ready"), sem1("std_ready"), sem1("h_ready")
            T_done, T_ready, p_done, p_used = sem1("T_done"), sem1("T_ready"), sem1("p_done"), sem1("p_used")
            dve, norm_ready, nstd_ready, beta_ready = (sem1(n) for n in ("dve", "norm_ready", "nstd_ready", "beta_ready"))
            with nc.Block() as block:
                @block.sync
                def _(sp):
                    def load(b):
                        sp.dma_start(x[:, bass.ds(b * BCOL, BCOL)], xs[:, bass.ds(b * BCOL, BCOL)]).then_inc(x_loaded, 16)

                    load(0)
                    at = 0
                    for n, width in (("q", D), ("k", D), ("v", D), ("beta", H)):
                        sp.dma_start(wcat[:, at:at + width], w["L0_attn_w" + n]).then_inc(w_loaded, 16)
                        sp.dma_start(bcat[:, at:at + width], w["L0_attn_b" + n].partition_broadcast(P)
                                     ).then_inc(w_loaded, 16)
                        at += width
                    for n in rows:
                        sp.dma_start(rows[n][:, :], w["L0_attn_" + n].partition_broadcast(P)).then_inc(w_loaded, 16)
                    for dst, n in ((ln1_scale, "ln1_scale"), (ln2_scale, "ln2_scale")):
                        sp.dma_start(dst[:, :], w["L0_attn_" + n].rearrange("(p o) -> p o", o=1)).then_inc(w_loaded, 16)
                    sp.dma_start(wo[:, :], w["L0_attn_wo"]).then_inc(w_loaded, 16)
                    sp.dma_start(w1[:, :], w["L0_attn_w1"]).then_inc(w_loaded, 16)
                    sp.dma_start(w2[:, :, :], w["L0_attn_w2"].rearrange("(c p) d -> p c d", p=P)).then_inc(w_loaded, 16)
                    sp.dma_start(b1[:, :], w["L0_attn_b1"].rearrange("(c p) -> p c", p=P),
                                 allow_slow_non_contiguous=True).then_inc(w_loaded, 16)
                    with sp.Fori(1, BATCH) as b:
                        apart(sp, x_loaded, b * 16)
                        load(b)
                    sp.wait_ge(w_loaded, 16 * 16)

                @block.vector
                def _(vec):
                    chain = Chain(vec, dve)
                    link = chain.link

                    def norms(b):
                        xb, hb = x[:, bass.ds(b * BCOL, BCOL)], hid[:, bass.ds(b * BCOL, BCOL)]
                        apart(vec, x_loaded, b * 16 + 16)
                        for n, src in enumerate((xb, hb)):
                            for t in range(BT):
                                last = vec.bn_stats(stats[:, t, :], src[:, t * D:(t + 1) * D])
                            link(last)
                            for t in range(BT):
                                last = vec.bn_aggr(mv[:, t, :], stats[:, t, :])
                            link(last)
                            if n == 0:
                                vec.tensor_copy(ms[:, :], mv[:, :, 1]).then_inc(stat_ready, 1)
                            else:
                                root_mean_square(vec, link, ms, mv).then_inc(stat_ready, 1)
                            vec.wait_ge(std_ready, b * 2 + (n + 1))
                            link(vec.reciprocal(rstd[:, :], std[:, :]))
                            if n == 0:
                                normalise(vec, link, hb, xb, mv, rstd)
                        reached(vec, T_done, b)
                        for t in range(BT):
                            last = vec.tensor_scalar(h[:, t * D:(t + 1) * D], hb[:, t * D:(t + 1) * D],
                                                     rstd[:, t:t + 1], None, ALU.mult)
                        last.then_inc(h_ready, 1)

                    def keys(b):
                        return qkvb[:, bass.ds(b * BT, BT), D:2 * D].rearrange("p t (h r) -> p t h r", r=HD)

                    def biases(b):
                        for t in range(BT):
                            vec.wait_ge(p_done, b * BT + (t + 1))
                            vec.tensor_tensor(qkvb[:, bass.ds(b * BT + t, 1), :].rearrange("p o c -> p (o c)"),
                                              pP[t % 4][:, 0:QKVB], bcat[:, :], ALU.add).then_inc(p_used, 1)
                        vec.wait_ge(p_used, b * BT + BT)
                        sq4 = sq[:, :, :].rearrange("p t (h r) -> p t h r", r=HD)
                        link(vec.tensor_tensor(sq4, keys(b), keys(b), ALU.mult))
                        vec.reduce_sum(norm[:, :, :], sq4, AX).then_inc(norm_ready, 1)

                    def unit_keys(b):
                        vec.wait_ge(nstd_ready, b + 1)
                        link(vec.tensor_scalar(nstd[:, :, :], nstd[:, :, :], 1e-6, None, ALU.add))
                        link(vec.reciprocal(norm[:, :, :], nstd[:, :, :]))
                        link(vec.tensor_tensor(keys(b), keys(b), norm[:, :, :].unsqueeze(3).to_broadcast([P, BT, H, HD]),
                                               ALU.mult))

                    def batch(b):
                        biases(b)
                        norms(b + 1)
                        unit_keys(b)

                    norms(0)
                    vec.wait_ge(w_loaded, 16 * 16)
                    batch(0)
                    for b in chain.each(BATCH - 2, 12, first=1):
                        batch(b)
                    biases(BATCH - 1)
                    unit_keys(BATCH - 1)
                    vec.wait_ge(beta_ready, 1)
                    vec.tensor_tensor(kbeta[:, :, :].rearrange("p j (h r) -> p j h r", r=HD),
                                      qkvb[:, :, D:2 * D].rearrange("p j (h r) -> p j h r", r=HD),
                                      qkvb[:, :, 3 * D:].unsqueeze(3).to_broadcast([P, SEG, H, HD]), ALU.mult)

                @block.scalar
                def _(act):
                    def roots(b):
                        for n in range(2):
                            act.wait_ge(stat_ready, b * 2 + (n + 1))
                            act.activation(std[:, :], ms[:, :], ACT.Sqrt, bias=c["eps"][:, n:n + 1]).then_inc(std_ready, 1)
                        act.wait_ge(T_done, b + 1)
                        reached(act, p_done, b * BT)
                        act.activation(hT[:, :], pT[:, :], ACT.Copy, scale=ln1_scale[:, 0:1]).then_inc(T_ready, 1)

                    def lengths(b):
                        act.wait_ge(norm_ready, b + 1)
                        act.activation(nstd[:, :, :], norm[:, :, :], ACT.Sqrt).then_inc(nstd_ready, 1)

                    def batch(b):
                        lengths(b)
                        roots(b + 1)

                    act.wait_ge(w_loaded, 16 * 16)
                    roots(0)
                    batch(0)
                    with act.Fori(1, BATCH - 1) as b:
                        batch(b)
                    lengths(BATCH - 1)
                    act.wait_ge(p_used, BATCH * BT)
                    act.activation(qkvb[:, :, 3 * D:], qkvb[:, :, 3 * D:], ACT.Sigmoid).then_inc(beta_ready, 1)

                @block.tensor
                def _(pe):
                    def project(b):
                        pe.wait_ge(h_ready, b + 1)
                        reached(pe, T_ready, b)
                        for t in range(BT):
                            last = pe.transpose(pT[:, t * P:(t + 1) * P], h[:, t * D:(t + 1) * D], c["ident"][:, :])
                        last.then_inc(T_done, 1)
                        pe.wait_ge(T_ready, b + 1)
                        for t in range(BT):
                            reached(pe, p_used, b * BT + (t - 3))
                            pe.matmul(pP[t % 4][:, 0:QKVB], hT[:, t * P:(t + 1) * P], wcat[:, :],
                                      start=True, stop=True).then_inc(p_done, 1)

                    pe.wait_ge(w_loaded, 16 * 16)
                    batches(pe, project)

        FULL = [P, H, R2, HD]
        with ExitStack() as in2:
            sb2 = lambda n, s, dt=F32: core.sb(in2, "g2_" + n, s, dt)
            sem2 = lambda n: core.sem(in2, "g2_" + n)
            R, prod, proq = sb2("R", FULL), sb2("prod", FULL), sb2("proq", FULL)
            Rk = sb2("Rk", [P, H, R2])
            pq = core.ps(in2, "g2_pq", [P, H * R2])
            start, dve, R_ready, q_mult, q_sum, q_kept = (sem2(n) for n in ("start", "dve", "R_ready", "q_mult", "q_sum", "q_kept"))
            stored, loaded = sem2("stored"), sem2("loaded")
            with nc.Block() as block:
                @block.gpsimd
                def _(pool):
                    pool.memset(R[:, :, :, :], 0.0).then_inc(start, 1)
                    pool.wait_ge(start, 1)
                    eye = R[:, :, HD:, :]
                    pool.affine_select(out=eye, in_=eye, compare_op=ALU.not_equal, fill=1.0, base=0,
                                       pattern=[[0, H], [1, HD], [-1, HD]], channel_multiplier=0).then_inc(start, 1)
                    with pool.Fori(0, SEG) as j:
                        pool.wait_ge(R_ready, j + 1)
                        q = qkvb[:, bass.ds(j, 1), 0:D].rearrange("p o (h r) -> p (o h) r", r=HD)
                        pool.tensor_tensor(proq[:, :, :, :], R[:, :, :, :], q.unsqueeze(2).to_broadcast(FULL),
                                           ALU.mult).then_inc(q_mult, 1)
                        apart(pool, q_sum, j + 1)

                @block.vector
                def _(vec):
                    chain = Chain(vec, dve)
                    link = chain.link
                    vec.wait_ge(start, 2)
                    def token(j):
                        k = qkvb[:, bass.ds(j, 1), D:2 * D].rearrange("p o (h r) -> p (o h) r", r=HD)
                        v = qkvb[:, bass.ds(j, 1), 2 * D:3 * D].rearrange("p o (h r) -> p (o h) r", r=HD)
                        kb = kbeta[:, bass.ds(j, 1), :].rearrange("p o (h r) -> p (o h) r", r=HD)
                        link(vec.tensor_tensor(prod[:, :, :, :], R[:, :, :, :], k.unsqueeze(2).to_broadcast(FULL), ALU.mult))
                        link(vec.reduce_sum(Rk[:, :, :], prod[:, :, :, :], AX))
                        link(vec.tensor_tensor(Rk[:, :, 0:HD], Rk[:, :, 0:HD], v, ALU.subtract))
                        link(vec.tensor_tensor(prod[:, :, :, :], Rk[:, :, :].unsqueeze(3).to_broadcast(FULL),
                                               kb.unsqueeze(2).to_broadcast(FULL), ALU.mult))
                        reached(vec, q_mult, j)
                        vec.tensor_tensor(R[:, :, :, :], R[:, :, :, :], prod[:, :, :, :], ALU.subtract).then_inc(R_ready, 1)
                        vec.wait_ge(R_ready, j + 1)

                    token(0)
                    token(1)
                    for turn in chain.each(SEG // 2 - 1, 8, first=1):
                        token(turn * 2)
                        token(turn * 2 + 1)

                @block.tensor
                def _(pe):
                    with pe.Fori(0, SEG) as j:
                        pe.wait_ge(q_mult, j + 1)
                        for e in range(HD):
                            last = pe.matmul(pq[:, :], c["ident"][:, :], proq[:, :, :, e].rearrange("p h r -> p (h r)"),
                                             start=e == 0, stop=e == HD - 1)
                        last.then_inc(q_sum, 1)
                        pe.wait_ge(q_kept, j + 1)

                @block.scalar
                def _(act):
                    with act.Fori(0, SEG) as j:
                        act.wait_ge(q_sum, j + 1)
                        act.copy(outs[:, bass.ds(j, 1), :, :].rearrange("p o h r -> p (o h r)"), pq[:, :]).then_inc(q_kept, 1)

                @block.sync
                def _(sp):
                    sp.wait_ge(R_ready, SEG)
                    sp.dma_start(w["segments"].rearrange("p h x -> p (h x)"),
                                 R[:, :, :, :].rearrange("p h r e -> p (h r e)")).then_inc(stored, 16)
                    sp.wait_ge(stored, 16)

        with ExitStack() as in3:
            sb3 = lambda n, s, dt=F32: core.sb(in3, "g3_" + n, s, dt)
            sem3 = lambda n: core.sem(in3, "g3_" + n)
            HR = HD // 2
            Rt, S = sb3("Rt", [P, SEGS, (HR + HD) * HD]), sb3("S", [P, SEGS, HR, HD])
            prod, part = sb3("prod", [P, HR, HD, HD]), sb3("part", [P, HR, HD])
            loaded, dve, S_ready, stored = sem3("loaded"), sem3("dve"), sem3("S_ready"), sem3("stored")
            ALL = [P, HR, HD, HD]
            with nc.Block() as block:
                @block.sync
                def _(sp):
                    for half in range(2):
                        for b in range(BATCH):
                            at = (half * BATCH + b) * H
                            segments = w["segments"][b * SEGS:(b + 1) * SEGS].rearrange("s h x -> h s x")
                            sp.dma_start(Rt[at:at + H, :, 0:HR * HD],
                                         segments[:, :, half * HR * HD:(half + 1) * HR * HD]).then_inc(loaded, 16)
                            sp.dma_start(Rt[at:at + H, :, HR * HD:], segments[:, :, HD * HD:]).then_inc(loaded, 16)
                    sp.wait_ge(S_ready, 1)
                    for half in range(2):
                        for b in range(BATCH):
                            at = (half * BATCH + b) * H
                            sp.dma_start(w["entries"][b * SEGS:(b + 1) * SEGS].rearrange("s h x -> h s x")
                                         [:, :, half * HR * HD:(half + 1) * HR * HD],
                                         S[at:at + H, :, :, :].rearrange("p s d e -> p s (d e)")).then_inc(stored, 16)
                    sp.wait_ge(stored, 16 * 2 * BATCH)

                @block.vector
                def _(vec):
                    chain = Chain(vec, dve)
                    link = chain.link
                    link(vec.memset(S[:, 0:1, :, :], 0.0))
                    vec.wait_ge(loaded, 16 * 4 * BATCH)
                    def segment(s):
                        Sv = S[:, bass.ds(s, 1), :, :].rearrange("p o d e -> p (o d) e")
                        M = Rt[:, bass.ds(s, 1), HR * HD:].rearrange("p o (e f) -> p (o f) e", e=HD)
                        local = Rt[:, bass.ds(s, 1), 0:HR * HD].rearrange("p o x -> p (o x)")
                        link(vec.tensor_tensor(prod[:, :, :, :], Sv.unsqueeze(2).to_broadcast(ALL),
                                               M.unsqueeze(1).to_broadcast(ALL), ALU.mult))
                        link(vec.reduce_sum(part[:, :, :], prod[:, :, :, :], AX))
                        link(vec.tensor_tensor(S[:, bass.ds(s + 1, 1), :, :].rearrange("p o d e -> p (o d e)"),
                                               part[:, :, :].rearrange("p d f -> p (d f)"), local, ALU.add))

                    segment(0)
                    for turn in chain.each((SEGS - 2) // 3, 9):
                        for n in range(3):
                            segment(turn * 3 + (n + 1))
                    vec.sem_inc(S_ready, 1)

        with ExitStack() as in4:
            sb4 = lambda n, s, dt=F32: core.sb(in4, "g4_" + n, s, dt)
            sem4 = lambda n: core.sem(in4, "g4_" + n)
            HALF = [P, H, HD, HD]
            MH = SEQ // 2
            S = sb4("S", HALF)
            prod = [sb4(f"prod{i}", HALF)[:, :, :, :] for i in range(HT)]
            prod += [kbeta[:, i * BT:(i + 1) * BT, :].rearrange("p t (h x) -> p (t h) x", h=2)
                     .rearrange("p h (d e) -> p h d e", d=HD) for i in range(HT)]
            stats, mv, ms = sb4("stats", [P, BT, 6]), sb4("mv", [P, BT, 2]), sb4("ms", [P, BT])
            std, rstd = sb4("std", [P, BT]), sb4("rstd", [P, BT])
            osum, oT = sb4("osum", [P, BT, D]), sb4("oT", [P, BCOL])
            h2, h2T = sb4("h2", [P, BCOL]), sb4("h2T", [P, BCOL])
            gT = [sb4(f"gT{i}", [P, MH]) for i in range(DFC)]
            pT, pO, pY = (core.ps(in4, "g4_" + n, [P, BCOL]) for n in ("pT", "pO", "pY"))
            pH = [core.ps(in4, f"g4_pH{i}", [P, MH]) for i in range(2)]
            (S_loaded, prod_ready, prod_used, osum_ready, oT_done, oT_ready, o_done, stat_ready, std_ready, h2_ready,
             hT_done, h2T_ready, h_done, g_ready, y_done, y_ready, y_stored, dve) = (sem4(n) for n in (
                 "S_loaded", "prod_ready", "prod_used", "osum_ready", "oT_done", "oT_ready", "o_done", "stat_ready",
                 "std_ready", "h2_ready", "hT_done", "h2T_ready", "h_done", "g_ready", "y_done", "y_ready", "y_stored",
                 "dve"))
            out_rows = x_out.rearrange("(p j) d -> p (j d)", j=SEG)
            with nc.Block() as block:
                @block.sync
                def _(sp):
                    sp.dma_start(S[:, :, :, :].rearrange("p h d e -> p (h d e)"),
                                 w["entries"].rearrange("p h x -> p (h x)")).then_inc(S_loaded, 16)
                    with sp.Fori(0, BATCH) as b:
                        sp.wait_ge(y_ready, b + 1)
                        sp.dma_start(out_rows[:, bass.ds(b * BCOL, BCOL)], x[:, bass.ds(b * BCOL, BCOL)]).then_inc(y_stored, 16)
                    sp.wait_ge(y_stored, 16 * BATCH)

                @block.gpsimd
                def _(pool):
                    pool.wait_ge(S_loaded, 16)

                    def products(b):
                        for t in range(BT):
                            reached(pool, prod_used, (b - 1) * BT + (t + 1))
                            Mq = outs[:, bass.ds(b * BT + t, 1), :, HD:].rearrange("p o h e -> p (o h) e")
                            pool.tensor_tensor(prod[t], S[:, :, :, :], Mq.unsqueeze(2).to_broadcast(HALF),
                                               ALU.mult).then_inc(prod_ready, 1)

                    batches(pool, products)

                @block.vector
                def _(vec):
                    chain = Chain(vec, dve)
                    link = chain.link

                    def sums(b):
                        reached(vec, oT_done, b)
                        for t in range(BT):
                            vec.wait_ge(prod_ready, b * BT + (t + 1))
                            vec.reduce_sum(osum[:, t, :].rearrange("p (h d) -> p h d", d=HD), prod[t],
                                           AX).then_inc(prod_used, 1)
                        own = outs[:, bass.ds(b * BT, BT), :, 0:HD]
                        o4 = osum[:, :, :].rearrange("p t (h d) -> p t h d", d=HD)
                        vec.wait_ge(prod_used, b * BT + BT)
                        vec.tensor_tensor(o4, o4, own, ALU.add).then_inc(osum_ready, 1)

                    def norm(b):
                        hb, xb = hid[:, bass.ds(b * BCOL, BCOL)], x[:, bass.ds(b * BCOL, BCOL)]
                        vec.wait_ge(o_done, b + 1)
                        link(vec.tensor_tensor(hb, hb, pO[:, :], ALU.add))
                        per_column(vec, link, hb, hb, rows["bo"], ALU.add)
                        for t in range(BT):
                            last = vec.bn_stats(stats[:, t, :], hb[:, t * D:(t + 1) * D])
                        link(last)
                        for t in range(BT):
                            last = vec.bn_aggr(mv[:, t, :], stats[:, t, :])
                        link(last)
                        root_mean_square(vec, link, ms, mv).then_inc(stat_ready, 1)
                        link(vec.tensor_tensor(xb, xb, hb, ALU.add))
                        vec.wait_ge(std_ready, b + 1)
                        link(vec.reciprocal(rstd[:, :], std[:, :]))
                        reached(vec, hT_done, b)
                        for t in range(BT):
                            last = vec.tensor_scalar(h2[:, t * D:(t + 1) * D], hb[:, t * D:(t + 1) * D],
                                                     rstd[:, t:t + 1], None, ALU.mult)
                        last.then_inc(h2_ready, 1)
                        per_column(vec, link, xb, xb, rows["b2"], ALU.add)

                    def finish(b):
                        xb = x[:, bass.ds(b * BCOL, BCOL)]
                        vec.wait_ge(y_done, b * 2 + 2)
                        vec.tensor_tensor(xb, xb, pY[:, :], ALU.add).then_inc(y_ready, 1)

                    def batch(b):
                        sums(b + 1)
                        norm(b + 1)
                        finish(b)

                    sums(0)
                    norm(0)
                    batch(0)
                    for b in chain.each(BATCH - 2, 8, first=1):
                        batch(b)
                    finish(BATCH - 1)

                @block.scalar
                def _(act):
                    def output(b):
                        act.wait_ge(oT_done, b + 1)
                        act.copy(oT[:, :], pT[:, :]).then_inc(oT_ready, 1)

                    def root(b):
                        act.wait_ge(stat_ready, b + 1)
                        act.activation(std[:, :], ms[:, :], ACT.Sqrt, bias=c["eps"][:, 1:2]).then_inc(std_ready, 1)

                    def gelu(b, half):
                        for f in range(DFC):
                            act.wait_ge(h_done, b * 8 + (half * DFC + f + 1))
                            if f == 0:
                                reached(act, y_done, b * 2 + half)
                            act.activation(gT[f][:, :], pH[f % 2][:, :], ACT.Gelu_apprx_tanh,
                                           bias=b1[:, f:f + 1]).then_inc(g_ready, 1)

                    def batch(b, more=True):
                        act.wait_ge(hT_done, b + 1)
                        act.activation(h2T[:, :], pT[:, :], ACT.Copy, scale=ln2_scale[:, 0:1]).then_inc(h2T_ready, 1)
                        gelu(b, 0)
                        if more:
                            output(b + 1)
                        gelu(b, 1)
                        if more:
                            root(b + 1)

                    output(0)
                    root(0)
                    batch(0)
                    with act.Fori(1, BATCH - 1) as b:
                        batch(b)
                    batch(BATCH - 1, more=False)

                @block.tensor
                def _(pe):
                    def output(b):
                        pe.wait_ge(osum_ready, b + 1)
                        reached(pe, h2T_ready, b)
                        for t in range(BT):
                            last = pe.transpose(pT[:, t * P:(t + 1) * P], osum[:, t, :], c["ident"][:, :])
                        last.then_inc(oT_done, 1)
                        pe.wait_ge(oT_ready, b + 1)
                        reached(pe, h2_ready, b)
                        for t in range(BT):
                            last = pe.matmul(pO[:, t * D:(t + 1) * D], oT[:, t * P:(t + 1) * P], wo[:, :], start=True, stop=True)
                        last.then_inc(o_done, 1)

                    def mlp(b, half):
                        for f in range(DFC):
                            reached(pe, g_ready, b * 8 + (half * DFC + f - 1))
                            pe.matmul(pH[f % 2][:, :], w1[:, f * P:(f + 1) * P], h2T[:, half * MH:(half + 1) * MH],
                                      start=True, stop=True).then_inc(h_done, 1)
                        pe.wait_ge(g_ready, b * 8 + (half * DFC + DFC))
                        if half == 0:
                            reached(pe, y_ready, b)
                        for t in range(half * HT, (half + 1) * HT):
                            for f in range(DFC):
                                last = pe.matmul(pY[:, t * D:(t + 1) * D], gT[f][:, (t % HT) * P:(t % HT + 1) * P],
                                                 w2[:, f, :], start=f == 0, stop=f == DFC - 1)
                        last.then_inc(y_done, 1)

                    def batch(b, more=True):
                        pe.wait_ge(h2_ready, b + 1)
                        for t in range(BT):
                            last = pe.transpose(pT[:, t * P:(t + 1) * P], h2[:, t * D:(t + 1) * D], c["ident"][:, :])
                        last.then_inc(hT_done, 1)
                        pe.wait_ge(h2T_ready, b + 1)
                        mlp(b, 0)
                        if more:
                            output(b + 1)
                        mlp(b, 1)

                    output(0)
                    batch(0)
                    with pe.Fori(1, BATCH - 1) as b:
                        batch(b)
                    batch(BATCH - 1, more=False)


def build(nc, names, aps, out):
    w = dict(zip(names, aps))
    with ExitStack() as ctx:
        core = Core(nc, ctx)
        scratch = lambda n, shape, dt=F32: nc.dram_tensor(n, shape, dt, kind="Internal").ap()
        w["qk_parts"] = scratch("qk_parts", [2, 3, UNITS, GH * HD, SEQ], BF16)
        w["neg_max"] = scratch("neg_max", [3, 3 * GH, SEQ], BF16)
        w["xin"] = scratch("xin", [SLOTS + TOK * 2, D])
        w["eout"] = scratch("eout", [SLOTS, D])
        w["segments"] = scratch("segments", [P, H, R2 * HD])
        w["entries"] = scratch("entries", [P, H, HD * HD])
        x1, x2 = scratch("x1", [TOK, D]), scratch("x2", [TOK, D])
        flat = lambda a: a.rearrange("b s d -> (b s) d")
        c = constants(core, ctx, w)
        with nc.cleanup_on_exit():
            ffn(core, w, c, flat(w["L0_attn_x"]), x1, "_1")
        with nc.cleanup_on_exit():
            delta_block(core, w, c, x1, x2)
        with nc.cleanup_on_exit():
            ffn(core, w, c, x2, flat(out), "_2")


_INS = ["L0_attn_x", "L0_attn_wq", "L0_attn_bq", "L0_attn_wk", "L0_attn_bk", "L0_attn_wv", "L0_attn_bv",
        "L0_attn_wbeta", "L0_attn_bbeta", "L0_attn_wo", "L0_attn_bo", "L0_attn_w1", "L0_attn_b1", "L0_attn_w2",
        "L0_attn_b2", "L0_attn_ln1_scale", "L0_attn_ln2_scale", "L0_ffn_ln1_w", "L0_ffn_ln1_b", "L0_ffn_q_w",
        "L0_ffn_q_b", "L0_ffn_k_w", "L0_ffn_k_b", "L0_ffn_v_w", "L0_ffn_v_b", "L0_ffn_o_w", "L0_ffn_o_b",
        "L0_ffn_ln2_w", "L0_ffn_ln2_b", "L0_ffn_router_w", "L0_ffn_fc1_w", "L0_ffn_fc1_b", "L0_ffn_fc2_w",
        "L0_ffn_fc2_b"]
_OUTS = [((4, 1024, 128), "float32")]


def kernel(**inputs):
    import numpy as _np
    import concourse.bacc as _bacc
    from concourse import mybir as _mybir
    from concourse.bass_utils import run_bass_kernel_spmd as _run

    nc = _bacc.Bacc("TRN2", target_bir_lowering=False, num_devices=1)
    arrays, args = {}, []
    for name in _INS:
        a = _np.ascontiguousarray(inputs[name])
        arrays[f"in_{name}_dram"] = a
        args.append(nc.dram_tensor(f"in_{name}_dram", a.shape, _mybir.dt.from_np(a.dtype), kind="ExternalInput").ap())
    for i, (shape, dtype) in enumerate(_OUTS):
        dt = _mybir.dt.from_np(_np.dtype(dtype))
        args.append(nc.dram_tensor(f"out_{i}_dram", shape, dt, kind="ExternalOutput").ap())
    build(nc, _INS, args[:-1], args[-1])
    r = _run(nc, [arrays], core_ids=[0])
    return r.results[0]["out_0_dram"]
```

```python
from contextlib import ExitStack

import concourse.bass as bass
from concourse import mybir

F32 = mybir.dt.float32
BF16 = mybir.dt.bfloat16
U32 = mybir.dt.uint32
ALU = mybir.AluOpType
ACT = mybir.ActivationFunctionType
AX = mybir.AxisListType.X

P = 128
BATCH, SEQ, D = 4, 1024, 128
TOK = BATCH * SEQ
TILES = TOK // P
BT = SEQ // P
BCOL = BT * D
H, HD = 16, 8
GH = 4
GROUPS = H // GH
UNITS = BATCH * GROUPS
E, F = 16, 512
FC = F // P
CAP = 2 * ((TOK + E - 1) // E)
CC = CAP // P
SLOTS = E * CAP
ROW = D + 1
WIPES = 8
LOWEST = -3.0e38
LN_EPS = 1e-5
RMS_EPS = 1e-6
F32_EPS = 1.1920928955078125e-07
Q_SPLIT = (0, 0, 0, 1, 1, 2)
K_SPLIT = (0, 1, 2, 0, 1, 0)
TERMS = len(Q_SPLIT)
KROWS = TERMS * HD
MROW = P - 3


PASSED = []


class Chain:

    def __init__(self, eng, sem):
        self.eng, self.sem, self.n, self.turn = eng, sem, 0, 0

    def link(self, ins):
        self.n += 1
        ins.then_inc(self.sem, 1)
        apart(self.eng, self.sem, self.turn + self.n)

    def each(self, turns, per_turn, first=0):
        base = self.n
        with self.eng.Fori(first, first + turns) as i:
            self.turn = i * per_turn - first * per_turn
            yield i
            assert self.n - base == per_turn, (self.n - base, per_turn)
        self.turn = 0
        self.n = base + turns * per_turn


class Core:

    def __init__(self, nc, ctx):
        self.nc = nc
        PASSED[:] = [self.sem(ctx, "passed")]

    def sb(self, ctx, name, shape, dt=F32):
        return ctx.enter_context(self.nc.sbuf_tensor(name, shape, dt))

    def ps(self, ctx, name, shape, dt=F32):
        return ctx.enter_context(self.nc.psum_tensor(name, shape, dt))

    def sem(self, ctx, name):
        return self.nc.alloc_semaphore(name)


def normalise(vec, link, out, x, mv, rstd):
    for t in range(BT):
        last = vec.tensor_scalar(out[:, t * D:(t + 1) * D], x[:, t * D:(t + 1) * D],
                                 mv[:, t, 0:1], rstd[:, t:t + 1], ALU.subtract, ALU.mult)
    link(last)


def per_column(vec, link, out, x, row, op):
    link(vec.tensor_tensor(out.rearrange("p (t d) -> p t d", d=D), x.rearrange("p (t d) -> p t d", d=D),
                           row[:, :].unsqueeze(1).to_broadcast([P, BT, D]), op))


def apart(eng, sem, count):
    eng.wait_ge(sem, count)
    if not isinstance(count, int):
        eng.sem_inc(PASSED[0], 1)


def reached(eng, sem, count):
    if not isinstance(count, int) or count > 0:
        eng.wait_ge(sem, count)


def constants(core, ctx, w):
    c = {}
    for name in ("ident", "upper", "ones"):
        c[name] = core.sb(ctx, name, [P, P])
    c["ident_b"] = core.sb(ctx, "ident_b", [P, P], BF16)
    c["causal"] = core.sb(ctx, "causal", [P, SEQ])
    c["rev"] = core.sb(ctx, "rev_expert", [P, E])
    c["num"] = core.sb(ctx, "expert_number", [P, E])
    c["spill"] = core.sb(ctx, "spill_row", [P, TILES])
    c["restart"] = core.sb(ctx, "restart", [P, E, TILES])
    c["eps"] = core.sb(ctx, "eps", [P, 2])
    c["zero"] = core.sb(ctx, "zero", [P, SLOTS * ROW // (P * 4)])
    c["slot"] = core.sb(ctx, "slot", [P, CC])
    c["unused"] = core.sb(ctx, "unused", [P, E, CC])
    c["wiped"] = core.sem(ctx, "slots_wiped")
    rows = ("L0_ffn_v_b", "L0_ffn_o_b", "L0_ffn_ln2_w", "L0_ffn_ln2_b")
    mats = ("L0_ffn_q_w", "L0_ffn_k_w", "L0_ffn_v_w", "L0_ffn_o_w")
    for n in rows:
        c[n] = core.sb(ctx, "row_" + n, [P, D])
    for n in mats:
        c[n] = core.sb(ctx, "sb_" + n, [P, D])
    c["router"] = core.sb(ctx, "sb_router", [P, E])
    cols = {"qb": "L0_ffn_q_b", "kb": "L0_ffn_k_b", "ln1_w": "L0_ffn_ln1_w", "ln1_b": "L0_ffn_ln1_b",
            "ln2_w": "L0_ffn_ln2_w", "ln2_b": "L0_ffn_ln2_b"}
    for n in (*cols, "qb_scaled"):
        c[n] = core.sb(ctx, "col_" + n, [P, 1])
    loads = len(rows) + len(mats) + 1 + len(cols)
    s_load = core.sem(ctx, "const_loaded")
    s_set = core.sem(ctx, "const_set")
    nc = core.nc
    with nc.Block() as block:
        @block.sync
        def _(sp):
            for n in rows:
                sp.dma_start(c[n][:, :], w[n].partition_broadcast(P)).then_inc(s_load, 16)
            for n in mats:
                sp.dma_start(c[n][:, :], w[n]).then_inc(s_load, 16)
            sp.dma_start(c["router"][:, :], w["L0_ffn_router_w"]).then_inc(s_load, 16)
            for n, vector in cols.items():
                sp.dma_start(c[n][:, :], w[vector].rearrange("(p o) -> p o", o=1)).then_inc(s_load, 16)
            sp.wait_ge(s_load, 16 * loads)

        @block.vector
        def _(vec):
            vec.memset(c["zero"][:, :], 0.0)
            vec.memset(c["eps"][:, 0:1], LN_EPS)
            vec.memset(c["eps"][:, 1:2], RMS_EPS)
            vec.memset(c["ones"][:, :], 1.0)
            vec.wait_ge(s_load, 16 * loads)
            vec.tensor_scalar(c["qb_scaled"][:, :], c["qb"][:, :], HD ** -0.5, None, ALU.mult)

        @block.gpsimd
        def _(pool):
            chain = Chain(pool, s_set)
            chain.link(pool.memset(c["ident"][:, :], 0.0))
            chain.link(pool.affine_select(out=c["ident"][:, :], in_=c["ident"][:, :], compare_op=ALU.not_equal, fill=1.0,
                                          base=0, pattern=[[-1, P]], channel_multiplier=1))
            chain.link(pool.tensor_copy(c["ident_b"][:, :], c["ident"][:, :]))
            chain.link(pool.memset(c["upper"][:, :], 1.0))
            chain.link(pool.affine_select(out=c["upper"][:, :], in_=c["upper"][:, :], compare_op=ALU.is_ge, fill=0.0,
                                          base=0, pattern=[[1, P]], channel_multiplier=-1))
            chain.link(pool.memset(c["causal"][:, :], 0.0))
            chain.link(pool.affine_select(out=c["causal"][:, SEQ - P:], in_=c["causal"][:, SEQ - P:],
                                          compare_op=ALU.is_ge, fill=LOWEST,
                                          base=0, pattern=[[-1, P]], channel_multiplier=1))
            pool.iota(c["rev"][:, :], pattern=[[-1, E]], base=E, channel_multiplier=0,
                      allow_small_or_imprecise_dtypes=True)
            pool.iota(c["num"][:, :], pattern=[[1, E]], base=0, channel_multiplier=0,
                      allow_small_or_imprecise_dtypes=True)
            pool.iota(c["spill"][:, :], pattern=[[P, TILES]], base=SLOTS, channel_multiplier=1,
                      allow_small_or_imprecise_dtypes=True)
            pool.iota(c["slot"][:, :], pattern=[[1, CC]], base=0, channel_multiplier=CC,
                      allow_small_or_imprecise_dtypes=True)
            pool.iota(c["unused"][:, :, :], pattern=[[CAP, E], [1, CC]], base=2 * TOK, channel_multiplier=CC,
                      allow_small_or_imprecise_dtypes=True)
            chain.link(pool.memset(c["restart"][:, :, :], 1.0))
            chain.link(pool.memset(c["restart"][:, :, 0:1], 0.0))
    return c


def wipe(sp, w, c):
    for target in (w["xin"][0:SLOTS, :], w["y"][0:2 * TOK, :]):
        flat = target.rearrange("r d -> (r d)").rearrange("(n p x) -> n p x", n=WIPES // 2, p=P)
        for n in range(WIPES // 2):
            sp.dma_start(flat[n], c["zero"][:, 0:flat.shape[2]]).then_inc(c["wiped"], 16)


def attention_buffers(core, ctx, tag):
    a = {"qa": [core.sb(ctx, f"qa{i}{tag}", [P, GH, SEQ], BF16) for i in range(3)],
         "ka": [core.sb(ctx, f"ka{i}{tag}", [P, GH, SEQ], BF16) for i in range(3)],
         "va": [core.sb(ctx, f"va{i}{tag}", [P, BT, GH, 32]) for i in range(3)],
         "qk_loaded": [core.sem(ctx, f"qk_loaded{i}{tag}") for i in range(3)]}
    return a


def load_qk(sp, w, a, stage, u):
    for dst, which, split in ((a["qa"][stage], 0, Q_SPLIT), (a["ka"][stage], 1, K_SPLIT)):
        for r in range(TERMS):
            sp.dma_start(dst[r * HD:(r + 1) * HD, :, :],
                         w["qk_parts"][which, split[r], bass.ds(u, 1)]
                         .rearrange("o (h d) t -> (o d) h t", d=HD)).then_inc(a["qk_loaded"][stage], 16)


def batches(eng, one):
    one(0)
    with eng.Fori(1, BATCH) as b:
        one(b)


def ffn_project(core, keep, w, c, a, x_dram, tag, first_layer=True):
    nc = core.nc
    with ExitStack() as ctx:
        sb = lambda n, s, dt=F32: core.sb(ctx, n + tag, s, dt)
        ps = lambda n, s, dt=F32: core.ps(ctx, n + tag, s, dt)
        sem = lambda n: core.sem(ctx, n + tag)
        stats, mv, rstd = sb("stats", [P, BT, 6]), sb("mv", [P, BT, 2]), sb("rstd", [P, BT])
        std = sb("std", [P, BT])
        xn, xT = sb("xn", [P, BCOL]), sb("xT", [P, SEQ])
        full = [sb("qf", [P, SEQ]), sb("kf", [P, SEQ])]
        rest = [sb("qr", [P, SEQ]), sb("kr", [P, SEQ])]
        parts = [sb("qp", [P, 3, SEQ], BF16), sb("kp", [P, 3, SEQ], BF16)]
        pT, pV = ps("pT", [P, SEQ]), ps("pV", [P, BCOL])
        pQK = [ps("pQ", [P, SEQ]), ps("pK", [P, SEQ])]
        x_loaded, var_ready, std_ready = sem("x_loaded"), sem("var_ready"), sem("std_ready")
        xn_ready, xnT_ready, xT_ready = sem("xn_ready"), sem("xnT_ready"), sem("xT_ready")
        qk_ready, v_ready, v_kept = sem("qk_ready"), sem("v_ready"), sem("v_kept")
        full_ready, rest_ready, second_ready = sem("full_ready"), sem("rest_ready"), sem("second_ready")
        parts_ready, parts_stored = sem("parts_ready"), sem("parts_stored")
        stages_set, va_zero, dve = sem("stages_set"), sem("va_zero"), sem("dve")
        x_rows = x_dram.rearrange("(b t p) d -> b p t d", p=P, t=BT)
        with nc.Block() as block:
            @block.sync
            def _(sp):
                with sp.Fori(0, BATCH) as b:
                    sp.dma_start(keep["x"][:, bass.ds(b * BCOL, BCOL)].rearrange("p (t d) -> p t d", d=D),
                                 x_rows[bass.ds(b, 1)].rearrange("o p t d -> (o p) t d")).then_inc(x_loaded, 16)
                    apart(sp, x_loaded, b * 16 + 16)

                def store(b):
                    for s in range(2):
                        sp.wait_ge(parts_ready, b * 2 + (s + 1))
                        for r in range(3):
                            sp.dma_start(w["qk_parts"][s, r, bass.ds(b * GROUPS, GROUPS)]
                                         .rearrange("g h t -> (g h) t"), parts[s][:, r, :]).then_inc(parts_stored, 16)

                store(0)
                sp.wait_ge(stages_set, 1)
                sp.wait_ge(parts_stored, 96)
                for u in range(3):
                    load_qk(sp, w, a, u, u)
                with sp.Fori(1, BATCH) as b:
                    store(b)
                sp.wait_ge(parts_stored, BATCH * 96)
                for u in range(3):
                    sp.wait_ge(a["qk_loaded"][u], 32 * TERMS)
                if first_layer:
                    wipe(sp, w, c)

            @block.gpsimd
            def _(pool):
                for st in range(3):
                    pool.memset(a["qa"][st][:, :, :], 0.0)
                    pool.memset(a["ka"][st][:, :, :], -1.0)
                    pool.memset(a["va"][st][:, :, :, :], 0.0).then_inc(va_zero, 1)
                pool.wait_ge(va_zero, 3)
                for st in range(3):
                    last = pool.memset(a["va"][st][:, :, :, HD:HD + 1], 1.0)
                last.then_inc(stages_set, 1)

            @block.vector
            def _(vec):
                chain = Chain(vec, dve)
                link = chain.link

                def norm(b, n):
                    x = keep["x"][:, bass.ds(b * BCOL, BCOL)]
                    hidden = keep["hid"][:, bass.ds(b * BCOL, BCOL)]
                    src, dst = ((x, hidden), (hidden, xn[:, :]))[n]
                    if n == 0:
                        apart(vec, x_loaded, b * 16 + 16)
                    for t in range(BT):
                        last = vec.bn_stats(stats[:, t, :], src[:, t * D:(t + 1) * D])
                    link(last)
                    for t in range(BT):
                        last = vec.bn_aggr(mv[:, t, :], stats[:, t, :])
                    last.then_inc(var_ready, 1)
                    vec.wait_ge(std_ready, b * 2 + (n + 1))
                    link(vec.reciprocal(rstd[:, :], std[:, :]))
                    if n == 1:
                        reached(vec, xnT_ready, b)
                    normalise(vec, link, dst, src, mv, rstd)
                    if n == 1:
                        vec.sem_inc(xn_ready, 1)

                def values(b):
                    vec.wait_ge(v_ready, b + 1)
                    vec.tensor_tensor(
                        keep["v"][:, bass.ds(b * GROUPS * BT * GH * HD, GROUPS * BT * GH * HD)]
                        .rearrange("p (g t r) -> p g t r", g=GROUPS, t=BT),
                        pV[:, :].rearrange("p (t g r) -> p g t r", t=BT, g=GROUPS),
                        c["L0_ffn_v_b"][:, :].rearrange("p (g r) -> p g r", g=GROUPS).unsqueeze(2)
                        .to_broadcast([P, GROUPS, BT, GH * HD]), ALU.add).then_inc(v_kept, 1)

                def remainder(b):
                    for s in range(2):
                        vec.wait_ge(full_ready, b * 2 + (s + 1))
                        vec.tensor_tensor(rest[s][:, :], full[s][:, :], parts[s][:, 0, :],
                                          ALU.subtract).then_inc(rest_ready, 1)

                def third(b):
                    for s in range(2):
                        vec.wait_ge(second_ready, b * 2 + (s + 1))
                        vec.tensor_tensor(parts[s][:, 2, :], rest[s][:, :], parts[s][:, 1, :],
                                          ALU.subtract).then_inc(parts_ready, 1)

                def batch(b):
                    norm(b + 1, 0)
                    values(b)
                    remainder(b)
                    norm(b + 1, 1)
                    third(b)

                norm(0, 0)
                norm(0, 1)
                batch(0)
                for b in chain.each(BATCH - 2, 6, first=1):
                    batch(b)
                values(BATCH - 1)
                remainder(BATCH - 1)
                third(BATCH - 1)

            @block.scalar
            def _(act):
                def root(b, n):
                    act.wait_ge(var_ready, b * 2 + (n + 1))
                    act.activation(std[:, :], mv[:, :, 1], ACT.Sqrt, bias=c["eps"][:, 0:1]).then_inc(std_ready, 1)

                def batch(b, more=True):
                    act.wait_ge(xnT_ready, b + 1)
                    reached(act, v_ready, b)
                    act.activation(xT[:, :], pT[:, :], ACT.Identity, bias=c["ln1_b"][:, 0:1],
                                   scale=c["ln1_w"][:, 0:1]).then_inc(xT_ready, 1)
                    if more:
                        root(b + 1, 0)
                    reached(act, parts_stored, b * 96)
                    for s, bias in ((0, "qb_scaled"), (1, "kb")):
                        scale = HD ** -0.5 if s == 0 else 1.0
                        act.wait_ge(qk_ready, b * 2 + (s + 1))
                        act.activation(full[s][:, :], pQK[s][:, :], ACT.Identity, bias=c[bias][:, 0:1], scale=scale)
                        act.activation(parts[s][:, 0, :], pQK[s][:, :], ACT.Identity, bias=c[bias][:, 0:1],
                                       scale=scale).then_inc(full_ready, 1)
                    for s in range(2):
                        act.wait_ge(rest_ready, b * 2 + (s + 1))
                        act.copy(parts[s][:, 1, :], rest[s][:, :]).then_inc(second_ready, 1)
                    if more:
                        root(b + 1, 1)

                root(0, 0)
                root(0, 1)
                batch(0)
                with act.Fori(1, BATCH - 1) as b:
                    batch(b)
                batch(BATCH - 1, more=False)

            @block.tensor
            def _(pe):
                def batch(b):
                    pe.wait_ge(xn_ready, b + 1)
                    reached(pe, xT_ready, b)
                    for t in range(BT):
                        last = pe.transpose(pT[:, t * P:(t + 1) * P], xn[:, t * D:(t + 1) * D], c["ident"][:, :])
                    last.then_inc(xnT_ready, 1)
                    pe.wait_ge(xT_ready, b + 1)
                    reached(pe, full_ready, b * 2)
                    for s, name in ((0, "L0_ffn_q_w"), (1, "L0_ffn_k_w")):
                        for half in range(2):
                            last = pe.matmul(pQK[s][:, half * 512:(half + 1) * 512], c[name][:, :],
                                             xT[:, half * 512:(half + 1) * 512], start=True, stop=True)
                        last.then_inc(qk_ready, 1)
                    reached(pe, v_kept, b)
                    for t in range(BT):
                        last = pe.matmul(pV[:, t * D:(t + 1) * D], xT[:, t * P:(t + 1) * P], c["L0_ffn_v_w"][:, :],
                                         start=True, stop=True)
                    last.then_inc(v_ready, 1)

                batches(pe, batch)


class Step:

    def __init__(self, u, stage, fills):
        self.u, self.stage, self.fills = u, stage, fills

    def shift(self, d):
        at = self.stage + d
        return Step(self.u + d, at % 3, self.fills + at // 3)


def attention_steps(eng, step, last_b, first_a):
    first_a(Step(0, 0, 0))
    step(Step(1, 1, 0))
    with eng.Fori(0, (UNITS - 4) // 3) as turn:
        for n in range(3):
            step(Step(turn * 3 + (n + 2), (n + 2) % 3, turn + (n + 2) // 3))
    for u in (UNITS - 2, UNITS - 1):
        step(Step(u, u % 3, u // 3))
    last_b(Step(UNITS, UNITS % 3, UNITS // 3))


def ffn_attention(core, keep, w, c, buffers, tag):
    nc = core.nc
    HALF = SEQ // 2
    HT = BT // 2
    PIECE = [(h, i, a, min(a + HALF, (i + 1) * P)) for tiles in (range(HT, BT), range(HT))
             for i in tiles for h in range(GH) for a in range(0, (i + 1) * P, HALF)]
    LATE = sum(i >= HT for h, i, a, b in PIECE)
    GROUP = [(j, max(j * P, HALF), SEQ) for j in (0, 7, 1, 6, 2, 5, 3, 4)]
    GROUP += [(j, j * P, HALF) for j in (0, 3, 1, 2)]
    LATE_G = BT
    DIAG = [j * P == a for j, a, e in GROUP]
    NDIAG = GH * sum(DIAG)
    NG, NCH = len(GROUP), GH * len(GROUP)
    MAX_LO, MAX_HI, CTX_HI, CTX_LO = "max_lo", "max_hi", "ctx_hi", "ctx_lo"

    def events(first, contexts):
        order = list(range(len(PIECE)))
        order.insert(LATE + 6, MAX_HI)
        if contexts:
            order[12:12] = [CTX_HI, CTX_LO]
        if not first:
            order.insert(7, MAX_LO)
        return order

    ORDER = (events(True, False), events(False, False), events(False, True))
    FINAL = [MAX_LO, CTX_HI, CTX_LO]
    NEV = len(ORDER[2])
    LINKS_LO, LINKS_HI, LINKS_CTX = 3, 4, 2
    NA, NB = 3, 3
    LEAD = 0.6
    NW, LAG = 3, 2
    NLINK = LINKS_LO + LINKS_HI + LINKS_CTX
    with ExitStack() as ctx:
        sb = lambda n, s, dt=F32: core.sb(ctx, n + tag, s, dt)
        ps = lambda n, s, dt=F32: core.ps(ctx, n + tag, s, dt)
        sem = lambda n: core.sem(ctx, n + tag)
        qa, ka, va, qk_loaded = (buffers[n] for n in ("qa", "ka", "va", "qk_loaded"))
        mx = [sb(f"mx{i}", [P, BT, GH]) for i in range(2)]
        top, rest = sb("top", [P, BT, GH]), sb("rest", [P, BT, GH])
        mparts = sb("mparts", [P, BT, GH, 3], BF16)
        mT = sb("mT", [3 * GH, SEQ], BF16)
        wt = [[sb(f"wt{i}{h}", [P, HALF]) for h in range(GH)] for i in range(NW)]
        cT = sb("cT", [P, SEQ])
        rden = sb("rden", [P, BT, GH])
        pA = [ps(f"pA{i}", [P, HALF]) for i in range(NA)]
        pB = [ps(f"pB{i}", [P, HALF]) for i in range(NB)]
        pC = ps("pC", [P, SEQ])
        v_staged = [sem(f"v_staged{i}") for i in range(3)]
        hi_loaded = [sem(f"max_hi_loaded{i}") for i in range(3)]
        lo_loaded = [sem(f"max_lo_loaded{i}") for i in range(3)]
        a_done, a_used, mparts_ready = sem("a_done"), sem("a_used"), sem("mparts_ready")
        st_done, exp_done, masked, pv_done, cT_ready = (sem("st_done"), sem("exp_done"), sem("masked"),
                                                        sem("pv_done"), sem("cT_ready"))
        dve = sem("dve_a")

        def fixed(s, upto):
            return isinstance(s.u, int) and s.u <= upto

        def order(s):
            if fixed(s, UNITS) and s.u == UNITS:
                return FINAL + [CTX_HI, CTX_LO]
            return ORDER[s.u] if fixed(s, 1) else ORDER[2]

        def before(s):
            if fixed(s, 1):
                return s.u * len(ORDER[0])
            return s.u * NEV + (len(ORDER[0]) + len(ORDER[1]) - 2 * NEV)

        def event(s, n):
            return before(s) + n

        def slot(s, n):
            u = s.u if isinstance(s.u, int) else s.stage + 3
            return pA[(before(Step(u, 0, 0)) + n) % NA]

        def links(s):
            if fixed(s, 1):
                return s.u * LINKS_HI
            return s.u * NLINK + (2 * LINKS_HI + LINKS_LO - 2 * NLINK)

        with nc.Block() as block:
            @block.sync
            def _(sp):
                def max_rows(s, n, stage, loaded, a):
                    sp.wait_ge(a_used, event(s, n) + 1)
                    for h in range(GH):
                        sp.dma_start(qa[stage][MROW:P, h, a:a + HALF],
                                     mT[3 * h:3 * h + 3, a:a + HALF]).then_inc(loaded[stage], 16)

                def rows(s):
                    for n, e in enumerate(order(s)):
                        if e == MAX_LO:
                            max_rows(s, n, s.shift(-1).stage, lo_loaded, 0)
                        if e == MAX_HI:
                            max_rows(s, n, s.stage, hi_loaded, HALF)

                def step(s):
                    rows(s)
                    if not isinstance(s.u, int) or s.u + 2 < UNITS:
                        sp.wait_ge(pv_done, s.u * NCH)
                        load_qk(sp, w, buffers, s.shift(2).stage, s.u + 2)

                attention_steps(sp, step, rows, rows)

            @block.tensor
            def _(pe):
                def piece(s, n, e):
                    h, i, a, b = PIECE[e]
                    if e == 0:
                        pe.wait_ge(qk_loaded[s.stage], s.fills * 32 * TERMS + 32 * TERMS)
                    reached(pe, a_used, event(s, n) - (NA - 1))
                    pe.matmul(slot(s, n)[:, 0:b - a], qa[s.stage][0:MROW, h, i * P:(i + 1) * P],
                              ka[s.stage][0:MROW, h, a:b], start=True, stop=True).then_inc(a_done, 1)

                def maxima(s, n, half, count):
                    pe.wait_ge(mparts_ready, count)
                    reached(pe, a_used, event(s, n) - (NA - 1))
                    rows = slot(s, n)[0:3 * GH, 0:HALF // 2].bitcast(BF16)
                    for i in range(HT):
                        last = pe.transpose(rows[:, i * P:(i + 1) * P],
                                            mparts[:, half * HT + i, :, :].rearrange("p h s -> p (h s)"),
                                            c["ident_b"][:, :])
                    last.then_inc(a_done, 1)

                def context(s, n, half, back):
                    pe.wait_ge(cT_ready, s.u * 2 - (2 * back - 2 + half))
                    reached(pe, a_used, event(s, n) - (NA - 1))
                    for i in range(HT):
                        at = (half * HT + i) * P
                        last = pe.transpose(slot(s, n)[:, i * P:(i + 1) * P], cT[:, at:at + P], c["ident"][:, :])
                    last.then_inc(a_done, 1)

                def run(s, n, back=2):
                    e = order(s)[n]
                    if e == MAX_LO:
                        maxima(s, n, 0, s.u * 2)
                    elif e == MAX_HI:
                        maxima(s, n, 1, s.u * 2 + 1)
                    elif e in (CTX_HI, CTX_LO):
                        context(s, n, int(e == CTX_HI), back)
                    else:
                        piece(s, n, e)

                def scores(s, g, h):
                    j, a, e = GROUP[g]
                    v = s.shift(-1)
                    if h == 0 and g in (0, LATE_G):
                        pe.wait_ge((lo_loaded if g else hi_loaded)[v.stage], v.fills * 16 * GH + 16 * GH)
                    reached(pe, exp_done, v.u * NCH + (g * GH + h - (NB - 1)))
                    pe.matmul(pB[(g * GH + h) % NB][:, 0:e - a], ka[v.stage][0:P, h, j * P:(j + 1) * P],
                              qa[v.stage][0:P, h, a:e], start=True, stop=True).then_inc(st_done, 1)

                def products(s, g):
                    j, a, e = GROUP[g]
                    v = s.shift(-1)
                    if g == 0:
                        pe.wait_ge(v_staged[v.stage], v.fills + 1)
                    if g in (0, LATE_G):
                        reached(pe, cT_ready, v.u * 2 - (0 if g else 1))
                    for h in range(GH):
                        if DIAG[g]:
                            pe.wait_ge(masked, v.u * NDIAG + (GH * sum(DIAG[:g]) + h + 1))
                        else:
                            pe.wait_ge(exp_done, v.u * NCH + (g * GH + h + 1))
                        pe.matmul(pC[32 * h:32 * h + 32, a:e], va[v.stage][:, j, h, :], wt[g % NW][h][:, 0:e - a],
                                  start=g in (0, LATE_G), stop=g in (LATE_G - 1, NG - 1)).then_inc(pv_done, 1)

                def first(s):
                    for n in range(len(order(s))):
                        run(s, n)

                def step(s, count=None):
                    count = count or len(order(s))
                    share = [PIECE[e][3] - PIECE[e][2] if isinstance(e, int) else HALF // 2 for e in order(s)[:count]]
                    total = 2 * sum(e - a for j, a, e in GROUP)
                    passed = n = 0
                    for g, (j, a, e) in enumerate(GROUP):
                        behind = GROUP[g - LAG][2] - GROUP[g - LAG][1] if g >= LAG else 0
                        for h in range(GH):
                            scores(s, g, h)
                            passed += (e - a) / GH + (behind * LEAD if h == GH - 1 else 0)
                            while n < count and sum(share[:n + 1]) <= sum(share) * passed / total:
                                run(s, n)
                                n += 1
                        if g >= LAG:
                            products(s, g - LAG)
                            passed += behind * (1 - LEAD)
                    for g in range(NG - LAG, NG):
                        passed += GROUP[g][2] - GROUP[g][1]
                        while n < count and sum(share[:n + 1]) <= sum(share) * passed / total:
                            run(s, n)
                            n += 1
                        products(s, g)

                def last_b(s):
                    step(s, len(FINAL))
                    for n in range(len(FINAL), len(order(s))):
                        run(s, n, 1)

                attention_steps(pe, step, last_b, first)

            @block.vector
            def _(vec):
                def split(s, half, k, n):
                    t = slice(half * HT, (half + 1) * HT)
                    src = top if half else mx[0]
                    if half == 0:
                        k += 1
                    first = k == (0 if half else 1)
                    if not first:
                        vec.wait_ge(dve, links(s) + n)
                    parts = [mparts[:, t, :, r] for r in range(3)]
                    if k == 0:
                        ins = vec.tensor_tensor(top[:, t, :], mx[0][:, t, :], mx[1][:, t, :], ALU.max)
                    elif k == 1:
                        ins = vec.tensor_copy(parts[0], src[:, t, :])
                    elif k == 2:
                        ins = vec.tensor_tensor(rest[:, t, :], src[:, t, :], parts[0], ALU.subtract)
                    elif k == 3:
                        ins = vec.tensor_copy(parts[1], rest[:, t, :])
                    else:
                        ins = vec.tensor_tensor(parts[2], rest[:, t, :], parts[1], ALU.subtract)
                    ins.then_inc(mparts_ready if k == 4 else dve, 1)

                def copy_maxima(s, n, half, unit, loaded):
                    vec.wait_ge(a_done, event(s, n) + 1)
                    if unit.fills is not None:
                        vec.wait_ge(loaded[unit.stage], unit.fills * 16 * GH + 16 * GH)
                    vec.tensor_copy(mT[:, half * HALF:(half + 1) * HALF],
                                    slot(s, n)[0:3 * GH, 0:HALF // 2].bitcast(BF16)).then_inc(a_used, 1)

                def context(s, n, half, link, back=2):
                    vec.wait_ge(a_done, event(s, n) + 1)
                    rows = slot(s, n)[:, :].rearrange("p (t h r) -> p t h r", t=HT, h=GH)
                    den = rden[:, half * HT:(half + 1) * HT, :]
                    vec.reciprocal(den, rows[:, :, :, HD]).then_inc(dve, 1)
                    vec.wait_ge(dve, links(s) + link)
                    size = HT * GH * HD
                    vec.tensor_tensor(keep["ctx"][:, bass.ds((s.u - back) * (2 * size) + half * size, size)]
                                      .rearrange("p (t h r) -> p t h r", t=HT, h=GH),
                                      rows[:, :, :, 0:HD], den.unsqueeze(3).to_broadcast([P, HT, GH, HD]),
                                      ALU.mult).then_inc(a_used, 1)

                def step(s):
                    n_lo = 0 if fixed(s, 0) else LINKS_LO
                    n_ctx = 0 if fixed(s, 1) else LINKS_CTX
                    for n, e in enumerate(order(s)):
                        if e == MAX_LO:
                            copy_maxima(s, n, 0, before_unit(s, 2), lo_loaded)
                        elif e == MAX_HI:
                            copy_maxima(s, n, 1, before_unit(s, 1), hi_loaded)
                        elif e == CTX_HI:
                            context(s, n, 1, n_lo + 1)
                        elif e == CTX_LO:
                            context(s, n, 0, n_lo + 2)
                        else:
                            h, i, a, b = PIECE[e]
                            size = b - a
                            mask = c["causal"][:, SEQ - size:] if b == (i + 1) * P else c["causal"][:, 0:size]
                            apart(vec, a_done, event(s, n) + 1)
                            vec.tensor_tensor_reduce(out=slot(s, n)[:, 0:size], in0=slot(s, n)[:, 0:size], in1=mask,
                                                     scale=1.0, scalar=LOWEST, op0=ALU.add, op1=ALU.max,
                                                     accum_out=mx[a // HALF][:, i, h:h + 1]).then_inc(a_used, 1)
                            if 0 <= e <= 3 and n_lo:
                                if e == 0:
                                    vec.wait_ge(a_used, before(s))
                                split(s, 0, e, e)
                            if LATE <= e <= LATE + 4:
                                if e == LATE:
                                    vec.wait_ge(a_used, event(s, n))
                                split(s, 1, e - LATE, n_lo + n_ctx + e - LATE)

                def before_unit(s, back):
                    if isinstance(s.u, int) and s.u < back:
                        return Step(0, 0, None)
                    return s.shift(-back)

                def last(s):
                    vec.wait_ge(a_used, before(s))
                    for k in range(4):
                        split(s, 0, k, k)
                    copy_maxima(s, 0, 0, s.shift(-2), lo_loaded)
                    context(s, 1, 1, LINKS_LO + 1)
                    context(s, 2, 0, LINKS_LO + 2)
                    vec.wait_ge(a_used, event(s, 3))
                    context(s, 3, 1, LINKS_LO + 3, 1)
                    context(s, 4, 0, LINKS_LO + 4, 1)

                attention_steps(vec, step, last, step)

            @block.scalar
            def _(act):
                def copy_context(half):
                    at = half * HALF
                    act.copy(cT[:, at:at + HALF], pC[:, at:at + HALF]).then_inc(cT_ready, 1)

                def weights(s):
                    v = s.shift(-1)
                    for g, (j, a, e) in enumerate(GROUP):
                        for h in range(GH):
                            act.wait_ge(st_done, v.u * NCH + (g * GH + h + 1))
                            reached(act, pv_done, v.u * NCH + ((g - NW) * GH + h + 1))
                            act.activation(wt[g % NW][h][:, 0:e - a], pB[(g * GH + h) % NB][:, 0:e - a], ACT.Exp).then_inc(exp_done, 1)
                        if g == 1 and not fixed(s, 1):
                            act.wait_ge(pv_done, v.u * NCH)
                            if not fixed(s, 2):
                                act.wait_ge(a_done, before(s) - (NEV - ORDER[2].index(CTX_LO) - 1))
                            copy_context(0)
                        if g == LATE_G + LAG:
                            act.wait_ge(pv_done, v.u * NCH + LATE_G * GH)
                            if not fixed(s, 1):
                                act.wait_ge(a_done, event(s, order(s).index(CTX_HI)) + 1)
                            copy_context(1)

                def last_weights(s):
                    weights(s)
                    act.wait_ge(pv_done, s.u * NCH)
                    act.wait_ge(a_done, event(s, len(FINAL)))
                    copy_context(0)

                attention_steps(act, weights, last_weights, lambda s: None)

            @block.gpsimd
            def _(pool):
                size = BT * GH * HD

                def stage(s):
                    pool.tensor_copy(va[s.stage][:, :, :, 0:HD],
                                     keep["v"][:, bass.ds(s.u * size, size)]
                                     .rearrange("p (t h r) -> p t h r", t=BT, h=GH)).then_inc(v_staged[s.stage], 1)

                def first(s):
                    for d in range(3):
                        stage(s.shift(d))

                def mask(s):
                    v = s.shift(-1)
                    for g in range(NG):
                        for h in range(GH if DIAG[g] else 0):
                            apart(pool, exp_done, v.u * NCH + (g * GH + h + 1))
                            block_ = wt[g % NW][h][:, 0:P]
                            pool.affine_select(out=block_, in_=block_, compare_op=ALU.is_ge, fill=0.0, base=0,
                                               pattern=[[1, P]], channel_multiplier=-1).then_inc(masked, 1)

                def step(s):
                    mask(s)
                    if not isinstance(s.u, int) or s.u + 2 < UNITS:
                        apart(pool, pv_done, s.u * NCH)
                        stage(s.shift(2))

                attention_steps(pool, step, mask, first)


def ffn_output(core, keep, w, c, tag):
    nc = core.nc
    with ExitStack() as ctx:
        sb = lambda n, s, dt=F32: core.sb(ctx, n + tag, s, dt)
        ps = lambda n, s, dt=F32: core.ps(ctx, n + tag, s, dt)
        sem = lambda n: core.sem(ctx, n + tag)
        rows, cT = sb("ctx_rows", [P, BCOL]), sb("ctxT", [P, SEQ])
        stats, mv = sb("stats_o", [P, BT, 6]), sb("mv_o", [P, BT, 2])
        std, rstd = sb("std_o", [P, BT]), sb("rstd_o", [P, BT])
        xn, xnT = sb("xn_o", [P, BCOL]), sb("xnT_o", [P, SEQ])
        pT, pO, pX, pL = ps("pT_o", [P, SEQ]), ps("pO", [P, BCOL]), ps("pX_o", [P, SEQ]), ps("pL", [P, BT * E])
        (rows_ready, bias_added, cT_done, cT_ready, o_done, o_used, var_ready, std_ready, xn_ready, xn_kept, xT_done,
         xT_ready, l_done, l_kept, dve, pool_chain) = (sem(n) for n in (
             "rows_ready", "bias_added", "octx_T_done", "octx_T_ready", "o_done", "o_used", "var_o", "std_rdy_o",
             "xn_ready_o", "xn_kept", "oxn_T_done", "oxn_T_ready", "l_done", "l_kept", "dve_o", "pool_o"))

        def staggered(eng, before, after):
            before(0)
            before(1)
            after(0)
            with eng.Fori(1, BATCH - 1) as b:
                before(b + 1)
                after(b)
            after(BATCH - 1)

        with nc.Block() as block:
            @block.gpsimd
            def _(pool):
                def before(b):
                    hidden = keep["hid"][:, bass.ds(b * BCOL, BCOL)].rearrange("p (t d) -> p t d", d=D)
                    pool.tensor_tensor(hidden, hidden, c["L0_ffn_o_b"][:, :].unsqueeze(1).to_broadcast([P, BT, D]),
                                       ALU.add).then_inc(bias_added, 1)

                def after(b):
                    xt = keep["xt"][:, bass.ds(b * BT * ROW, BT * ROW)].rearrange("p (t c) -> p t c", c=ROW)[:, :, 0:D]
                    apart(pool, xn_ready, b + 1)
                    pool.tensor_tensor(xt, xn[:, :].rearrange("p (t d) -> p t d", d=D),
                                       c["L0_ffn_ln2_w"][:, :].unsqueeze(1).to_broadcast([P, BT, D]),
                                       ALU.mult).then_inc(xn_kept, 1)
                    apart(pool, xn_kept, b + 1)
                    pool.tensor_tensor(xt, xt, c["L0_ffn_ln2_b"][:, :].unsqueeze(1).to_broadcast([P, BT, D]), ALU.add)

                staggered(pool, before, after)

            @block.tensor
            def _(pe):
                def project(b):
                    pe.wait_ge(rows_ready, b + 1)
                    for t in range(BT):
                        last = pe.transpose(pT[:, t * P:(t + 1) * P], rows[:, t * D:(t + 1) * D], c["ident"][:, :])
                    last.then_inc(cT_done, 1)
                    pe.wait_ge(cT_ready, b + 1)
                    reached(pe, o_used, b)
                    for t in range(BT):
                        last = pe.matmul(pO[:, t * D:(t + 1) * D], cT[:, t * P:(t + 1) * P], c["L0_ffn_o_w"][:, :],
                                         start=True, stop=True)
                    last.then_inc(o_done, 1)

                def logits(b):
                    pe.wait_ge(xn_ready, b + 1)
                    for t in range(BT):
                        last = pe.transpose(pX[:, t * P:(t + 1) * P], xn[:, t * D:(t + 1) * D], c["ident"][:, :])
                    last.then_inc(xT_done, 1)
                    pe.wait_ge(xT_ready, b + 1)
                    reached(pe, l_kept, b)
                    for t in range(BT):
                        last = pe.matmul(pL[:, t * E:(t + 1) * E], xnT[:, t * P:(t + 1) * P], c["router"][:, :],
                                         start=True, stop=True)
                    last.then_inc(l_done, 1)

                staggered(pe, project, logits)

            @block.scalar
            def _(act):
                def side_by_side(b):
                    reached(act, cT_done, b)
                    act.copy(rows[:, :].rearrange("p (t g r) -> p g t r", t=BT, g=GROUPS),
                             keep["ctx"][:, bass.ds(b * BCOL, BCOL)]
                             .rearrange("p (g t r) -> p g t r", g=GROUPS, t=BT)).then_inc(rows_ready, 1)

                def transposed(b):
                    act.wait_ge(cT_done, b + 1)
                    reached(act, o_done, b)
                    act.copy(cT[:, :], pT[:, :]).then_inc(cT_ready, 1)

                def batch(b, more=True):
                    if more:
                        side_by_side(b + 1)
                    act.wait_ge(var_ready, b + 1)
                    act.activation(std[:, :], mv[:, :, 1], ACT.Sqrt, bias=c["eps"][:, 0:1]).then_inc(std_ready, 1)
                    if more:
                        transposed(b + 1)
                    act.wait_ge(xT_done, b + 1)
                    reached(act, l_done, b)
                    act.activation(xnT[:, :], pX[:, :], ACT.Identity, bias=c["ln2_b"][:, 0:1],
                                   scale=c["ln2_w"][:, 0:1]).then_inc(xT_ready, 1)
                    act.wait_ge(l_done, b + 1)
                    act.copy(keep["logits"][:, bass.ds(b * BT * E, BT * E)], pL[:, :]).then_inc(l_kept, 1)

                side_by_side(0)
                transposed(0)
                batch(0)
                with act.Fori(1, BATCH - 1) as b:
                    batch(b)
                batch(BATCH - 1, more=False)

            @block.vector
            def _(vec):
                chain = Chain(vec, dve)
                link = chain.link

                def batch(b):
                    hidden = keep["hid"][:, bass.ds(b * BCOL, BCOL)]
                    vec.wait_ge(bias_added, b + 1)
                    vec.wait_ge(o_done, b + 1)
                    vec.tensor_tensor(hidden, hidden, pO[:, :], ALU.add).then_inc(o_used, 1)
                    apart(vec, o_used, b + 1)
                    for t in range(BT):
                        last = vec.bn_stats(stats[:, t, :], hidden[:, t * D:(t + 1) * D])
                    link(last)
                    for t in range(BT):
                        last = vec.bn_aggr(mv[:, t, :], stats[:, t, :])
                    last.then_inc(var_ready, 1)
                    vec.wait_ge(std_ready, b + 1)
                    link(vec.reciprocal(rstd[:, :], std[:, :]))
                    reached(vec, xT_done, b)
                    reached(vec, xn_kept, b)
                    normalise(vec, link, xn[:, :], hidden, mv, rstd)
                    vec.sem_inc(xn_ready, 1)

                batch(0)
                for b in chain.each(BATCH - 1, 3, first=1):
                    batch(b)


def ffn_route(core, keep, w, c, tag):
    nc = core.nc
    with ExitStack() as ctx:
        sb = lambda n, s, dt=F32: core.sb(ctx, n + tag, s, dt)
        sem = lambda n: core.sem(ctx, n + tag)
        G = [P, TILES, E]
        prob, logit2, work, one = sb("prob", G), sb("logit2", G), sb("work_r", G), [sb("top1", G), sb("top2", G)]
        kept, loc = [sb("kept1", G), sb("kept2", G)], [sb("loc1", G), sb("loc2", G)]
        tot, run = [sb("tot1", [P, E, TILES]), sb("tot2", [P, E, TILES])], [sb("run1", [P, E, TILES]), sb("run2", [P, E, TILES])]
        best, first, total, recip = (sb(n, [P, TILES]) for n in ("best", "first", "total", "recip"))
        gate, at, dropped = (sb("gate", [P, 2, TILES]), sb("at", [P, 2, TILES]), sb("dropped", [P, TILES]))
        place = sb("place", [P, 2, TILES])
        pCum = [core.ps(ctx, f"pCum{i}{tag}", [P, TILES * E]) for i in range(2)]
        pTot = [core.ps(ctx, f"pTot{i}{tag}", [P, TILES * E]) for i in range(2)]
        max_found, exps_ready, one_ready, counted, dve = (sem("max_found"), sem("exps_ready"), sem("one_ready"),
                                                          sem("counted"), sem("dve_r"))
        send_ready, sent, number_set = sem("send_ready"), sem("sent"), sem("number_set")
        used, inside = sb("used", [P, E]), sb("inside", [P, E, CC])
        over_e = lambda v: v.unsqueeze(2).to_broadcast(G)
        over_t = lambda v: v.unsqueeze(1).to_broadcast(G)
        L = keep["logits"][:, :].rearrange("p (t e) -> p t e", e=E)
        with nc.Block() as block:
            @block.vector
            def _(vec):
                link = Chain(vec, dve).link

                def top(values, n):
                    link(vec.reduce_max(best[:, :], values, AX))
                    link(vec.tensor_tensor(work[:, :, :], values, over_e(best[:, :]), ALU.is_equal))
                    link(vec.tensor_tensor(work[:, :, :], work[:, :, :], over_t(c["rev"][:, :]), ALU.mult))
                    link(vec.reduce_max(first[:, :], work[:, :, :], AX))
                    vec.tensor_tensor(one[n][:, :, :], over_t(c["rev"][:, :]), over_e(first[:, :]),
                                      ALU.is_equal).then_inc(one_ready, 1)
                    vec.wait_ge(one_ready, n + 1)

                link(vec.reduce_max(best[:, :], L, AX))
                vec.tensor_tensor(work[:, :, :], L, over_e(best[:, :]), ALU.subtract).then_inc(max_found, 1)
                vec.wait_ge(exps_ready, 1)
                link(vec.reduce_sum(total[:, :], prob[:, :, :], AX))
                link(vec.reciprocal(recip[:, :], total[:, :]))
                link(vec.tensor_tensor(prob[:, :, :], prob[:, :, :], over_e(recip[:, :]), ALU.mult))
                top(prob[:, :, :], 0)
                for n in range(2):
                    if n == 1:
                        link(vec.scalar_tensor_tensor(logit2[:, :, :], one[0][:, :, :], LOWEST, L, ALU.mult, ALU.add))
                        top(logit2[:, :, :], 1)
                    vec.wait_ge(counted, n + 1)
                    link(vec.tensor_copy(tot[n][:, :, :], pTot[n][:, :].rearrange("p (t e) -> p e t", e=E)))
                    link(vec.tensor_tensor_scan(run[n][:, :, :].rearrange("p e t -> p (e t)"),
                                                c["restart"][:, :, :].rearrange("p e t -> p (e t)"),
                                                tot[n][:, :, :].rearrange("p e t -> p (e t)"), 0.0, ALU.mult, ALU.add))
                    link(vec.tensor_tensor(tot[n][:, :, :], run[n][:, :, :], tot[n][:, :, :], ALU.subtract))
                    link(vec.scalar_tensor_tensor(loc[n][:, :, :], pCum[n][:, :].rearrange("p (t e) -> p t e", e=E), -1.0,
                                                  tot[n][:, :, :].rearrange("p e t -> p t e"), ALU.add, ALU.add))
                    if n == 1:
                        link(vec.tensor_tensor(loc[1][:, :, :], loc[1][:, :, :], over_t(run[0][:, :, TILES - 1]), ALU.add))
                    link(vec.scalar_tensor_tensor(kept[n][:, :, :], loc[n][:, :, :], float(CAP), one[n][:, :, :],
                                                  ALU.is_lt, ALU.mult))
                    link(vec.tensor_tensor(work[:, :, :], prob[:, :, :], kept[n][:, :, :], ALU.mult))
                    link(vec.reduce_sum(gate[:, n, :], work[:, :, :], AX))
                    link(vec.scalar_tensor_tensor(loc[n][:, :, :], over_t(c["num"][:, :]), float(CAP), loc[n][:, :, :],
                                                  ALU.mult, ALU.add))
                    link(vec.tensor_tensor(work[:, :, :], loc[n][:, :, :], kept[n][:, :, :], ALU.mult))
                    link(vec.reduce_sum(at[:, n, :], work[:, :, :], AX))
                    link(vec.reduce_sum(dropped[:, :], kept[n][:, :, :], AX))
                    link(vec.tensor_scalar(dropped[:, :], dropped[:, :], -1.0, 1.0, ALU.mult, ALU.add))
                    link(vec.scalar_tensor_tensor(place[:, n, :], c["spill"][:, :], float(n * TOK), dropped[:, :],
                                                  ALU.add, ALU.mult))
                    link(vec.tensor_tensor(place[:, n, :], place[:, n, :], at[:, n, :], ALU.add))
                    vec.tensor_copy(keep["send"][:, n, :], place[:, n, :]).then_inc(send_ready, 1)
                link(vec.tensor_tensor(total[:, :], gate[:, 0, :], gate[:, 1, :], ALU.add))
                link(vec.tensor_scalar(total[:, :], total[:, :], F32_EPS, None, ALU.max))
                link(vec.reciprocal(recip[:, :], total[:, :]))
                link(vec.tensor_tensor(gate[:, :, :], gate[:, :, :],
                                       recip[:, :].unsqueeze(1).to_broadcast([P, 2, TILES]), ALU.mult))
                vec.tensor_scalar(keep["gate"][:, :, :], gate[:, :, :], 0.5, None, ALU.mult)
                link(vec.tensor_tensor(used[:, :], run[0][:, :, TILES - 1], run[1][:, :, TILES - 1], ALU.add))
                link(vec.tensor_tensor(keep["filled"][:, :, :], c["slot"][:, :].unsqueeze(1).to_broadcast([P, E, CC]),
                                       used[:, :].unsqueeze(2).to_broadcast([P, E, CC]), ALU.is_lt))
                link(vec.tensor_tensor(inside[:, :, :], keep["filled"][:, :, :], c["unused"][:, :, :], ALU.mult))
                vec.tensor_tensor(keep["away"][:, :, :], c["unused"][:, :, :], inside[:, :, :], ALU.subtract)

            @block.gpsimd
            def _(pool):
                rows = keep["xt"][:, :].rearrange("p (t c) -> p t c", c=ROW)
                pool.wait_ge(c["wiped"], 16 * WIPES)
                for n in range(2):
                    if n == 1:
                        pool.wait_ge(sent, 16 * TILES)
                    pool.iota(rows[:, :, D:ROW].rearrange("p t o -> p (t o)").bitcast(U32), pattern=[[P, TILES]],
                              base=n * TOK, channel_multiplier=1).then_inc(number_set, 1)
                    pool.wait_ge(number_set, n + 1)
                    pool.wait_ge(send_ready, n + 1)
                    for t in range(TILES):
                        pool.indirect_dma_start(
                            out=w["xin"], out_offset=bass.IndirectOffsetOnAxis(ap=keep["send"][:, n, t:t + 1], axis=0),
                            in_=rows[:, t, :], in_offset=None).then_inc(sent, 16)
                pool.wait_ge(sent, 16 * 2 * TILES)

            @block.scalar
            def _(act):
                act.wait_ge(max_found, 1)
                act.activation(prob[:, :, :], work[:, :, :], ACT.Exp).then_inc(exps_ready, 1)

            @block.tensor
            def _(pe):
                for n in range(2):
                    pe.wait_ge(one_ready, n + 1)
                    flat = one[n][:, :, :].rearrange("p t e -> p (t e)")
                    pe.matmul(pCum[n][:, :], c["upper"][:, :], flat, start=True, stop=True)
                    pe.matmul(pTot[n][:, :], c["ones"][:, :], flat, start=True, stop=True).then_inc(counted, 1)


def ffn_experts(core, keep, w, c, x_out, tag):
    nc = core.nc
    with ExitStack() as ctx:
        sb = lambda n, s, dt=F32: core.sb(ctx, n + tag, s, dt)
        ps = lambda n, s, dt=F32: core.ps(ctx, n + tag, s, dt)
        sem = lambda n: core.sem(ctx, n + tag)
        two = range(2)
        xi = [sb(f"xi{i}", [P, CC, ROW]) for i in two]
        number, dest = [sb(f"number{i}", [P, CC]) for i in two], [sb(f"dest{i}", [P, CC], U32) for i in two]
        w1 = [sb(f"w1_{i}", [P, F]) for i in two]
        w2 = [sb(f"w2_{i}", [P, FC, D]) for i in two]
        b1 = [sb(f"b1_{i}", [P, FC]) for i in two]
        b2 = [sb(f"b2_{i}", [P, D]) for i in two]
        b2s = [sb(f"b2s_{i}", [P, D]) for i in two]
        xiT = sb("xiT", [P, CAP])
        hT = [sb(f"hT{i}", [P, CAP]) for i in range(FC)]
        eo = [sb(f"eo{i}", [P, CC, D]) for i in two]
        pX = ps("pXi", [P, CAP])
        pH = [ps(f"pH{i}", [P, CAP]) for i in range(FC)]
        pO = [ps(f"pOe{i}", [P, CC, D]) for i in two]
        x_loaded = [sem(f"xi_loaded{i}") for i in two]
        w_loaded = [sem(f"we_loaded{i}") for i in two]
        xT_done, xT_ready, h_done, h_ready, o_done, o_ready, b_ready = (
            sem(n) for n in ("xiT_done", "xiT_ready", "h_done", "h_ready", "oe_done", "oe_ready", "b2s_ready"))
        stored = [sem(f"eo_stored{i}") for i in two]
        dest_chain, dest_ready = sem("dest_chain"), sem("dest_ready")
        xin = w["xin"][0:SLOTS, :].rearrange("(e p c) d -> e p c d", p=P, c=CC)
        with nc.Block() as block:
            def experts(eng, one_expert):
                for n in two:
                    one_expert(n, n, 0)
                with eng.Fori(1, E // 2 - 1) as turn:
                    for n in two:
                        one_expert(turn * 2 + n, n, turn)
                for n in two:
                    one_expert(E - 2 + n, n, E // 2 - 1)

            def beyond(e):
                return not isinstance(e, int) or e >= 2

            @block.sync
            def _(sp):
                def load(e, n, turn):
                    one = bass.ds(e, 1)
                    if beyond(e):
                        sp.wait_ge(xT_done, e - 1)
                        sp.wait_ge(dest_ready, e - 1)
                    sp.dma_start(xi[n][:, :, :], xin[one].rearrange("o p c d -> (o p) c d")).then_inc(x_loaded[n], 16)
                    if beyond(e):
                        sp.wait_ge(h_done, (e - 1) * FC)
                    sp.dma_start(w1[n][:, :], w["L0_ffn_fc1_w"][one].rearrange("o d f -> (o d) f")).then_inc(w_loaded[n], 16)
                    if beyond(e):
                        sp.wait_ge(h_ready, (e - 1) * FC)
                    sp.dma_start(b1[n][:, :], w["L0_ffn_fc1_b"][one].rearrange("o (p c) -> (o p) c", c=FC)
                                 ).then_inc(w_loaded[n], 16)
                    if beyond(e):
                        sp.wait_ge(b_ready, e - 1)
                    sp.dma_start(b2[n][:, :], w["L0_ffn_fc2_b"][one].rearrange("o d -> (o d)").partition_broadcast(P)
                                 ).then_inc(w_loaded[n], 16)
                    if beyond(e):
                        sp.wait_ge(o_done, e - 1)
                    sp.dma_start(w2[n][:, :, :], w["L0_ffn_fc2_w"][one].rearrange("o (p c) d -> (o p) c d", c=FC)
                                 ).then_inc(w_loaded[n], 16)

                experts(sp, load)

            @block.tensor
            def _(pe):
                def transposes(e, n, turn):
                    pe.wait_ge(x_loaded[n], turn * 16 + 16)
                    for cc in range(CC):
                        last = pe.transpose(pX[:, cc * P:(cc + 1) * P], xi[n][:, cc, 0:D], c["ident"][:, :])
                    last.then_inc(xT_done, 1)

                def run(e, n, turn):
                    if isinstance(e, int) and e == 0:
                        transposes(0, 0, 0)
                    pe.wait_ge(w_loaded[n], turn * 64 + 64)
                    pe.wait_ge(xT_ready, e + 1)
                    cols = w1[n][:, :].rearrange("d (p c) -> d c p", c=FC)
                    for f in range(FC):
                        pe.matmul(pH[f][:, :], cols[:, f, :], xiT[:, :], start=True, stop=True).then_inc(h_done, 1)
                    if not isinstance(e, int) or e + 1 < E:
                        transposes(e + 1, 1 - n, turn + n)
                    pe.wait_ge(h_ready, e * FC + FC)
                    if beyond(e):
                        pe.wait_ge(o_ready, e - 1)
                    for cc in range(CC):
                        for f in range(FC):
                            last = pe.matmul(pO[n][:, cc, :], hT[f][:, cc * P:(cc + 1) * P], w2[n][:, f, :],
                                             start=f == 0, stop=f == FC - 1)
                    last.then_inc(o_done, 1)

                experts(pe, run)

            @block.scalar
            def _(act):
                def gelu(e, n, turn):
                    act.wait_ge(w_loaded[n], turn * 64 + 64)
                    for f in range(FC):
                        act.wait_ge(h_done, e * FC + (f + 1))
                        if f == 0:
                            reached(act, o_done, e)
                        act.activation(hT[f][:, :], pH[f][:, :], ACT.Gelu, bias=b1[n][:, f:f + 1]).then_inc(h_ready, 1)

                experts(act, gelu)

            @block.gpsimd
            def _(pool):
                def send(e, n, turn):
                    pool.wait_ge(dest_ready, e + 1)
                    apart(pool, o_ready, e + 1)
                    for cc in range(CC):
                        pool.indirect_dma_start(
                            out=w["y"], out_offset=bass.IndirectOffsetOnAxis(ap=dest[n][:, cc:cc + 1], axis=0),
                            in_=eo[n][:, cc, :], in_offset=None).then_inc(stored[n], 16)

                experts(pool, send)
                for n in two:
                    pool.wait_ge(stored[n], 16 * CC * (E // 2))

            @block.vector
            def _(vec):
                vec.scalar_tensor_tensor(keep["x"][:, :], keep["hid"][:, :], 0.5, keep["x"][:, :], ALU.mult, ALU.add)

                def link(e, k, ins):
                    ins.then_inc(dest_chain, 1)
                    apart(vec, dest_chain, e * 3 + k)

                def inputs(e, n, turn):
                    vec.wait_ge(xT_done, e + 1)
                    vec.tensor_copy(xiT[:, :], pX[:, :]).then_inc(xT_ready, 1)
                    at = bass.ds(e * CC, CC)
                    filled, away = (keep[name][:, :, :].rearrange("p e c -> p (e c)")[:, at] for name in ("filled", "away"))
                    vec.wait_ge(x_loaded[n], turn * 16 + 16)
                    if beyond(e):
                        vec.wait_ge(dest_ready, e - 1)
                    link(e, 1, vec.tensor_copy(number[n][:, :], xi[n][:, :, D:ROW].rearrange("p c o -> p (c o)").bitcast(U32)))
                    link(e, 2, vec.tensor_tensor(number[n][:, :], number[n][:, :], filled, ALU.mult))
                    link(e, 3, vec.tensor_tensor(number[n][:, :], number[n][:, :], away, ALU.add))
                    if beyond(e):
                        vec.wait_ge(stored[n], turn * 16 * CC)
                    vec.tensor_copy(dest[n][:, :], number[n][:, :]).then_inc(dest_ready, 1)

                def finish(e, n, turn):
                    if isinstance(e, int) and e == 0:
                        inputs(0, 0, 0)
                    if not isinstance(e, int) or e + 1 < E:
                        inputs(e + 1, 1 - n, turn + n)
                    vec.wait_ge(w_loaded[n], turn * 64 + 64)
                    vec.tensor_scalar(b2s[n][:, :], b2[n][:, :], 0.8, None, ALU.mult).then_inc(b_ready, 1)
                    vec.wait_ge(b_ready, e + 1)
                    vec.wait_ge(o_done, e + 1)
                    if beyond(e):
                        vec.wait_ge(stored[n], turn * 16 * CC)
                    vec.scalar_tensor_tensor(eo[n][:, :, :], pO[n][:, :, :], 0.8,
                                             b2s[n][:, :].unsqueeze(1).to_broadcast([P, CC, D]),
                                             ALU.mult, ALU.add).then_inc(o_ready, 1)

                experts(vec, finish)

    with ExitStack() as ctx:
        sb = lambda n, s, dt=F32: core.sb(ctx, n + tag, s, dt)
        sem = lambda n: core.sem(ctx, n + tag)
        got = [keep["ctx"], keep["xt"]]
        loaded = [sem(f"y_loaded{b}") for b in range(BATCH)]
        first_added, x_ready, x_stored = sem("first_added"), sem("x_ready"), sem("x_stored")
        x_rows = x_out.rearrange("(b t p) d -> b p t d", p=P, t=BT)
        y_rows = w["y"][0:2 * TOK].rearrange("(n b t p) d -> n b p t d", n=2, p=P, t=BT)
        cols = [slice(b * BCOL, (b + 1) * BCOL) for b in range(BATCH)]

        def load(eng, n):
            for b in range(BATCH):
                eng.dma_start(got[n][:, cols[b]].rearrange("p (t d) -> p t d", d=D), y_rows[n, b]).then_inc(loaded[b], 16)

        with nc.Block() as block:
            @block.scalar
            def _(act):
                load(act, 1)

            @block.vector
            def _(vec):
                for b in range(BATCH):
                    vec.wait_ge(loaded[b], 32)
                    for n in range(2):
                        for t in range(b * BT, (b + 1) * BT):
                            x_tile, y_tile = (a[:, t * D:(t + 1) * D] for a in (keep["x"], got[n]))
                            last = vec.scalar_tensor_tensor(x_tile, y_tile, keep["gate"][:, n, t:t + 1], x_tile,
                                                            ALU.mult, ALU.add)
                        last.then_inc(x_ready if n else first_added, 1)
                        if n == 0:
                            vec.wait_ge(first_added, b + 1)

            @block.sync
            def _(sp):
                load(sp, 0)
                for b in range(BATCH):
                    sp.wait_ge(x_ready, b + 1)
                    sp.dma_start(x_rows[b], keep["x"][:, cols[b]].rearrange("p (t d) -> p t d", d=D)
                                 ).then_inc(x_stored, 16)
                sp.wait_ge(x_stored, 16 * BATCH)


def ffn(core, w, c, x, x_out, tag, first_layer=True):
    with ExitStack() as ctx:
        keep = {n: core.sb(ctx, f"keep_{n}{tag}", [P, TILES * (ROW if n == "v" else D)]) for n in ("x", "hid", "v", "ctx")}
        keep["xt"] = keep["v"]
        keep["logits"] = core.sb(ctx, f"keep_logits{tag}", [P, TILES * E])
        keep["gate"] = core.sb(ctx, f"keep_gate{tag}", [P, 2, TILES])
        for n in ("filled", "away"):
            keep[n] = core.sb(ctx, f"keep_{n}{tag}", [P, E, CC])
        keep["send"] = core.sb(ctx, f"keep_send{tag}", [P, 2, TILES], U32)
        with ExitStack() as units:
            buffers = attention_buffers(core, units, tag)
            ffn_project(core, keep, w, c, buffers, x, tag, first_layer)
            ffn_attention(core, keep, w, c, buffers, tag)
        ffn_output(core, keep, w, c, tag)
        ffn_route(core, keep, w, c, tag)
        ffn_experts(core, keep, w, c, x_out, tag)


QKVB = 3 * D + H
SEG = TOK // P
SEGS = SEQ // SEG
R2 = 2 * HD
DFC = F // P
HT = BT // 2


def root_mean_square(vec, link, ms, mv):
    link(vec.tensor_tensor(ms[:, :], mv[:, :, 0], mv[:, :, 0], ALU.mult))
    return vec.tensor_tensor(ms[:, :], ms[:, :], mv[:, :, 1], ALU.add)


def delta_block(core, w, c, x_dram, x_out):
    nc = core.nc
    with ExitStack() as ctx:
        sb = lambda n, s, dt=F32: core.sb(ctx, "g_" + n, s, dt)
        sem = lambda n: core.sem(ctx, "g_" + n)
        x, hid = sb("x", [P, SEG * D]), sb("hid", [P, SEG * D])
        qkvb, kbeta = sb("qkvb", [P, SEG, QKVB]), sb("kbeta", [P, SEG, D])
        outs = sb("outs", [P, SEG, H, R2])
        wcat, bcat = sb("wcat", [P, QKVB]), sb("bcat", [P, QKVB])
        wo, w1, w2, b1 = sb("wo", [P, D]), sb("w1", [P, F]), sb("w2", [P, DFC, D]), sb("b1", [P, DFC])
        rows = {n: sb("row_" + n, [P, D]) for n in ("bo", "b2")}
        ln1_scale, ln2_scale = sb("ln1_scale", [P, 1]), sb("ln2_scale", [P, 1])
        w_loaded = sem("w_loaded")
        xs = x_dram.rearrange("(p j) d -> p (j d)", j=SEG)
        with ExitStack() as in1:
            sb1 = lambda n, s, dt=F32: core.sb(in1, "g1_" + n, s, dt)
            sem1 = lambda n: core.sem(in1, "g1_" + n)
            stats, mv, ms = sb1("stats", [P, BT, 6]), sb1("mv", [P, BT, 2]), sb1("ms", [P, BT])
            std, rstd = sb1("std", [P, BT]), sb1("rstd", [P, BT])
            h, hT = sb1("h", [P, BCOL]), sb1("hT", [P, BCOL])
            sq, norm = sb1("sq", [P, BT, D]), sb1("norm", [P, BT, H])
            nstd = sb1("nstd", [P, BT, H])
            pT = core.ps(in1, "g1_pT", [P, BCOL])
            pP = [core.ps(in1, f"g1_pP{i}", [P, 512]) for i in range(4)]
            x_loaded, stat_ready, std_ready, h_ready = sem1("x_loaded"), sem1("stat_ready"), sem1("std_ready"), sem1("h_ready")
            T_done, T_ready, p_done, p_used = sem1("T_done"), sem1("T_ready"), sem1("p_done"), sem1("p_used")
            dve, norm_ready, nstd_ready, beta_ready = (sem1(n) for n in ("dve", "norm_ready", "nstd_ready", "beta_ready"))
            with nc.Block() as block:
                @block.sync
                def _(sp):
                    def load(b):
                        sp.dma_start(x[:, bass.ds(b * BCOL, BCOL)], xs[:, bass.ds(b * BCOL, BCOL)]).then_inc(x_loaded, 16)

                    load(0)
                    at = 0
                    for n, width in (("q", D), ("k", D), ("v", D), ("beta", H)):
                        sp.dma_start(wcat[:, at:at + width], w["L0_attn_w" + n]).then_inc(w_loaded, 16)
                        sp.dma_start(bcat[:, at:at + width], w["L0_attn_b" + n].partition_broadcast(P)
                                     ).then_inc(w_loaded, 16)
                        at += width
                    for n in rows:
                        sp.dma_start(rows[n][:, :], w["L0_attn_" + n].partition_broadcast(P)).then_inc(w_loaded, 16)
                    for dst, n in ((ln1_scale, "ln1_scale"), (ln2_scale, "ln2_scale")):
                        sp.dma_start(dst[:, :], w["L0_attn_" + n].rearrange("(p o) -> p o", o=1)).then_inc(w_loaded, 16)
                    sp.dma_start(wo[:, :], w["L0_attn_wo"]).then_inc(w_loaded, 16)
                    sp.dma_start(w1[:, :], w["L0_attn_w1"]).then_inc(w_loaded, 16)
                    sp.dma_start(w2[:, :, :], w["L0_attn_w2"].rearrange("(c p) d -> p c d", p=P)).then_inc(w_loaded, 16)
                    sp.dma_start(b1[:, :], w["L0_attn_b1"].rearrange("(c p) -> p c", p=P),
                                 allow_slow_non_contiguous=True).then_inc(w_loaded, 16)
                    with sp.Fori(1, BATCH) as b:
                        apart(sp, x_loaded, b * 16)
                        load(b)
                    sp.wait_ge(w_loaded, 16 * 16)

                @block.vector
                def _(vec):
                    chain = Chain(vec, dve)
                    link = chain.link

                    def norms(b):
                        xb, hb = x[:, bass.ds(b * BCOL, BCOL)], hid[:, bass.ds(b * BCOL, BCOL)]
                        apart(vec, x_loaded, b * 16 + 16)
                        for n, src in enumerate((xb, hb)):
                            for t in range(BT):
                                last = vec.bn_stats(stats[:, t, :], src[:, t * D:(t + 1) * D])
                            link(last)
                            for t in range(BT):
                                last = vec.bn_aggr(mv[:, t, :], stats[:, t, :])
                            link(last)
                            if n == 0:
                                vec.tensor_copy(ms[:, :], mv[:, :, 1]).then_inc(stat_ready, 1)
                            else:
                                root_mean_square(vec, link, ms, mv).then_inc(stat_ready, 1)
                            vec.wait_ge(std_ready, b * 2 + (n + 1))
                            link(vec.reciprocal(rstd[:, :], std[:, :]))
                            if n == 0:
                                normalise(vec, link, hb, xb, mv, rstd)
                        reached(vec, T_done, b)
                        for t in range(BT):
                            last = vec.tensor_scalar(h[:, t * D:(t + 1) * D], hb[:, t * D:(t + 1) * D],
                                                     rstd[:, t:t + 1], None, ALU.mult)
                        last.then_inc(h_ready, 1)

                    def keys(b):
                        return qkvb[:, bass.ds(b * BT, BT), D:2 * D].rearrange("p t (h r) -> p t h r", r=HD)

                    def biases(b):
                        for t in range(BT):
                            vec.wait_ge(p_done, b * BT + (t + 1))
                            vec.tensor_tensor(qkvb[:, bass.ds(b * BT + t, 1), :].rearrange("p o c -> p (o c)"),
                                              pP[t % 4][:, 0:QKVB], bcat[:, :], ALU.add).then_inc(p_used, 1)
                        vec.wait_ge(p_used, b * BT + BT)
                        sq4 = sq[:, :, :].rearrange("p t (h r) -> p t h r", r=HD)
                        link(vec.tensor_tensor(sq4, keys(b), keys(b), ALU.mult))
                        vec.reduce_sum(norm[:, :, :], sq4, AX).then_inc(norm_ready, 1)

                    def unit_keys(b):
                        vec.wait_ge(nstd_ready, b + 1)
                        link(vec.tensor_scalar(nstd[:, :, :], nstd[:, :, :], 1e-6, None, ALU.add))
                        link(vec.reciprocal(norm[:, :, :], nstd[:, :, :]))
                        link(vec.tensor_tensor(keys(b), keys(b), norm[:, :, :].unsqueeze(3).to_broadcast([P, BT, H, HD]),
                                               ALU.mult))

                    def batch(b):
                        biases(b)
                        norms(b + 1)
                        unit_keys(b)

                    norms(0)
                    vec.wait_ge(w_loaded, 16 * 16)
                    batch(0)
                    for b in chain.each(BATCH - 2, 12, first=1):
                        batch(b)
                    biases(BATCH - 1)
                    unit_keys(BATCH - 1)
                    vec.wait_ge(beta_ready, 1)
                    vec.tensor_tensor(kbeta[:, :, :].rearrange("p j (h r) -> p j h r", r=HD),
                                      qkvb[:, :, D:2 * D].rearrange("p j (h r) -> p j h r", r=HD),
                                      qkvb[:, :, 3 * D:].unsqueeze(3).to_broadcast([P, SEG, H, HD]), ALU.mult)

                @block.scalar
                def _(act):
                    def roots(b):
                        for n in range(2):
                            act.wait_ge(stat_ready, b * 2 + (n + 1))
                            act.activation(std[:, :], ms[:, :], ACT.Sqrt, bias=c["eps"][:, n:n + 1]).then_inc(std_ready, 1)
                        act.wait_ge(T_done, b + 1)
                        reached(act, p_done, b * BT)
                        act.activation(hT[:, :], pT[:, :], ACT.Copy, scale=ln1_scale[:, 0:1]).then_inc(T_ready, 1)

                    def lengths(b):
                        act.wait_ge(norm_ready, b + 1)
                        act.activation(nstd[:, :, :], norm[:, :, :], ACT.Sqrt).then_inc(nstd_ready, 1)

                    def batch(b):
                        lengths(b)
                        roots(b + 1)

                    act.wait_ge(w_loaded, 16 * 16)
                    roots(0)
                    batch(0)
                    with act.Fori(1, BATCH - 1) as b:
                        batch(b)
                    lengths(BATCH - 1)
                    act.wait_ge(p_used, BATCH * BT)
                    act.activation(qkvb[:, :, 3 * D:], qkvb[:, :, 3 * D:], ACT.Sigmoid).then_inc(beta_ready, 1)

                @block.tensor
                def _(pe):
                    def project(b):
                        pe.wait_ge(h_ready, b + 1)
                        reached(pe, T_ready, b)
                        for t in range(BT):
                            last = pe.transpose(pT[:, t * P:(t + 1) * P], h[:, t * D:(t + 1) * D], c["ident"][:, :])
                        last.then_inc(T_done, 1)
                        pe.wait_ge(T_ready, b + 1)
                        for t in range(BT):
                            reached(pe, p_used, b * BT + (t - 3))
                            pe.matmul(pP[t % 4][:, 0:QKVB], hT[:, t * P:(t + 1) * P], wcat[:, :],
                                      start=True, stop=True).then_inc(p_done, 1)

                    pe.wait_ge(w_loaded, 16 * 16)
                    batches(pe, project)

        FULL = [P, H, R2, HD]
        HH = H // 2
        PART = [P, HH, R2, HD]
        with ExitStack() as in2:
            sb2 = lambda n, s, dt=F32: core.sb(in2, "g2_" + n, s, dt)
            sem2 = lambda n: core.sem(in2, "g2_" + n)
            R = sb2("R", FULL)
            prod, Rk = [sb2(f"prod{i}", PART) for i in range(2)], [sb2(f"Rk{i}", [P, HH, R2]) for i in range(2)]
            proq = [sb2(f"proq{i}", FULL) for i in range(2)]
            pq = core.ps(in2, "g2_pq", [P, H * R2])
            start, dve, R_ready, k_ready, k_mult, q_mult, q_sum, q_kept = (
                sem2(n) for n in ("start", "dve", "R_ready", "k_ready", "k_mult", "q_mult", "q_sum", "q_kept"))
            stored = sem2("stored")

            def heads(a, j, at, i):
                first = at + i * HH * HD
                return a[:, bass.ds(j, 1), first:first + HH * HD].rearrange("p o (h r) -> p (o h) r", r=HD)

            def rows_by(v):
                return v.unsqueeze(2).to_broadcast(PART)

            def tokens(eng, one):
                one(0, 0)
                one(1, 1)
                with eng.Fori(1, SEG // 2 - 1) as turn:
                    for n in range(2):
                        one(turn * 2 + n, n)
                one(SEG - 2, 0)
                one(SEG - 1, 1)

            with nc.Block() as block:
                @block.gpsimd
                def _(pool):
                    pool.memset(R[:, :, :, :], 0.0).then_inc(start, 1)
                    pool.wait_ge(start, 1)
                    eye = R[:, :, HD:, :]
                    pool.affine_select(out=eye, in_=eye, compare_op=ALU.not_equal, fill=1.0, base=0,
                                       pattern=[[0, H], [1, HD], [-1, HD]], channel_multiplier=0).then_inc(start, 1)

                    def multiply(j):
                        pool.tensor_tensor(prod[1][:, :, :, :], R[:, HH:, :, :], rows_by(heads(qkvb, j, D, 1)),
                                           ALU.mult).then_inc(k_mult, 1)

                    def token(j, n):
                        pool.wait_ge(R_ready, j * 2 + 2)
                        if not isinstance(j, int) or j < SEG - 1:
                            multiply(j + 1)
                        if not isinstance(j, int) or j >= 2:
                            pool.wait_ge(q_sum, j - 1)
                        for i in range(2):
                            pool.tensor_tensor(proq[n][:, i * HH:(i + 1) * HH, :, :], R[:, i * HH:(i + 1) * HH, :, :],
                                               rows_by(heads(qkvb, j, 0, i)), ALU.mult).then_inc(q_mult, 1)

                    pool.wait_ge(start, 2)
                    multiply(0)
                    tokens(pool, token)

                @block.vector
                def _(vec):
                    vec.wait_ge(start, 2)
                    LINKS = 6

                    def multiply(j):
                        reached(vec, R_ready, j * 2 - 1)
                        vec.tensor_tensor(prod[0][:, :, :, :], R[:, 0:HH, :, :], rows_by(heads(qkvb, j, D, 0)),
                                          ALU.mult).then_inc(k_ready, 1)

                    def token(j, n):
                        for i in range(2):
                            vec.wait_ge(k_mult if i else k_ready, j + 1)
                            vec.reduce_sum(Rk[i][:, :, :], prod[i][:, :, :, :], AX).then_inc(dve, 1)
                        for i in range(2):
                            vec.wait_ge(dve, j * LINKS + (i + 1))
                            vec.tensor_tensor(Rk[i][:, :, 0:HD], Rk[i][:, :, 0:HD], heads(qkvb, j, 2 * D, i),
                                              ALU.subtract).then_inc(dve, 1)
                        for i in range(2):
                            vec.wait_ge(dve, j * LINKS + (i + 3))
                            vec.tensor_tensor(prod[i][:, :, :, :], Rk[i][:, :, :].unsqueeze(3).to_broadcast(PART),
                                              rows_by(heads(kbeta, j, 0, i)), ALU.mult).then_inc(dve, 1)
                        for i in range(2):
                            part = R[:, i * HH:(i + 1) * HH, :, :]
                            vec.wait_ge(dve, j * LINKS + (i + 5))
                            reached(vec, q_mult, j * 2 + (i - 1))
                            vec.tensor_tensor(part, part, prod[i][:, :, :, :], ALU.subtract).then_inc(R_ready, 1)
                        if not isinstance(j, int) or j < SEG - 1:
                            multiply(j + 1)

                    multiply(0)
                    tokens(vec, token)

                @block.tensor
                def _(pe):
                    def token(j, n):
                        pe.wait_ge(q_mult, j * 2 + 2)
                        reached(pe, q_kept, j)
                        for e in range(HD):
                            last = pe.matmul(pq[:, :], c["ident"][:, :], proq[n][:, :, :, e].rearrange("p h r -> p (h r)"),
                                             start=e == 0, stop=e == HD - 1)
                        last.then_inc(q_sum, 1)

                    tokens(pe, token)

                @block.scalar
                def _(act):
                    with act.Fori(0, SEG) as j:
                        act.wait_ge(q_sum, j + 1)
                        act.copy(outs[:, bass.ds(j, 1), :, :].rearrange("p o h r -> p (o h r)"), pq[:, :]).then_inc(q_kept, 1)

                @block.sync
                def _(sp):
                    sp.wait_ge(R_ready, SEG * 2)
                    sp.dma_start(w["segments"].rearrange("p h x -> p (h x)"),
                                 R[:, :, :, :].rearrange("p h r e -> p (h r e)")).then_inc(stored, 16)
                    sp.wait_ge(stored, 16)

        with ExitStack() as in3:
            sb3 = lambda n, s, dt=F32: core.sb(in3, "g3_" + n, s, dt)
            sem3 = lambda n: core.sem(in3, "g3_" + n)
            HR = HD // 2
            Rt, S = sb3("Rt", [P, SEGS, (HR + HD) * HD]), sb3("S", [P, SEGS, HR, HD])
            prod, part = sb3("prod", [P, HR, HD, HD]), sb3("part", [P, HR, HD])
            loaded, dve, S_ready, stored = sem3("loaded"), sem3("dve"), sem3("S_ready"), sem3("stored")
            ALL = [P, HR, HD, HD]
            with nc.Block() as block:
                @block.sync
                def _(sp):
                    for half in range(2):
                        for b in range(BATCH):
                            at = (half * BATCH + b) * H
                            segments = w["segments"][b * SEGS:(b + 1) * SEGS].rearrange("s h x -> h s x")
                            sp.dma_start(Rt[at:at + H, :, 0:HR * HD],
                                         segments[:, :, half * HR * HD:(half + 1) * HR * HD]).then_inc(loaded, 16)
                            sp.dma_start(Rt[at:at + H, :, HR * HD:], segments[:, :, HD * HD:]).then_inc(loaded, 16)
                    sp.wait_ge(S_ready, 1)
                    for half in range(2):
                        for b in range(BATCH):
                            at = (half * BATCH + b) * H
                            sp.dma_start(w["entries"][b * SEGS:(b + 1) * SEGS].rearrange("s h x -> h s x")
                                         [:, :, half * HR * HD:(half + 1) * HR * HD],
                                         S[at:at + H, :, :, :].rearrange("p s d e -> p s (d e)")).then_inc(stored, 16)
                    sp.wait_ge(stored, 16 * 2 * BATCH)

                @block.vector
                def _(vec):
                    chain = Chain(vec, dve)
                    link = chain.link
                    link(vec.memset(S[:, 0:1, :, :], 0.0))
                    vec.wait_ge(loaded, 16 * 4 * BATCH)
                    def segment(s):
                        Sv = S[:, bass.ds(s, 1), :, :].rearrange("p o d e -> p (o d) e")
                        M = Rt[:, bass.ds(s, 1), HR * HD:].rearrange("p o (e f) -> p (o f) e", e=HD)
                        local = Rt[:, bass.ds(s, 1), 0:HR * HD].rearrange("p o x -> p (o x)")
                        link(vec.tensor_tensor(prod[:, :, :, :], Sv.unsqueeze(2).to_broadcast(ALL),
                                               M.unsqueeze(1).to_broadcast(ALL), ALU.mult))
                        link(vec.reduce_sum(part[:, :, :], prod[:, :, :, :], AX))
                        link(vec.tensor_tensor(S[:, bass.ds(s + 1, 1), :, :].rearrange("p o d e -> p (o d e)"),
                                               part[:, :, :].rearrange("p d f -> p (d f)"), local, ALU.add))

                    segment(0)
                    for turn in chain.each((SEGS - 2) // 3, 9):
                        for n in range(3):
                            segment(turn * 3 + (n + 1))
                    vec.sem_inc(S_ready, 1)

        with ExitStack() as in4:
            sb4 = lambda n, s, dt=F32: core.sb(in4, "g4_" + n, s, dt)
            sem4 = lambda n: core.sem(in4, "g4_" + n)
            HALF = [P, H, HD, HD]
            MH = SEQ // 2
            S = sb4("S", HALF)
            prod = [sb4(f"prod{i}", HALF)[:, :, :, :] for i in range(HT)]
            prod += [kbeta[:, i * BT:(i + 1) * BT, :].rearrange("p t (h x) -> p (t h) x", h=2)
                     .rearrange("p h (d e) -> p h d e", d=HD) for i in range(HT)]
            stats, mv, ms = sb4("stats", [P, BT, 6]), sb4("mv", [P, BT, 2]), sb4("ms", [P, BT])
            std, rstd = sb4("std", [P, BT]), sb4("rstd", [P, BT])
            osum, oT = sb4("osum", [P, BT, D]), sb4("oT", [P, BCOL])
            h2, h2T = sb4("h2", [P, BCOL]), sb4("h2T", [P, BCOL])
            gT = [sb4(f"gT{i}", [P, MH]) for i in range(DFC)]
            pT, pO, pY = (core.ps(in4, "g4_" + n, [P, BCOL]) for n in ("pT", "pO", "pY"))
            pH = [core.ps(in4, f"g4_pH{i}", [P, MH]) for i in range(2)]
            (S_loaded, prod_ready, prod_used, osum_ready, oT_done, oT_ready, o_done, stat_ready, std_ready, h2_ready,
             hT_done, h2T_ready, h_done, g_ready, y_done, y_ready, y_stored, dve) = (sem4(n) for n in (
                 "S_loaded", "prod_ready", "prod_used", "osum_ready", "oT_done", "oT_ready", "o_done", "stat_ready",
                 "std_ready", "h2_ready", "hT_done", "h2T_ready", "h_done", "g_ready", "y_done", "y_ready", "y_stored",
                 "dve"))
            out_rows = x_out.rearrange("(p j) d -> p (j d)", j=SEG)
            with nc.Block() as block:
                @block.sync
                def _(sp):
                    sp.dma_start(S[:, :, :, :].rearrange("p h d e -> p (h d e)"),
                                 w["entries"].rearrange("p h x -> p (h x)")).then_inc(S_loaded, 16)
                    with sp.Fori(0, BATCH) as b:
                        sp.wait_ge(y_ready, b + 1)
                        sp.dma_start(out_rows[:, bass.ds(b * BCOL, BCOL)], x[:, bass.ds(b * BCOL, BCOL)]).then_inc(y_stored, 16)
                    sp.wait_ge(y_stored, 16 * BATCH)

                @block.gpsimd
                def _(pool):
                    pool.wait_ge(S_loaded, 16)

                    def products(b):
                        for t in range(BT):
                            reached(pool, prod_used, (b - 1) * BT + (t + 1))
                            Mq = outs[:, bass.ds(b * BT + t, 1), :, HD:].rearrange("p o h e -> p (o h) e")
                            pool.tensor_tensor(prod[t], S[:, :, :, :], Mq.unsqueeze(2).to_broadcast(HALF),
                                               ALU.mult).then_inc(prod_ready, 1)

                    batches(pool, products)

                @block.vector
                def _(vec):
                    chain = Chain(vec, dve)
                    link = chain.link

                    def sums(b):
                        reached(vec, oT_done, b)
                        for t in range(BT):
                            vec.wait_ge(prod_ready, b * BT + (t + 1))
                            vec.reduce_sum(osum[:, t, :].rearrange("p (h d) -> p h d", d=HD), prod[t],
                                           AX).then_inc(prod_used, 1)
                        own = outs[:, bass.ds(b * BT, BT), :, 0:HD]
                        o4 = osum[:, :, :].rearrange("p t (h d) -> p t h d", d=HD)
                        vec.wait_ge(prod_used, b * BT + BT)
                        vec.tensor_tensor(o4, o4, own, ALU.add).then_inc(osum_ready, 1)

                    def norm(b):
                        hb, xb = hid[:, bass.ds(b * BCOL, BCOL)], x[:, bass.ds(b * BCOL, BCOL)]
                        vec.wait_ge(o_done, b + 1)
                        link(vec.tensor_tensor(hb, hb, pO[:, :], ALU.add))
                        per_column(vec, link, hb, hb, rows["bo"], ALU.add)
                        for t in range(BT):
                            last = vec.bn_stats(stats[:, t, :], hb[:, t * D:(t + 1) * D])
                        link(last)
                        for t in range(BT):
                            last = vec.bn_aggr(mv[:, t, :], stats[:, t, :])
                        link(last)
                        root_mean_square(vec, link, ms, mv).then_inc(stat_ready, 1)
                        link(vec.tensor_tensor(xb, xb, hb, ALU.add))
                        vec.wait_ge(std_ready, b + 1)
                        link(vec.reciprocal(rstd[:, :], std[:, :]))
                        reached(vec, hT_done, b)
                        for t in range(BT):
                            last = vec.tensor_scalar(h2[:, t * D:(t + 1) * D], hb[:, t * D:(t + 1) * D],
                                                     rstd[:, t:t + 1], None, ALU.mult)
                        last.then_inc(h2_ready, 1)
                        per_column(vec, link, xb, xb, rows["b2"], ALU.add)

                    def finish(b):
                        xb = x[:, bass.ds(b * BCOL, BCOL)]
                        vec.wait_ge(y_done, b * 2 + 2)
                        vec.tensor_tensor(xb, xb, pY[:, :], ALU.add).then_inc(y_ready, 1)

                    def batch(b):
                        sums(b + 1)
                        norm(b + 1)
                        finish(b)

                    sums(0)
                    norm(0)
                    batch(0)
                    for b in chain.each(BATCH - 2, 8, first=1):
                        batch(b)
                    finish(BATCH - 1)

                @block.scalar
                def _(act):
                    def output(b):
                        act.wait_ge(oT_done, b + 1)
                        act.copy(oT[:, :], pT[:, :]).then_inc(oT_ready, 1)

                    def root(b):
                        act.wait_ge(stat_ready, b + 1)
                        act.activation(std[:, :], ms[:, :], ACT.Sqrt, bias=c["eps"][:, 1:2]).then_inc(std_ready, 1)

                    def gelu(b, half):
                        for f in range(DFC):
                            act.wait_ge(h_done, b * 8 + (half * DFC + f + 1))
                            if f == 0:
                                reached(act, y_done, b * 2 + half)
                            act.activation(gT[f][:, :], pH[f % 2][:, :], ACT.Gelu_apprx_tanh,
                                           bias=b1[:, f:f + 1]).then_inc(g_ready, 1)

                    def batch(b, more=True):
                        act.wait_ge(hT_done, b + 1)
                        act.activation(h2T[:, :], pT[:, :], ACT.Copy, scale=ln2_scale[:, 0:1]).then_inc(h2T_ready, 1)
                        gelu(b, 0)
                        if more:
                            output(b + 1)
                        gelu(b, 1)
                        if more:
                            root(b + 1)

                    output(0)
                    root(0)
                    batch(0)
                    with act.Fori(1, BATCH - 1) as b:
                        batch(b)
                    batch(BATCH - 1, more=False)

                @block.tensor
                def _(pe):
                    def output(b):
                        pe.wait_ge(osum_ready, b + 1)
                        reached(pe, h2T_ready, b)
                        for t in range(BT):
                            last = pe.transpose(pT[:, t * P:(t + 1) * P], osum[:, t, :], c["ident"][:, :])
                        last.then_inc(oT_done, 1)
                        pe.wait_ge(oT_ready, b + 1)
                        reached(pe, h2_ready, b)
                        for t in range(BT):
                            last = pe.matmul(pO[:, t * D:(t + 1) * D], oT[:, t * P:(t + 1) * P], wo[:, :], start=True, stop=True)
                        last.then_inc(o_done, 1)

                    def mlp(b, half):
                        for f in range(DFC):
                            reached(pe, g_ready, b * 8 + (half * DFC + f - 1))
                            pe.matmul(pH[f % 2][:, :], w1[:, f * P:(f + 1) * P], h2T[:, half * MH:(half + 1) * MH],
                                      start=True, stop=True).then_inc(h_done, 1)
                        pe.wait_ge(g_ready, b * 8 + (half * DFC + DFC))
                        if half == 0:
                            reached(pe, y_ready, b)
                        for t in range(half * HT, (half + 1) * HT):
                            for f in range(DFC):
                                last = pe.matmul(pY[:, t * D:(t + 1) * D], gT[f][:, (t % HT) * P:(t % HT + 1) * P],
                                                 w2[:, f, :], start=f == 0, stop=f == DFC - 1)
                        last.then_inc(y_done, 1)

                    def batch(b, more=True):
                        pe.wait_ge(h2_ready, b + 1)
                        for t in range(BT):
                            last = pe.transpose(pT[:, t * P:(t + 1) * P], h2[:, t * D:(t + 1) * D], c["ident"][:, :])
                        last.then_inc(hT_done, 1)
                        pe.wait_ge(h2T_ready, b + 1)
                        mlp(b, 0)
                        if more:
                            output(b + 1)
                        mlp(b, 1)

                    output(0)
                    batch(0)
                    with pe.Fori(1, BATCH - 1) as b:
                        batch(b)
                    batch(BATCH - 1, more=False)


def build(nc, names, aps, out):
    w = dict(zip(names, aps))
    with ExitStack() as ctx:
        core = Core(nc, ctx)
        scratch = lambda n, shape, dt=F32: nc.dram_tensor(n, shape, dt, kind="Internal").ap()
        w["qk_parts"] = scratch("qk_parts", [2, 3, UNITS, GH * HD, SEQ], BF16)
        w["xin"] = scratch("xin", [SLOTS + TOK * 2, ROW])
        w["y"] = scratch("y", [2 * TOK + SLOTS, D])
        w["segments"] = scratch("segments", [P, H, R2 * HD])
        w["entries"] = scratch("entries", [P, H, HD * HD])
        x1, x2 = scratch("x1", [TOK, D]), scratch("x2", [TOK, D])
        flat = lambda a: a.rearrange("b s d -> (b s) d")
        c = constants(core, ctx, w)
        with nc.cleanup_on_exit():
            ffn(core, w, c, flat(w["L0_attn_x"]), x1, "_1")
        with nc.cleanup_on_exit():
            delta_block(core, w, c, x1, x2)
        with nc.cleanup_on_exit():
            ffn(core, w, c, x2, flat(out), "_2", first_layer=False)


_INS = ["L0_attn_x", "L0_attn_wq", "L0_attn_bq", "L0_attn_wk", "L0_attn_bk", "L0_attn_wv", "L0_attn_bv",
        "L0_attn_wbeta", "L0_attn_bbeta", "L0_attn_wo", "L0_attn_bo", "L0_attn_w1", "L0_attn_b1", "L0_attn_w2",
        "L0_attn_b2", "L0_attn_ln1_scale", "L0_attn_ln2_scale", "L0_ffn_ln1_w", "L0_ffn_ln1_b", "L0_ffn_q_w",
        "L0_ffn_q_b", "L0_ffn_k_w", "L0_ffn_k_b", "L0_ffn_v_w", "L0_ffn_v_b", "L0_ffn_o_w", "L0_ffn_o_b",
        "L0_ffn_ln2_w", "L0_ffn_ln2_b", "L0_ffn_router_w", "L0_ffn_fc1_w", "L0_ffn_fc1_b", "L0_ffn_fc2_w",
        "L0_ffn_fc2_b"]
_OUTS = [((4, 1024, 128), "float32")]


def kernel(**inputs):
    import numpy as _np
    import concourse.bacc as _bacc
    from concourse import mybir as _mybir
    from concourse.bass_utils import run_bass_kernel_spmd as _run

    nc = _bacc.Bacc("TRN2", target_bir_lowering=False, num_devices=1)
    arrays, args = {}, []
    for name in _INS:
        a = _np.ascontiguousarray(inputs[name])
        arrays[f"in_{name}_dram"] = a
        args.append(nc.dram_tensor(f"in_{name}_dram", a.shape, _mybir.dt.from_np(a.dtype), kind="ExternalInput").ap())
    for i, (shape, dtype) in enumerate(_OUTS):
        dt = _mybir.dt.from_np(_np.dtype(dtype))
        args.append(nc.dram_tensor(f"out_{i}_dram", shape, dt, kind="ExternalOutput").ap())
    build(nc, _INS, args[:-1], args[-1])
    r = _run(nc, [arrays], core_ids=[0])
    return r.results[0]["out_0_dram"]
```
